# Optimizing a Trainium2 kernel written in Bass

```python
import numpy as np
import jax
import jax.numpy as jnp

def _softmax(x, axis=-1):
    return jax.nn.softmax(x, axis=axis)

def _gelu(x):
    return jax.nn.gelu(x, approximate=True)

def _silu(x):
    return jax.nn.silu(x)

def _sigmoid(x):
    return jax.nn.sigmoid(x)

def _layernorm(x, axis=-1, eps=1e-05):
    m = jnp.mean(x, axis=axis, keepdims=True)
    v = jnp.var(x, axis=axis, keepdims=True)
    return (x - m) / jnp.sqrt(v + eps)

def _scatter_add(tgt, idx, src, axis=0):
    return tgt.at[idx].add(src)

def _segment_sum(src, seg, n):
    return jax.ops.segment_sum(src, seg, n)
kernel_name = 'mk_seq_postln_d1_jaxref_r8_bbdcb9'

def setup_inputs(seed: int=0):
    np.random.seed(seed)
    _w = jnp.asarray

    def _L0_attn_setup():
        import jax, jax.numpy as jnp
        import numpy as np
        D = 256
        H = 16
        KVH = 4
        HD = 128
        G = H // KVH
        CAP = 50.0
        EPS = 1e-06
        SCALE = HD ** (-0.5)
        B, T = (2, 256)

        def _rmsnorm(x, gamma):
            return x * jax.lax.rsqrt(jnp.mean(x * x, axis=-1, keepdims=True) + EPS) * gamma
        key = jax.random.key(seed)
        ks = jax.random.split(key, 5)
        s = 0.02
        return {'x': jax.random.normal(ks[0], (B, T, D), dtype=jnp.float32), 'wq': jax.random.normal(ks[1], (H * HD, D), dtype=jnp.float32) * s, 'wk': jax.random.normal(ks[2], (KVH * HD, D), dtype=jnp.float32) * s, 'wv': jax.random.normal(ks[3], (KVH * HD, D), dtype=jnp.float32) * s, 'wo': jax.random.normal(ks[4], (D, H * HD), dtype=jnp.float32) * s, 'q_gamma': jnp.ones((HD,), dtype=jnp.float32), 'k_gamma': jnp.ones((HD,), dtype=jnp.float32)}
    _L0_attn_in = _L0_attn_setup()

    def _L0_ffn_setup():
        import jax, jax.numpy as jnp
        import numpy as np
        D_MODEL = 256
        D_HIDDEN = 176
        NUM_SHARED = 2
        NUM_ROUTED = 32
        TOP_K = 6

        def _expert_apply(xf, w1, b1, w2, b2):
            return jnp.maximum(xf @ w1 + b1, 0.0) @ w2 + b2
        key = jax.random.key(seed)
        ks = jax.random.split(key, 11)
        d, h = (D_MODEL, D_HIDDEN)
        s1 = 1.0 / np.sqrt(d)
        s2 = 1.0 / np.sqrt(h)
        x = jax.random.normal(ks[0], (2, 256, d), dtype=jnp.float32)
        sw1 = jax.random.uniform(ks[1], (NUM_SHARED, d, h), jnp.float32, -s1, s1)
        sb1 = jax.random.uniform(ks[2], (NUM_SHARED, h), jnp.float32, -s1, s1)
        sw2 = jax.random.uniform(ks[3], (NUM_SHARED, h, d), jnp.float32, -s2, s2)
        sb2 = jax.random.uniform(ks[4], (NUM_SHARED, d), jnp.float32, -s2, s2)
        rw1 = jax.random.uniform(ks[5], (NUM_ROUTED, d, h), jnp.float32, -s1, s1)
        rb1 = jax.random.uniform(ks[6], (NUM_ROUTED, h), jnp.float32, -s1, s1)
        rw2 = jax.random.uniform(ks[7], (NUM_ROUTED, h, d), jnp.float32, -s2, s2)
        rb2 = jax.random.uniform(ks[8], (NUM_ROUTED, d), jnp.float32, -s2, s2)
        router_w = jax.random.uniform(ks[9], (d, NUM_ROUTED), jnp.float32, -s1, s1)
        router_b = jax.random.uniform(ks[10], (NUM_ROUTED,), jnp.float32, -s1, s1)
        return {'x': x, 'sw1': sw1, 'sb1': sb1, 'sw2': sw2, 'sb2': sb2, 'rw1': rw1, 'rb1': rb1, 'rw2': rw2, 'rb2': rb2, 'router_w': router_w, 'router_b': router_b}
    _L0_ffn_in = _L0_ffn_setup()
    _d = {'L0_attn_x': _L0_attn_in['x'], 'L0_attn_wq': _L0_attn_in['wq'], 'L0_attn_wk': _L0_attn_in['wk'], 'L0_attn_wv': _L0_attn_in['wv'], 'L0_attn_wo': _L0_attn_in['wo'], 'L0_attn_q_gamma': _L0_attn_in['q_gamma'], 'L0_attn_k_gamma': _L0_attn_in['k_gamma'], 'L0_ffn_sw1': _L0_ffn_in['sw1'], 'L0_ffn_sb1': _L0_ffn_in['sb1'], 'L0_ffn_sw2': _L0_ffn_in['sw2'], 'L0_ffn_sb2': _L0_ffn_in['sb2'], 'L0_ffn_rw1': _L0_ffn_in['rw1'], 'L0_ffn_rb1': _L0_ffn_in['rb1'], 'L0_ffn_rw2': _L0_ffn_in['rw2'], 'L0_ffn_rb2': _L0_ffn_in['rb2'], 'L0_ffn_router_w': _L0_ffn_in['router_w'], 'L0_ffn_router_b': _L0_ffn_in['router_b']}
    _x0 = _d['L0_attn_x']
    _d['L0_attn_x'] = jax.random.normal(jax.random.fold_in(jax.random.key(seed), 1), (1, 1024, 256), dtype=_x0.dtype)
    del _x0
    return _d

def reference(L0_attn_x, L0_attn_wq, L0_attn_wk, L0_attn_wv, L0_attn_wo, L0_attn_q_gamma, L0_attn_k_gamma, L0_ffn_sw1, L0_ffn_sb1, L0_ffn_sw2, L0_ffn_sb2, L0_ffn_rw1, L0_ffn_rb1, L0_ffn_rw2, L0_ffn_rb2, L0_ffn_router_w, L0_ffn_router_b):

    def _L0_attn_ref(x, wq, wk, wv, wo, q_gamma, k_gamma):
        import jax, jax.numpy as jnp
        import numpy as np
        D = 256
        H = 16
        KVH = 4
        HD = 128
        G = H // KVH
        CAP = 50.0
        EPS = 1e-06
        SCALE = HD ** (-0.5)
        B, T = (2, 256)

        def _rmsnorm(x, gamma):
            return x * jax.lax.rsqrt(jnp.mean(x * x, axis=-1, keepdims=True) + EPS) * gamma
        b, t, _ = x.shape
        q = (x @ wq.T).reshape(b, t, H, HD).transpose(0, 2, 1, 3)
        k = (x @ wk.T).reshape(b, t, KVH, HD).transpose(0, 2, 1, 3)
        v = (x @ wv.T).reshape(b, t, KVH, HD).transpose(0, 2, 1, 3)
        q = _rmsnorm(q, q_gamma)
        k = _rmsnorm(k, k_gamma)
        k = jnp.repeat(k, G, axis=1)
        v = jnp.repeat(v, G, axis=1)
        attn = jnp.einsum('bhtd,bhsd->bhts', q, k) * SCALE
        attn = CAP * jnp.tanh(attn / CAP)
        causal = jnp.triu(jnp.ones((t, t), dtype=bool), k=1)
        attn = jnp.where(causal, -jnp.inf, attn)
        attn = jax.nn.softmax(attn, axis=-1)
        out = jnp.einsum('bhts,bhsd->bhtd', attn, v)
        out = out.transpose(0, 2, 1, 3).reshape(b, t, H * HD)
        return out @ wo.T

    def _L0_ffn_ref(x, sw1, sb1, sw2, sb2, rw1, rb1, rw2, rb2, router_w, router_b):
        import jax, jax.numpy as jnp
        import numpy as np
        D_MODEL = 256
        D_HIDDEN = 176
        NUM_SHARED = 2
        NUM_ROUTED = 32
        TOP_K = 6

        def _expert_apply(xf, w1, b1, w2, b2):
            return jnp.maximum(xf @ w1 + b1, 0.0) @ w2 + b2
        B, S, d = x.shape
        flat = x.reshape(-1, d)
        T = flat.shape[0]

        def sh_body(acc, p):
            w1, b1, w2, b2 = p
            return (acc + _expert_apply(flat, w1, b1, w2, b2), None)
        shared_out, _ = jax.lax.scan(sh_body, jnp.zeros_like(flat), (sw1, sb1, sw2, sb2))
        shared_out = shared_out / NUM_SHARED
        logits = flat @ router_w + router_b
        probs = jax.nn.softmax(logits, axis=-1)
        topk_p, topk_i = jax.lax.top_k(probs, TOP_K)
        topk_p = topk_p / jnp.sum(topk_p, axis=-1, keepdims=True)
        gates = jnp.zeros((T, NUM_ROUTED), dtype=flat.dtype)
        gates = gates.at[jnp.arange(T)[:, None], topk_i].add(topk_p)

        def r_body(acc, p):
            w1, b1, w2, b2, g = p
            return (acc + g[:, None] * _expert_apply(flat, w1, b1, w2, b2), None)
        routed_out, _ = jax.lax.scan(r_body, jnp.zeros_like(flat), (rw1, rb1, rw2, rb2, gates.T))
        return (shared_out + routed_out).reshape(B, S, d)
    x = L0_attn_x
    x = _layernorm(x + _L0_attn_ref(x, L0_attn_wq, L0_attn_wk, L0_attn_wv, L0_attn_wo, L0_attn_q_gamma, L0_attn_k_gamma), axis=-1)
    x = _layernorm(x + _L0_ffn_ref(x, L0_ffn_sw1, L0_ffn_sb1, L0_ffn_sw2, L0_ffn_sb2, L0_ffn_rw1, L0_ffn_rb1, L0_ffn_rw2, L0_ffn_rb2, L0_ffn_router_w, L0_ffn_router_b), axis=-1)
    return x

_drawn_inputs = setup_inputs


def setup_inputs(seed=0):
    import zlib

    import numpy as np

    out = dict(_drawn_inputs(seed))
    spreads = {'L0_attn_q_gamma': (1.0, 0.6), 'L0_attn_k_gamma': (1.0, 0.6)}
    factors = {'L0_ffn_sb1': 5.221, 'L0_ffn_rb1': 8.0, 'L0_ffn_rb2': 3.16, 'L0_ffn_router_b': 2.918}
    for name, (base, spread) in spreads.items():
        noise = np.random.default_rng([zlib.crc32(name.encode()), seed]).standard_normal(out[name].shape)
        drawn = base * np.exp(spread * noise) if base else spread * noise
        out[name] = jnp.asarray(drawn.astype(out[name].dtype))
    for name, factor in factors.items():
        out[name] = (out[name] * factor).astype(out[name].dtype)
    return out
```

```python
from contextlib import ExitStack

import concourse.bass as bass
from concourse import mybir

F32 = mybir.dt.float32
F32R = mybir.dt.float32r
U32 = mybir.dt.uint32
ALU = mybir.AluOpType
ACT = mybir.ActivationFunctionType
AX = mybir.AxisListType

P = 128
T, D = 1024, 256
H, KVH, HD = 16, 4, 128
G = H // KVH
NT = T // P
DC = D // P
QB = 512
NB = T // QB
CAP, RMS_EPS, LN_EPS = 50.0, 1e-6, 1e-5
SCALE = HD ** -0.5

NE, NS, HID, TOPK = 32, 2, 176, 6
EROWS = P // NE
NROUTED = HID // EROWS
NSHARED = -(-NS * HID // P)

HEAD_STEPS = (
    ((0, 0, 0, 512), (0, 3, 512, 128), (0, 1, 640, 384)),
    ((1, 0, 0, 512), (1, 1, 512, 512)),
    ((0, 2, 0, 256), (1, 6, 256, 256)),
    ((1, 2, 0, 512), (1, 3, 512, 512)),
    ((1, 4, 0, 512), (1, 7, 512, 128), (1, 5, 640, 384)),
)
STEP_WIDTH = (1024, 1024, 512, 1024, 1024)
STEP_MASKS = (((0, 1, 128), (512, 2, 128)), (), ((0, 2, 256),), (), ((0, 1, 128), (512, 2, 128)))
STEP_ADDS = (
    ((0, (0, 128), 0, "copy"), (0, (128, 512), 128, 640), (0, (384, 512), 512, None)),
    ((1, (0, 512), 0, 512),),
    ((0, (256, 512), 0, None), (1, (256, 512), 256, None)),
    ((1, (0, 512), 0, None), (1, (0, 512), 512, None)),
    ((1, (0, 512), 0, None), (1, (128, 512), 640, None), (1, (384, 512), 512, None)),
)
NSTEP = len(HEAD_STEPS)
STEPS = G * NSTEP
PAIRS = NB * G
HI_ON_ACT = (1, 3)
HALF = NT // NB

LOOP_START = 9


def last_step(p):
    return NSTEP * (p // NB) + (2, 4)[p % NB]


def pairs(n, lag, end):
    return [p for p in range(NB * end // NSTEP) if last_step(p) + lag == n]


def q_heads(n, lead, end):
    return [j for j in range(2, end // NSTEP) if NSTEP * j - lead == n]


def q_halves(n, leads, end):
    return [(j, b) for b in range(NB) for j in q_heads(n, leads[b], end)]


OUT_UNITS = [(b, d) for b in range(NB) for d in range(DC)]
OUT_STEP = 24
WO_STEP = 14
LOOP, LAST = 2 * STEPS, STEPS


def slots(uses, first=0):
    return {u: ((first + i) % 2, uses[i - 2] if i >= 2 else None) for i, u in enumerate(uses)}


def step_uses(n, end):
    scores = [("scores", n + 2)] if n + 2 < end else []
    out = [("out", n - OUT_STEP)] if OUT_STEP <= n < OUT_STEP + len(OUT_UNITS) else []
    q = [("q", j) for j in q_heads(n, 10, end)]
    return (out + scores if n == OUT_STEP + len(OUT_UNITS) - 1 else scores + out) + q


FIRST_USES = [u for k in range(KVH) for u in (("q", k - KVH), ("v", k))] + [("q", 0), ("q", 1), ("scores", 0), ("scores", 1)]
PLAN_FIRST = slots(FIRST_USES + [u for n in range(LOOP_START) for u in step_uses(n, LOOP)])
CARRIED = [("scores", LOOP_START), ("scores", LOOP_START + 1)]
PLAN_LOOP = slots(CARRIED + [u for n in range(LOOP_START, LOOP_START + STEPS) for u in step_uses(n, LOOP)],
                  PLAN_FIRST[CARRIED[0]][0])
PLAN_LAST = slots(CARRIED + [u for n in range(LOOP_START, LOOP_START + STEPS) for u in step_uses(n, LAST)],
                  PLAN_FIRST[CARRIED[0]][0])
for u in CARRIED:
    assert PLAN_FIRST[u][0] == PLAN_LOOP[u][0] == PLAN_LOOP[u[0], u[1] + STEPS][0]


class Signal:

    def __init__(self, sem, per_round=1, credit=0, unit=1):
        self.sem, self.per_round, self.credit, self.unit = sem, per_round, credit, unit

    def value(self, g, n):
        return g * (self.per_round * self.unit) + (n + 1 + self.credit) * self.unit


def f32(ap):
    return ap.bitcast(F32)


def split3(stat_hi, stat_lo, move_hi, move_lo):
    return ((stat_hi, move_hi), (stat_lo, move_hi), (stat_hi, move_lo))


ADDS = [(h, i, a) for h in range(LOOP // NSTEP) for i in range(NSTEP) for a in STEP_ADDS[i]]


def last_add(n):
    return max(k for k, (h, i, _) in enumerate(ADDS) if NSTEP * h + i == n)


def attention(nc, kept, dram):
    resT, ident, minus_half = kept["resT"], kept["ident"], kept["minus_half"]
    with ExitStack() as ctx:
        def sb(name, shape, dt=F32):
            return ctx.enter_context(nc.sbuf_tensor(name, shape, dt))

        def signal(name, per_round=1, credit=0, unit=1):
            return Signal(ctx.enter_context(nc.semaphore(name)), per_round, credit, unit)

        xT_hi, xT_lo = sb("xT_hi", [P, DC, T], F32R), sb("xT_lo", [P, DC, T], F32R)
        wq_raw = sb("wq_raw", [P, DC, G * HD])
        wq_hi, wq_lo = sb("wq_hi", [P, DC, G * HD], F32R), sb("wq_lo", [P, DC, G * HD], F32R)
        wo_raw = sb("wo_raw", [P, G, D])
        wo_hi, wo_lo = sb("wo_hi", [P, G, D], F32R), sb("wo_lo", [P, G, D], F32R)
        gammas = sb("gammas", [P, 2])
        causal = sb("causal", [P, 2, P])
        q_square = sb("q_square", [P, T])
        q_raw = sb("q_raw", [P, T])
        q_sum = sb("q_sum", [P, NB, HALF])
        q_var = sb("q_var", [P, NB, HALF])
        q_rinv = sb("q_rinv", [P, NB, HALF])
        q_norm = sb("q_norm", [P, NB, QB])
        qT_hi, qT_lo = sb("qT_hi", [P, 2, T], F32R), sb("qT_lo", [P, 2, T], F32R)
        k_norm = sb("k_norm", [P, KVH, T])
        v_all = sb("v_all", [P, KVH, NT, HD])
        kT_hi, kT_lo = sb("kT_hi", [P, T], F32R), sb("kT_lo", [P, T], F32R)
        v_hi, v_lo = sb("v_hi", [P, NT, HD], F32R), sb("v_lo", [P, NT, HD], F32R)
        capped = sb("capped", [P, 2, 1024])
        prob = sb("prob", [P, 2, 1024])
        prob_hi, prob_lo = sb("prob_hi", [P, 2, 1024], F32R), sb("prob_lo", [P, 2, 1024], F32R)
        prob_sum = sb("prob_sum", [P, 2, NB, QB])
        key_sum = sb("key_sum", [P, NB, HALF])
        inv_sum = sb("inv_sum", [P, NB, HALF])
        o_raw = sb("o_raw", [P, NB, QB])
        o_norm = sb("o_norm", [P, NB, QB])
        oT_hi, oT_lo = sb("oT_hi", [P, G, T], F32R), sb("oT_lo", [P, G, T], F32R)
        wkv_raw = [capped[:, n, :].rearrange("p (c k) -> p c k", c=DC) for n in range(2)]
        wkv_hi = [oT_hi[:, n, :].rearrange("p (c k) -> p c k", c=DC) for n in range(2)]
        wkv_lo = [oT_lo[:, n, :].rearrange("p (c k) -> p c k", c=DC) for n in range(2)]

        psum = ctx.enter_context(nc.psum_tensor("psum_attn", [P, 8, 512], F32))
        slot = [psum[:, 2 * s:2 * s + 2, :].rearrange("p b c -> p (b c)") for s in range(2)]
        o_ps = [psum[:, 4 + b, :] for b in range(NB)]
        x_ps = [psum[:, 6 + b, :] for b in range(NB)]

        def norm_ps(j, b):
            return (o_ps if j in (1, -1, -3) else x_ps)[b]

        def square_of(j):
            return prob[:, 0, :] if j in (1, -1, -3) else q_square[:]

        def raw_of(j):
            return prob[:, 1, :] if j in (1, -1, -3) else q_raw[:]

        x_in = signal("x_in", unit=16)
        gammas_in = signal("gammas_in", unit=16)
        wkv_in = [signal(f"w{n}_in", unit=16) for n in "kv"]
        wq_in = signal("wq_in", unit=16)
        wo_in = signal("wo_in", unit=16)
        consts = signal("consts")
        x_hi_done, x_lo_done = signal("x_hi_done"), signal("x_lo_done")
        wkv_hi_done = [signal(f"w{n}_hi_done") for n in "kv"]
        wkv_split = [signal(f"w{n}_split") for n in "kv"]
        wq_hi_done, wq_split = signal("wq_hi_done"), signal("wq_split")
        wo_hi_done, wo_split = signal("wo_hi_done"), signal("wo_split", credit=1)
        v_projected, v_copied = signal("v_projected", KVH), signal("v_copied", KVH)
        q_projected = signal("q_projected", G, credit=KVH)
        q_squared = signal("q_squared", G, credit=KVH)
        q_copied = signal("q_copied", G, credit=KVH)
        q_turned = signal("q_turned", NB * G, credit=NB * KVH)
        q_summed = signal("q_summed", NB * G, credit=NB * KVH)
        q_var_done = signal("q_var_done", NB * G, credit=NB * KVH)
        q_rinv_done = signal("q_rinv_done", NB * G, credit=NB * KVH)
        q_spread = signal("q_spread", NB * G, credit=NB * KVH)
        q_normed = signal("q_normed", NB * G, credit=NB * KVH)
        q_hi_done = signal("q_hi_done", NB * G)
        q_split = signal("q_split", NB * G)
        k_hi_done, k_split = signal("k_hi_done", NB), signal("k_split", NB)
        v_hi_done, v_split = signal("v_hi_done", NB), signal("v_split", NB)
        scored = signal("scored", STEPS)
        tanh_done = signal("tanh_done", STEPS)
        exp_done = signal("exp_done", STEPS)
        masked = signal("masked", 3 * G)
        hi_act = signal("hi_act", len(HI_ON_ACT) * G)
        hi_dve = signal("hi_dve", (NSTEP - len(HI_ON_ACT)) * G)
        prob_split = signal("prob_split", STEPS)
        added = signal("added", len(ADDS) // 2)
        weighted = signal("weighted", STEPS)
        sums_turned = signal("sums_turned", PAIRS)
        sums_done = signal("sums_done", PAIRS)
        inv_done = signal("inv_done", PAIRS)
        spread = signal("spread", PAIRS)
        o_copied = signal("o_copied", PAIRS)
        o_normed = signal("o_normed", PAIRS)
        o_hi_done = signal("o_hi_done", PAIRS)
        o_split = signal("o_split", PAIRS)
        out_projected = signal("out_projected", len(OUT_UNITS))
        res_added = signal("res_added", len(OUT_UNITS))

        def hi_event(n):
            h, i = divmod(n, NSTEP)
            if i in HI_ON_ACT:
                return hi_act, h * len(HI_ON_ACT) + HI_ON_ACT.index(i)
            rest = [j for j in range(NSTEP) if j not in HI_ON_ACT]
            return hi_dve, h * len(rest) + rest.index(i)

        def mask_event(n):
            return 3 * (n // NSTEP) + (n % NSTEP) // 2



        def q_dst(j, b):
            return k_norm[:, j + KVH, b * QB:(b + 1) * QB] if j < 0 else q_norm[:, b, :]

        block = ctx.enter_context(nc.Block())

        @block.sync
        def _(sp):
            sp.dma_start(resT[:], dram["xT"]).then_inc(x_in.sem, 16)
            for n in range(2):
                sp.dma_start(wkv_raw[n], dram["wkv"][n]).then_inc(wkv_in[n].sem, 16)
            sp.dma_start(gammas[:], dram["gammas"]).then_inc(gammas_in.sem, 16)
            sp.dma_start(wq_raw[:], dram["wq"][0]).then_inc(wq_in.sem, 16)
            with sp.Fori(0, KVH - 1) as g:
                sp.wait_ge(wo_split.sem, wo_split.value(g, -1))
                sp.dma_start(wo_raw[:], dram["wo"][g]).then_inc(wo_in.sem, 16)
                sp.wait_ge(wq_split.sem, wq_split.value(g, 0))
                sp.dma_start(wq_raw[:], dram["wq"][g + 1]).then_inc(wq_in.sem, 16)
            sp.wait_ge(wo_split.sem, wo_split.value(KVH - 1, -1))
            sp.dma_start(wo_raw[:], dram["wo"][KVH - 1]).then_inc(wo_in.sem, 16)

        @block.gpsimd
        def _(pool):
            nc.gpsimd.memset(minus_half[:], -0.5).then_inc(consts.sem, 1)
            nc.gpsimd.memset(ident[:], 0.0).then_inc(consts.sem, 1)
            nc.gpsimd.memset(causal[:], 1.0).then_inc(consts.sem, 1)
            pool.wait_ge(consts.sem, consts.value(0, 2))
            nc.gpsimd.affine_select(out=ident[:], in_=ident[:], compare_op=ALU.not_equal, fill=1.0, base=0,
                                    pattern=[[-1, P]], channel_multiplier=1).then_inc(consts.sem, 1)
            nc.gpsimd.affine_select(out=causal[:], in_=causal[:], compare_op=ALU.is_ge, fill=0.0, base=0,
                                    pattern=[[0, 2], [1, P]], channel_multiplier=-1).then_inc(consts.sem, 1)
            pool.wait_ge(consts.sem, consts.value(0, 4))

            def inverse_rms(g, j, b):
                pool.wait_ge(q_var_done.sem, q_var_done.value(g, NB * j + b))
                nc.gpsimd.tensor_tensor(q_rinv[:, b, :], q_var[:, b, :], minus_half[:, 0:HALF],
                                        ALU.pow).then_inc(q_rinv_done.sem, 1)

            def lo(out, whole, hi):
                return nc.gpsimd.tensor_tensor(out, whole, f32(hi), ALU.subtract)

            def q_lo(g, j, b):
                pool.wait_ge(q_hi_done.sem, q_hi_done.value(g, NB * j + b))
                cols = slice(b * QB, (b + 1) * QB)
                lo(qT_lo[:, j % 2, cols], q_norm[:, b, :], qT_hi[:, j % 2, cols]).then_inc(q_split.sem, 1)

            def step(g, n, end):
                if n < end and STEP_MASKS[n % NSTEP]:
                    pool.wait_ge(exp_done.sem, exp_done.value(g, n))
                    for first, blocks, stride in STEP_MASKS[n % NSTEP]:
                        part = prob[:, n % 2, first:first + blocks * stride].rearrange(
                            "p (b c) -> p b c", b=blocks)[:, :, 0:P]
                        last = nc.gpsimd.tensor_tensor(part, part, causal[:, 0:blocks, :], ALU.mult)
                    last.then_inc(masked.sem, 1)
                for j, b in q_halves(n, (7, 5), end):
                    inverse_rms(g, j, b)
                if n == WO_STEP + 1:
                    pool.wait_ge(wo_hi_done.sem, wo_hi_done.value(g, 0))
                    lo(wo_lo[:], wo_raw[:], wo_hi[:]).then_inc(wo_split.sem, 1)
                for j, b in q_halves(n, (3, 2), end):
                    q_lo(g, j, b)
                for p in pairs(n, 7, end):
                    h, b = divmod(p, NB)
                    cols = slice(b * QB, (b + 1) * QB)
                    pool.wait_ge(o_hi_done.sem, o_hi_done.value(g, p))
                    lo(oT_lo[:, h % G, cols], o_norm[:, b, :], oT_hi[:, h % G, cols]).then_inc(o_split.sem, 1)

            for j in range(-KVH, 2):
                for b in range(NB):
                    inverse_rms(0, j, b)
            for j in range(2):
                for b in range(NB):
                    q_lo(0, j, b)
            for n in range(LOOP_START):
                step(0, n, LOOP)
            with pool.Fori(0, KVH - 1) as g:
                for n in range(LOOP_START, LOOP_START + STEPS):
                    step(g, n, LOOP)
            for n in range(LOOP_START, LOOP_START + STEPS):
                step(KVH - 1, n, LAST)

        @block.scalar
        def _(act):
            act.wait_ge(x_in.sem, x_in.value(0, 0))
            nc.scalar.activation(xT_hi[:], resT[:], ACT.Copy).then_inc(x_hi_done.sem, 1)
            act.wait_ge(wkv_in[1].sem, wkv_in[1].value(0, 0))
            nc.scalar.activation(wkv_hi[1], wkv_raw[1], ACT.Copy).then_inc(wkv_hi_done[1].sem, 1)
            act.wait_ge(gammas_in.sem, gammas_in.value(0, 0))

            def wq_hi_half(g, r):
                act.wait_ge(wq_in.sem, wq_in.value(g, r))
                if r > 0:
                    act.wait_ge(q_projected.sem, q_projected.value(g, G * r - 1))
                nc.scalar.activation(wq_hi[:], wq_raw[:], ACT.Copy).then_inc(wq_hi_done.sem, 1)

            def k_hi(g, r, b):
                cols = slice(b * QB, (b + 1) * QB)
                src = k_norm[:, r, cols] if isinstance(g, int) and g == 0 and r == 0 else k_norm[:, bass.ds(g + r, 1), cols]
                nc.scalar.activation(kT_hi[:, cols], src, ACT.Copy).then_inc(k_hi_done.sem, 1)

            def v_hi_half(g, r, b):
                tiles = slice(b * HALF, (b + 1) * HALF)
                src = v_all[:, r, tiles, :] if isinstance(g, int) and g == 0 and r == 0 else v_all[:, bass.ds(g + r, 1), tiles, :]
                nc.scalar.activation(v_hi[:, tiles, :], src, ACT.Copy).then_inc(v_hi_done.sem, 1)

            def leave_slot(g, j, plan):
                s, _ = plan["q", j]
                act.wait_ge(q_projected.sem, q_projected.value(g, j))
                before = j - 2 if j < 2 else j - 1
                if before >= -KVH:
                    act.wait_ge(q_turned.sem, q_turned.value(g, NB * before + NB - 1))
                nc.scalar.activation(square_of(j), slot[s], ACT.Square).then_inc(q_squared.sem, 1)
                if before >= -KVH:
                    act.wait_ge(q_normed.sem, q_normed.value(g, NB * before + NB - 1))
                gamma = gammas[:, 1:2] if j < 0 else gammas[:, 0:1]
                nc.scalar.activation(raw_of(j), slot[s], ACT.Copy, scale=gamma).then_inc(q_copied.sem, 1)

            def q_hi(g, j, b):
                act.wait_ge(q_normed.sem, q_normed.value(g, NB * j + b))
                nc.scalar.activation(qT_hi[:, j % 2, b * QB:(b + 1) * QB], q_norm[:, b, :],
                                     ACT.Copy).then_inc(q_hi_done.sem, 1)

            def step(g, n, end, plan):
                if n == NSTEP * 2 - 1 and end == LOOP:
                    wq_hi_half(g, 1)
                for j in q_heads(n, 7, end):
                    leave_slot(g, j, plan)
                if n < end:
                    s, w = n % 2, STEP_WIDTH[n % NSTEP]
                    act.wait_ge(scored.sem, scored.value(g, n))
                    nc.scalar.activation(capped[:, s, 0:w], slot[plan["scores", n][0]][:, 0:w], ACT.Tanh,
                                         scale=SCALE / CAP).then_inc(tanh_done.sem, 1)
                    act.wait_ge(tanh_done.sem, tanh_done.value(g, n))
                    if n >= 2:
                        act.wait_ge(added.sem, added.value(g, last_add(n - 2)))
                    nc.scalar.activation(prob[:, s, 0:w], capped[:, s, 0:w], ACT.Exp,
                                         scale=CAP).then_inc(exp_done.sem, 1)

                    if n % NSTEP in HI_ON_ACT:
                        act.wait_ge(exp_done.sem, exp_done.value(g, n))
                        if n >= 2:
                            act.wait_ge(weighted.sem, weighted.value(g, n - 2))
                        nc.scalar.activation(prob_hi[:, s, 0:w], prob[:, s, 0:w], ACT.Copy).then_inc(hi_act.sem, 1)
                if n in (STEPS - 2, STEPS - 1) and end == LOOP:
                    k_hi(g, 1, n - (STEPS - 2))
                if n in (STEPS, STEPS + 1) and end == LOOP:
                    act.wait_ge(weighted.sem, weighted.value(g, n - 2))
                    v_hi_half(g, 1, n - STEPS)
                for p in pairs(n, 2, end):
                    act.wait_ge(weighted.sem, weighted.value(g, last_step(p)))
                    if p >= NB:
                        act.wait_ge(o_normed.sem, o_normed.value(g, p - NB))
                    nc.scalar.activation(o_raw[:, p % NB, :], o_ps[p % NB], ACT.Copy).then_inc(o_copied.sem, 1)
                for j, b in q_halves(n, (4, 2), end):
                    q_hi(g, j, b)
                for p in pairs(n, 6, end):
                    h, b = divmod(p, NB)
                    act.wait_ge(o_normed.sem, o_normed.value(g, p))
                    if p >= PAIRS:
                        act.wait_ge(out_projected.sem, out_projected.value(g, DC * b + DC - 1))
                    nc.scalar.activation(oT_hi[:, h % G, b * QB:(b + 1) * QB], o_norm[:, b, :],
                                         ACT.Copy).then_inc(o_hi_done.sem, 1)
                if n == WO_STEP:
                    act.wait_ge(wo_in.sem, wo_in.value(g, 0))
                    nc.scalar.activation(wo_hi[:], wo_raw[:], ACT.Copy).then_inc(wo_hi_done.sem, 1)

            for j in range(-KVH, 2):
                leave_slot(0, j, PLAN_FIRST)
                if j < 0:
                    i = j + KVH
                    act.wait_ge(v_projected.sem, v_projected.value(0, i))
                    nc.scalar.activation(
                        v_all[:, :, 2 * i:2 * i + 2, :].rearrange("p g t c -> p t g c"),
                        slot[PLAN_FIRST["v", i][0]].rearrange("p (t g c) -> p t g c", t=2, g=KVH),
                        ACT.Copy).then_inc(v_copied.sem, 1)
                if j == -KVH:
                    wq_hi_half(0, 0)
                if j == -1:
                    act.wait_ge(q_normed.sem, q_normed.value(0, NB * (1 - KVH) - 1))
                    act.wait_ge(v_copied.sem, v_copied.value(0, KVH - 1))
                    for b in range(NB):
                        k_hi(0, 0, b)
                        v_hi_half(0, 0, b)
            for j in range(2):
                for b in range(NB):
                    q_hi(0, j, b)
            for n in range(LOOP_START):
                step(0, n, LOOP, PLAN_FIRST)
            with act.Fori(0, KVH - 1) as g:
                for n in range(LOOP_START, LOOP_START + STEPS):
                    step(g, n, LOOP, PLAN_LOOP)
            for n in range(LOOP_START, LOOP_START + STEPS):
                step(KVH - 1, n, LAST, PLAN_LAST)

        @block.vector
        def _(dve):
            dve.sem_inc(wo_split.sem, 1)

            def lo(out, whole, hi):
                return nc.vector.tensor_tensor(out, whole, f32(hi), ALU.subtract)

            dve.wait_ge(wkv_in[0].sem, wkv_in[0].value(0, 0))
            nc.vector.tensor_copy(wkv_hi[0], wkv_raw[0]).then_inc(wkv_hi_done[0].sem, 1)
            dve.wait_ge(wkv_hi_done[0].sem, wkv_hi_done[0].value(0, 0))
            lo(wkv_lo[0], wkv_raw[0], wkv_hi[0]).then_inc(wkv_split[0].sem, 1)
            dve.wait_ge(x_hi_done.sem, x_hi_done.value(0, 0))
            lo(xT_lo[:], resT[:], xT_hi[:]).then_inc(x_lo_done.sem, 1)
            dve.wait_ge(wkv_hi_done[1].sem, wkv_hi_done[1].value(0, 0))
            lo(wkv_lo[1], wkv_raw[1], wkv_hi[1]).then_inc(wkv_split[1].sem, 1)

            def wq_lo_half(g, r):
                dve.wait_ge(wq_hi_done.sem, wq_hi_done.value(g, r))
                lo(wq_lo[:], wq_raw[:], wq_hi[:]).then_inc(wq_split.sem, 1)

            def k_lo(g, r, b):
                cols = slice(b * QB, (b + 1) * QB)
                src = k_norm[:, r, cols] if isinstance(g, int) and g == 0 and r == 0 else k_norm[:, bass.ds(g + r, 1), cols]
                dve.wait_ge(k_hi_done.sem, k_hi_done.value(g, NB * r + b))
                lo(kT_lo[:, cols], src, kT_hi[:, cols]).then_inc(k_split.sem, 1)

            def v_lo_half(g, r, b):
                tiles = slice(b * HALF, (b + 1) * HALF)
                src = v_all[:, r, tiles, :] if isinstance(g, int) and g == 0 and r == 0 else v_all[:, bass.ds(g + r, 1), tiles, :]
                dve.wait_ge(v_hi_done.sem, v_hi_done.value(g, NB * r + b))
                lo(v_lo[:, tiles, :], src, v_hi[:, tiles, :]).then_inc(v_split.sem, 1)

            def mean_square(g, j, b):
                dve.wait_ge(q_turned.sem, q_turned.value(g, NB * j + b))
                if j > -KVH:
                    dve.wait_ge(q_rinv_done.sem, q_rinv_done.value(g, NB * (j - 1) + b))
                nc.vector.tensor_reduce(q_sum[:, b, :], norm_ps(j, b).rearrange("p (i c) -> p i c", i=HALF), AX.X,
                                        ALU.add).then_inc(q_summed.sem, 1)
                dve.wait_ge(q_summed.sem, q_summed.value(g, NB * j + b))
                nc.vector.tensor_scalar(q_var[:, b, :], q_sum[:, b, :], 1.0 / HD, RMS_EPS, ALU.mult,
                                        ALU.add).then_inc(q_var_done.sem, 1)

            def normalise_q(g, j, b):
                dve.wait_ge(q_spread.sem, q_spread.value(g, NB * j + b))
                dve.wait_ge(q_copied.sem, q_copied.value(g, j))
                if j > 0:
                    dve.wait_ge(q_split.sem, q_split.value(g, NB * (j - 1) + b))
                nc.vector.tensor_tensor(q_dst(j, b), raw_of(j)[:, b * QB:(b + 1) * QB], norm_ps(j, b),
                                        ALU.mult).then_inc(q_normed.sem, 1)

            def step(g, n, end, plan):
                if n == NSTEP * 2 - 1 and end == LOOP:
                    wq_lo_half(g, 1)
                if OUT_STEP < n <= OUT_STEP + len(OUT_UNITS):
                    u = n - OUT_STEP - 1
                    b, d = OUT_UNITS[u]
                    cols = slice(b * QB, (b + 1) * QB)
                    dve.wait_ge(out_projected.sem, out_projected.value(g, u))
                    nc.vector.tensor_tensor(resT[:, d, cols], resT[:, d, cols], slot[plan["out", u][0]][:, 0:QB],
                                            ALU.add).then_inc(res_added.sem, 1)
                for p in pairs(n, 5, end):
                    b = p % NB
                    dve.wait_ge(spread.sem, spread.value(g, p))
                    dve.wait_ge(o_copied.sem, o_copied.value(g, p))
                    if p >= NB:
                        dve.wait_ge(o_split.sem, o_split.value(g, p - NB))
                    nc.vector.tensor_tensor(o_norm[:, b, :], o_raw[:, b, :], x_ps[b], ALU.mult).then_inc(o_normed.sem, 1)
                for j, b in q_halves(n, (7, 5), end):
                    mean_square(g, j, b)
                for j, b in q_halves(n, (6, 4), end):
                    normalise_q(g, j, b)
                h, i = divmod(n, NSTEP)
                s, w = n % 2, STEP_WIDTH[i]
                if n < end:
                    if STEP_MASKS[i]:
                        dve.wait_ge(masked.sem, masked.value(g, mask_event(n)))
                    if n >= 2:
                        dve.wait_ge(weighted.sem, weighted.value(g, n - 2))
                    if i not in HI_ON_ACT:
                        nc.vector.tensor_copy(prob_hi[:, s, 0:w], prob[:, s, 0:w]).then_inc(hi_dve.sem, 1)
                    hi_done, event = hi_event(n)
                    dve.wait_ge(hi_done.sem, hi_done.value(g, event))
                    lo(prob_lo[:, s, 0:w], prob[:, s, 0:w], prob_hi[:, s, 0:w]).then_inc(prob_split.sem, 1)
                if n in (STEPS, STEPS + 1) and end == LOOP:
                    v_lo_half(g, 1, n - STEPS)
                if n in (STEPS - 2, STEPS - 1) and end == LOOP:
                    k_lo(g, 1, n - (STEPS - 2))
                if n < end:
                    for k, (head, at, (b, (c0, c1), first, second)) in enumerate(ADDS):
                        if NSTEP * head + at != n:
                            continue
                        to = prob_sum[:, h % 2, b, c0:c1]
                        one = prob[:, s, first:first + c1 - c0]
                        if second is None:
                            dve.wait_ge(added.sem, added.value(g, k - 1))
                            add = nc.vector.tensor_tensor(to, to, one, ALU.add)
                        else:
                            if h >= 2:
                                dve.wait_ge(sums_turned.sem, sums_turned.value(g, NB * (h - 2) + b))
                            if second == "copy":
                                add = nc.vector.tensor_copy(to, one)
                            else:
                                add = nc.vector.tensor_tensor(to, one, prob[:, s, second:second + c1 - c0], ALU.add)
                        add.then_inc(added.sem, 1)
                for p in pairs(n, 3, end):
                    dve.wait_ge(sums_turned.sem, sums_turned.value(g, p))
                    nc.vector.tensor_reduce(key_sum[:, p % NB, :], x_ps[p % NB].rearrange("p (i c) -> p i c", i=HALF),
                                            AX.X, ALU.add).then_inc(sums_done.sem, 1)
                    dve.wait_ge(sums_done.sem, sums_done.value(g, p))
                    nc.vector.reciprocal(inv_sum[:, p % NB, :], key_sum[:, p % NB, :]).then_inc(inv_done.sem, 1)




            for j in range(-KVH, 2):
                for b in range(NB):
                    mean_square(0, j, b)
                if j == -KVH:
                    wq_lo_half(0, 0)
                for b in range(NB):
                    normalise_q(0, j, b)
                if j == -1:
                    for b in range(NB):
                        k_lo(0, 0, b)
                        v_lo_half(0, 0, b)
            for n in range(LOOP_START):
                step(0, n, LOOP, PLAN_FIRST)
            with dve.Fori(0, KVH - 1) as g:
                for n in range(LOOP_START, LOOP_START + STEPS):
                    step(g, n, LOOP, PLAN_LOOP)
            for n in range(LOOP_START, LOOP_START + STEPS):
                step(KVH - 1, n, LAST, PLAN_LAST)

        @block.tensor
        def _(pe):
            pe.wait_ge(consts.sem, consts.value(0, 4))
            pe.wait_ge(x_lo_done.sem, x_lo_done.value(0, 0))

            def accumulate(out, passes, first=True, final=True):
                for j, (stationary, moving) in enumerate(passes):
                    mm = nc.tensor.matmul(out, stationary, moving, start=first and j == 0,
                                          stop=final and j == len(passes) - 1, skip_group_check=True)
                return mm

            def take_slot(g, use, plan):
                s, before = plan[use]
                if before is not None:
                    kind, i = before
                    if kind == "scores":
                        pe.wait_ge(tanh_done.sem, tanh_done.value(g, i))
                    elif kind == "q":
                        pe.wait_ge(q_copied.sem, q_copied.value(g, i))
                    elif kind == "v":
                        pe.wait_ge(v_copied.sem, v_copied.value(g, i))
                    else:
                        pe.wait_ge(res_added.sem, res_added.value(g, i))
                return slot[s]

            def project_q(g, j, plan):
                out = take_slot(g, ("q", j), plan)
                if j < 0:
                    w_hi, w_lo, head = wkv_hi[0], wkv_lo[0], slice((j + KVH) * HD, (j + KVH + 1) * HD)
                    pe.wait_ge(wkv_split[0].sem, wkv_split[0].value(0, 0))
                else:
                    w_hi, w_lo, head = wq_hi, wq_lo, slice(j % G * HD, (j % G + 1) * HD)
                    pe.wait_ge(wq_split.sem, wq_split.value(g, j // G))
                for b in range(NB):
                    cols = slice(b * QB, (b + 1) * QB)
                    mm = accumulate(out[:, cols], [x for c in range(DC) for x in split3(
                        w_hi[:, c, head], w_lo[:, c, head], xT_hi[:, c, cols], xT_lo[:, c, cols])])
                mm.then_inc(q_projected.sem, 1)

            def project_v(i):
                out = take_slot(0, ("v", i), PLAN_FIRST)
                pe.wait_ge(wkv_split[1].sem, wkv_split[1].value(0, 0))
                for t in range(2):
                    tok = slice((2 * i + t) * P, (2 * i + t + 1) * P)
                    mm = accumulate(out[:, t * 512:(t + 1) * 512], [x for c in range(DC) for x in split3(
                        xT_hi[:, c, tok], xT_lo[:, c, tok], wkv_hi[1][:, c, :], wkv_lo[1][:, c, :])])
                mm.then_inc(v_projected.sem, 1)

            def sum_squares(g, j, b):
                pe.wait_ge(q_squared.sem, q_squared.value(g, j))
                if j >= 3:
                    pe.wait_ge(o_normed.sem, o_normed.value(g, NB * (j - 3) + b))
                elif j > 1 - KVH:
                    pe.wait_ge(q_normed.sem, q_normed.value(g, NB * (j - 2) + b))
                turn(norm_ps(j, b), square_of(j)[:, b * QB:(b + 1) * QB]).then_inc(q_turned.sem, 1)

            def turn(out, rows):
                for i in range(HALF):
                    mm = nc.tensor.transpose(out[:, i * P:(i + 1) * P], rows[:, i * P:(i + 1) * P], ident[:])
                return mm

            def spread_columns(out, columns):
                for i in range(HALF):
                    mm = nc.tensor.transpose(out[:, i * P:(i + 1) * P], columns[:, i:i + 1].broadcast_to([P, P]), ident[:])
                return mm

            def spread_rms(g, j, b):
                pe.wait_ge(q_rinv_done.sem, q_rinv_done.value(g, NB * j + b))
                spread_columns(norm_ps(j, b), q_rinv[:, b, :]).then_inc(q_spread.sem, 1)

            def score(g, n, plan):
                h, i = divmod(n, NSTEP)
                out = take_slot(g, ("scores", n), plan)
                pe.wait_ge(q_split.sem, q_split.value(g, NB * h + (i >= 1)))
                if h % G == 0 and i in (0, 2):
                    pe.wait_ge(k_split.sem, k_split.value(g, NB * (h // G) + (i == 2)))
                for b, kt, col, w in HEAD_STEPS[i]:
                    keys = slice(kt * P, (kt + 1) * P)
                    queries = slice((b + 1) * QB - w, (b + 1) * QB)
                    mm = accumulate(out[:, col:col + w], split3(
                        kT_hi[:, keys], kT_lo[:, keys], qT_hi[:, h % 2, queries], qT_lo[:, h % 2, queries]))
                mm.then_inc(scored.sem, 1)

            def weigh(g, n):
                h, i = divmod(n, NSTEP)
                s = n % 2
                pe.wait_ge(prob_split.sem, prob_split.value(g, n))
                if h % G == 0 and i in (0, 2):
                    pe.wait_ge(v_split.sem, v_split.value(g, NB * (h // G) + (i == 2)))
                for b, kt, col, w in HEAD_STEPS[i]:
                    p = NB * h + b
                    if kt == 0:
                        if p >= NB:
                            pe.wait_ge(o_copied.sem, o_copied.value(g, p - NB))
                        else:
                            pe.wait_ge(q_normed.sem, q_normed.value(g, NB + b))
                    mm = accumulate(o_ps[b][:, QB - w:QB], split3(
                        v_hi[:, kt, :], v_lo[:, kt, :], prob_hi[:, s, col:col + w], prob_lo[:, s, col:col + w]),
                        first=kt == 0, final=n == last_step(p))
                mm.then_inc(weighted.sem, 1)

            def sum_keys(g, p, end):
                h, b = divmod(p, NB)
                pe.wait_ge(added.sem, added.value(g, last_add(last_step(p))))
                if h + 2 < end // NSTEP:
                    pe.wait_ge(q_normed.sem, q_normed.value(g, NB * (h + 2) + b))
                elif p >= NB:
                    pe.wait_ge(o_normed.sem, o_normed.value(g, p - NB))
                turn(x_ps[b], prob_sum[:, h % 2, b, :]).then_inc(sums_turned.sem, 1)

            def project_out(g, u, plan):
                b, d = OUT_UNITS[u]
                out = take_slot(g, ("out", u), plan)
                pe.wait_ge(wo_split.sem, wo_split.value(g, 0))
                pe.wait_ge(o_split.sem, o_split.value(g, NB * (G - 1) + b))
                cols, feats = slice(b * QB, (b + 1) * QB), slice(d * P, (d + 1) * P)
                accumulate(out[:, 0:QB], [x for h in range(G) for x in split3(
                    wo_hi[:, h, feats], wo_lo[:, h, feats], oT_hi[:, h, cols], oT_lo[:, h, cols])]
                ).then_inc(out_projected.sem, 1)

            def step(g, n, end, plan):
                for kind, i in step_uses(n, end):
                    if kind == "out":
                        project_out(g, i, plan)
                    elif kind == "scores":
                        score(g, i, plan)
                    else:
                        project_q(g, i, plan)
                for j, b in q_halves(n, (7, 5), end):
                    spread_rms(g, j, b)
                for p in pairs(n, 2, end):
                    sum_keys(g, p, end)
                if n < end:
                    weigh(g, n)
                for j, b in q_halves(n, (9, 7), end):
                    sum_squares(g, j, b)
                for p in pairs(n, 3, end):
                    pe.wait_ge(inv_done.sem, inv_done.value(g, p))
                    spread_columns(x_ps[p % NB], inv_sum[:, p % NB, :]).then_inc(spread.sem, 1)

            for j in range(-KVH, 3):
                if j < 2:
                    project_q(0, j, PLAN_FIRST)
                if j > -KVH:
                    for b in range(NB):
                        sum_squares(0, j - 1, b)
                if j < 0:
                    project_v(j + KVH)
                if j == 2:
                    score(0, 0, PLAN_FIRST)
                if j > -KVH:
                    for b in range(NB):
                        spread_rms(0, j - 1, b)
            score(0, 1, PLAN_FIRST)
            for n in range(LOOP_START):
                step(0, n, LOOP, PLAN_FIRST)
            with pe.Fori(0, KVH - 1) as g:
                for n in range(LOOP_START, LOOP_START + STEPS):
                    step(g, n, LOOP, PLAN_LOOP)
            for n in range(LOOP_START, LOOP_START + STEPS):
                step(KVH - 1, n, LAST, PLAN_LAST)


def experts(nc, kept, dram):
    resT, ident, minus_half = kept["resT"], kept["ident"], kept["minus_half"]
    NSTEPS = NSHARED + 1 + NROUTED
    GATES = NSHARED
    FIRST, LAST = GATES + 3, NSTEPS - 2
    ROUNDS = (LAST - FIRST) // 2
    assert FIRST % 2 == 0 and (LAST - FIRST) % 2 == 0

    def w1_tile(step):
        assert step != GATES
        return step - 1 if step > GATES else step

    def w1_load(step):
        return sum(1 for x in range(step % 2, step, 2) if x != GATES)

    with ExitStack() as ctx:
        def sb(name, shape, dt=F32):
            return ctx.enter_context(nc.sbuf_tensor(name, shape, dt))

        def signal(name, per_round=1, credit=0, unit=1):
            return Signal(ctx.enter_context(nc.semaphore(name)), per_round, credit, unit)

        w1_raw, w2_raw = sb("w1_raw", [P, 2, DC, P]), sb("w2_raw", [P, 2, D])
        w1_hi, w1_lo = sb("w1_hi", [P, 2, DC, P], F32R), sb("w1_lo", [P, 2, DC, P], F32R)
        w2_hi, w2_lo = sb("w2_hi", [P, 2, D], F32R), sb("w2_lo", [P, 2, D], F32R)
        b1 = sb("b1", [P, NSHARED + NROUTED])
        shared_b2 = sb("shared_b2", [P, NS, DC])
        shared_b2_sum = sb("shared_b2_sum", [P, DC])
        shared_b2_mean = sb("shared_b2_mean", [P, DC])
        router = sb("router", [P, DC, NE])
        router_b = sb("router_b", [P, NE])
        stats = sb("stats", [P, 2, NT, 6])
        mean_var = sb("mean_var", [P, 2, NT, 2])
        var_eps = sb("ln_var_eps", [P, 2, NT])
        rstd = sb("rstd", [P, 2, NT])
        x1 = sb("x1", [P, NT, D])
        x1T = sb("x1T", [P, DC, T])
        x1T_hi, x1T_lo = sb("x1T_hi", [P, DC, T], F32R), sb("x1T_lo", [P, DC, T], F32R)
        logits = sb("logits", [P, NT, NE])
        top8 = sb("top8", [P, NT, 8])
        top_id = sb("top_id", [P, NT, 8], U32)
        top_id_f = sb("top_id_f", [P, NT, 8])
        expert_id = sb("expert_id", [P, NE])
        chosen_by = sb("chosen_by", [P, NT, NE, TOPK])
        chosen = sb("chosen", [P, NT, NE])
        below_max = sb("below_max", [P, NT, NE])
        weight = sb("weight", [P, NT, NE])
        kept_weight = sb("kept_weight", [P, NT, NE])
        weight_sum = sb("weight_sum", [P, NT])
        weight_inv = sb("weight_inv", [P, NT])
        gates = sb("gates", [P, NT, NE])
        gates_spread = sb("gates_spread", [P, NT, NE, EROWS])
        gatesT = sb("gatesT", [P, T])
        hidden = sb("hidden", [P, 2, T])
        gated = sb("gated", [P, 2, T])
        h_hi, h_lo = sb("h_hi", [P, 2, T], F32R), sb("h_lo", [P, 2, T], F32R)
        outT = sb("outT", [P, DC, T])
        result = sb("result", [P, NT, D])

        psum = ctx.enter_context(nc.psum_tensor("psum_moe", [P, 8, 512], F32))
        yT = [[psum[:, NB * d + b, :] for b in range(NB)] for d in range(DC)]
        slot = [psum[:, 4 + 2 * s:6 + 2 * s, :].rearrange("p b c -> p (b c)") for s in range(2)]
        norm_in = [psum[:, 4 * k:4 * k + 4, :].rearrange("p b (i c) -> p (b i) c", c=D) for k in range(2)]
        logits_ps = psum[:, 0, 0:NT * NE].rearrange("p (i e) -> p i e", i=NT)

        small_in = signal("moe_small_in", unit=16)
        w1_in = [signal(f"w1_in{s}", unit=16) for s in range(2)]
        w2_in = [signal(f"w2_in{s}", unit=16) for s in range(2)]
        expert_id_done = signal("expert_id_done")
        norm_turned = signal("norm_turned", NT)
        norm_stats = signal("norm_stats", NT)
        norm_mean = signal("norm_mean", NT)
        norm_var = signal("norm_var")
        norm_rstd = signal("norm_rstd")
        normed = signal("moe_normed", NT)
        x1_turned = signal("x1_turned", NB * DC)
        x1_hi_done = signal("x1_hi_done", NB * DC)
        x1_copied = signal("x1_copied", NB * DC)
        x1_split = signal("x1_split", NB * DC)
        bias_done = signal("bias_done")
        logits_done = signal("logits_done")
        routed = signal("routed")
        below_max_done = signal("below_max_done")
        weight_done = signal("weight_done")
        gates_done = signal("gates_done")
        w1_hi_done, w1_split = signal("w1_hi_done", 2), signal("w1_split", 2)
        w2_hi_done, w2_split = signal("w2_hi_done", 2), signal("w2_split", 2)
        upped = signal("upped", 2)
        relu_done = signal("relu_done", 2)
        gate_done = signal("gate_done", 2)
        h_hi_done = signal("h_hi_done", 2)
        h_split = signal("h_split", 2)
        downed = signal("downed", 2)
        res_done = signal("moe_res_done", NB * DC)
        stored = signal("stored", unit=16)

        block = ctx.enter_context(nc.Block())


        @block.sync
        def _(sp):
            def load(g, step):
                s = step % 2
                if step != GATES:
                    if step >= 2:
                        before = step - 2 if step - 2 != GATES else step - 4
                        sp.wait_ge(w1_split.sem, w1_split.value(g, w1_tile(before)))
                    sp.dma_start(w1_raw[:, s], dram["w1"][2 * g + w1_tile(step)]).then_inc(w1_in[s].sem, 16)
                if step >= 2:
                    sp.wait_ge(w2_split.sem, w2_split.value(g, step - 2))
                sp.dma_start(w2_raw[:, s], dram["w2"][2 * g + step]).then_inc(w2_in[s].sem, 16)

            load(0, 0)
            load(0, 1)
            for to, of in ((router, "router"), (router_b, "router_b"), (b1, "b1"), (shared_b2, "shared_b2")):
                sp.dma_start(to[:], dram[of]).then_inc(small_in.sem, 16)
            for step in range(2, FIRST):
                load(0, step)
            with sp.Fori(0, ROUNDS) as g:
                load(g, FIRST)
                load(g, FIRST + 1)
            for step in range(LAST, NSTEPS):
                load(0, step)
            out = dram["out"].rearrange("(i p) d -> p i d", p=P)
            for b in range(NB):
                tiles = slice(b * HALF, (b + 1) * HALF)
                sp.wait_ge(normed.sem, normed.value(1, (b + 1) * HALF - 1))
                sp.dma_start(out[:, tiles, :], result[:, tiles, :]).then_inc(stored.sem, 16)
            sp.wait_ge(stored.sem, stored.value(0, NB - 1))

        @block.gpsimd
        def _(pool):
            nc.gpsimd.iota(expert_id[:], pattern=[[1, NE]], base=0, channel_multiplier=0,
                           allow_small_or_imprecise_dtypes=True).then_inc(expert_id_done.sem, 1)
            for k in range(2):
                pool.wait_ge(norm_var.sem, norm_var.value(k, 0))
                nc.gpsimd.tensor_tensor(rstd[:, k, :], var_eps[:, k, :], minus_half[:],
                                        ALU.pow).then_inc(norm_rstd.sem, 1)

        @block.scalar
        def _(act):
            for u in range(NB * DC):
                b, d = divmod(u, DC)
                cols = slice(b * QB, (b + 1) * QB)
                turned = slot[b][:, d * QB:(d + 1) * QB]
                act.wait_ge(x1_turned.sem, x1_turned.value(0, u))
                nc.scalar.activation(x1T_hi[:, d, cols], turned, ACT.Copy).then_inc(x1_hi_done.sem, 1)
                nc.scalar.activation(x1T[:, d, cols], turned, ACT.Copy).then_inc(x1_copied.sem, 1)
            act.wait_ge(small_in.sem, small_in.value(0, 3))

            def relu(g, step):
                s = step % 2
                act.wait_ge(upped.sem, upped.value(g, step))
                if step >= 2:
                    act.wait_ge(gate_done.sem, gate_done.value(g, step - 2))
                if step == GATES:
                    nc.scalar.activation(gatesT[:], slot[s], ACT.Copy).then_inc(relu_done.sem, 1)
                else:
                    t = w1_tile(step) if step < FIRST or step >= LAST + 1 else bass.ds(2 * g + w1_tile(step), 1)
                    bias = b1[:, t:t + 1] if isinstance(t, int) else b1[:, t]
                    nc.scalar.activation(hidden[:, s, :], slot[s], ACT.Relu, bias=bias).then_inc(relu_done.sem, 1)

            def hi(g, step):
                s = step % 2
                act.wait_ge(gate_done.sem, gate_done.value(g, step))
                if step >= 2:
                    act.wait_ge(downed.sem, downed.value(g, step - 2))
                nc.scalar.activation(h_hi[:, s, :], gated[:, s, :], ACT.Copy).then_inc(h_hi_done.sem, 1)

            relu(0, 0)
            for step in range(FIRST - 1):
                relu(0, step + 1)
                hi(0, step)
                if step == 0:
                    act.wait_ge(below_max_done.sem, below_max_done.value(0, 0))
                    nc.scalar.activation(weight[:], below_max[:], ACT.Exp).then_inc(weight_done.sem, 1)
            with act.Fori(0, ROUNDS) as g:
                for step in (FIRST, FIRST + 1):
                    relu(g, step)
                    hi(g, step - 1)
            for step in range(LAST, NSTEPS):
                relu(0, step)
                hi(0, step - 1)
            hi(0, NSTEPS - 1)

        @block.vector
        def _(dve):
            def statistics(k):
                for i in range(NT):
                    dve.wait_ge(norm_turned.sem, norm_turned.value(k, i | 1))
                    nc.vector.bn_stats(stats[:, k, i, :], norm_in[k][:, i, :]).then_inc(norm_stats.sem, 1)
                for i in range(NT):
                    dve.wait_ge(norm_stats.sem, norm_stats.value(k, i))
                    nc.vector.bn_aggr(mean_var[:, k, i, :], stats[:, k, i, :]).then_inc(norm_mean.sem, 1)
                dve.wait_ge(norm_mean.sem, norm_mean.value(k, NT - 1))
                nc.vector.tensor_scalar(var_eps[:, k, :], mean_var[:, k, :, 1], LN_EPS, None,
                                        ALU.add).then_inc(norm_var.sem, 1)

            def normalise(k, to):
                dve.wait_ge(norm_rstd.sem, norm_rstd.value(k, 0))
                for i in range(NT):
                    nc.vector.tensor_scalar(to[:, i, :], norm_in[k][:, i, :], mean_var[:, k, i, 0:1],
                                            rstd[:, k, i:i + 1], ALU.subtract, ALU.mult).then_inc(normed.sem, 1)

            def split_w1(g, step):
                s = step % 2
                t = w1_tile(step)
                dve.wait_ge(w1_in[s].sem, w1_in[s].value(g, w1_load(step)))
                if step >= 2:
                    dve.wait_ge(upped.sem, upped.value(g, step - 2))
                nc.vector.tensor_copy(w1_hi[:, s], w1_raw[:, s]).then_inc(w1_hi_done.sem, 1)
                dve.wait_ge(w1_hi_done.sem, w1_hi_done.value(g, t))
                nc.vector.tensor_tensor(w1_lo[:, s], w1_raw[:, s], f32(w1_hi[:, s]), ALU.subtract).then_inc(w1_split.sem, 1)

            def split_w2(g, step):
                s = step % 2
                dve.wait_ge(w2_in[s].sem, w2_in[s].value(g, step // 2))
                if step >= 2:
                    dve.wait_ge(downed.sem, downed.value(g, step - 2))
                nc.vector.tensor_copy(w2_hi[:, s], w2_raw[:, s]).then_inc(w2_hi_done.sem, 1)
                dve.wait_ge(w2_hi_done.sem, w2_hi_done.value(g, step))
                nc.vector.tensor_tensor(w2_lo[:, s], w2_raw[:, s], f32(w2_hi[:, s]), ALU.subtract).then_inc(w2_split.sem, 1)

            def hidden_step(g, step):
                s = step % 2
                split_w2(g, step)
                dve.wait_ge(relu_done.sem, relu_done.value(g, step))
                if step < GATES:
                    gate = nc.vector.tensor_scalar(gated[:, s, :], hidden[:, s, :], 1.0 / NS, None, ALU.mult)
                elif step == GATES:
                    gate = nc.vector.tensor_scalar(gated[:, s, :], gatesT[:], 1.0 / EROWS, None, ALU.mult)
                else:
                    gate = nc.vector.tensor_tensor(gated[:, s, :], hidden[:, s, :], gatesT[:], ALU.mult)
                gate.then_inc(gate_done.sem, 1)
                if step + 2 < NSTEPS and step + 2 != GATES:
                    split_w1(g, step + 2)
                dve.wait_ge(h_hi_done.sem, h_hi_done.value(g, step))
                nc.vector.tensor_tensor(h_lo[:, s, :], gated[:, s, :], f32(h_hi[:, s, :]), ALU.subtract).then_inc(h_split.sem, 1)

            statistics(0)
            split_w1(0, 0)
            normalise(0, x1)
            split_w1(0, 1)
            for u in range(NB * DC):
                b, d = divmod(u, DC)
                cols = slice(b * QB, (b + 1) * QB)
                dve.wait_ge(x1_copied.sem, x1_copied.value(0, u))
                nc.vector.tensor_tensor(x1T_lo[:, d, cols], slot[b][:, d * QB:(d + 1) * QB], f32(x1T_hi[:, d, cols]),
                                        ALU.subtract).then_inc(x1_split.sem, 1)
            dve.wait_ge(small_in.sem, small_in.value(0, 3))
            nc.vector.tensor_tensor(shared_b2_sum[:], shared_b2[:, 0, :], shared_b2[:, 1, :], ALU.add).then_inc(bias_done.sem, 1)
            dve.wait_ge(bias_done.sem, bias_done.value(0, 0))
            nc.vector.tensor_scalar(shared_b2_mean[:], shared_b2_sum[:], 1.0 / NS, None, ALU.mult).then_inc(bias_done.sem, 1)

            dve.wait_ge(logits_done.sem, logits_done.value(0, 0))
            nc.vector.tensor_tensor(logits[:], logits_ps, router_b[:].unsqueeze(1).broadcast_to([P, NT, NE]),
                                    ALU.add).then_inc(routed.sem, 1)
            dve.wait_ge(routed.sem, routed.value(0, 0))
            for i in range(NT):
                last = nc.vector.max(top8[:, i, :], logits[:, i, :])
            last.then_inc(routed.sem, 1)
            dve.wait_ge(routed.sem, routed.value(0, 1))
            nc.vector.tensor_tensor(below_max[:], logits[:], top8[:, :, 0:1].broadcast_to([P, NT, NE]),
                                    ALU.subtract).then_inc(below_max_done.sem, 1)
            for i in range(NT):
                last = nc.vector.max_index(top_id[:, i, :], top8[:, i, :], logits[:, i, :])
            last.then_inc(routed.sem, 1)
            dve.wait_ge(routed.sem, routed.value(0, 2))
            nc.vector.tensor_copy(top_id_f[:], top_id[:]).then_inc(routed.sem, 1)

            hidden_step(0, 0)

            dve.wait_ge(routed.sem, routed.value(0, 3))
            dve.wait_ge(expert_id_done.sem, expert_id_done.value(0, 0))
            nc.vector.tensor_tensor(
                chosen_by[:], expert_id[:].unsqueeze(1).unsqueeze(3).broadcast_to([P, NT, NE, TOPK]),
                top_id_f[:, :, 0:TOPK].unsqueeze(2).broadcast_to([P, NT, NE, TOPK]), ALU.is_equal).then_inc(routed.sem, 1)
            dve.wait_ge(routed.sem, routed.value(0, 4))
            nc.vector.tensor_reduce(chosen[:], chosen_by[:], AX.X, ALU.max).then_inc(routed.sem, 1)
            dve.wait_ge(routed.sem, routed.value(0, 5))
            dve.wait_ge(weight_done.sem, weight_done.value(0, 0))
            nc.vector.tensor_tensor(kept_weight[:], weight[:], chosen[:], ALU.mult).then_inc(routed.sem, 1)
            dve.wait_ge(routed.sem, routed.value(0, 6))
            nc.vector.tensor_reduce(weight_sum[:], kept_weight[:], AX.X, ALU.add).then_inc(routed.sem, 1)
            dve.wait_ge(routed.sem, routed.value(0, 7))
            nc.vector.reciprocal(weight_inv[:], weight_sum[:]).then_inc(routed.sem, 1)
            dve.wait_ge(routed.sem, routed.value(0, 8))
            nc.vector.tensor_tensor(gates[:], kept_weight[:], weight_inv[:].unsqueeze(2).broadcast_to([P, NT, NE]),
                                    ALU.mult).then_inc(routed.sem, 1)
            dve.wait_ge(routed.sem, routed.value(0, 9))
            nc.vector.tensor_copy(gates_spread[:], gates[:].unsqueeze(3).broadcast_to([P, NT, NE, EROWS])
                                  ).then_inc(gates_done.sem, 1)

            for step in range(1, FIRST):
                hidden_step(0, step)
            with dve.Fori(0, ROUNDS) as g:
                hidden_step(g, FIRST)
                hidden_step(g, FIRST + 1)
            for step in range(LAST, NSTEPS):
                hidden_step(0, step)

            dve.wait_ge(downed.sem, downed.value(0, NSTEPS - 1))
            for b in range(NB):
                for d in range(DC):
                    cols = slice(b * QB, (b + 1) * QB)
                    nc.vector.scalar_tensor_tensor(out=outT[:, d, cols], in0=yT[d][b], scalar=shared_b2_mean[:, d:d + 1],
                                                   in1=x1T[:, d, cols], op0=ALU.add,
                                                   op1=ALU.add).then_inc(res_done.sem, 1)
            statistics(1)
            normalise(1, result)

        @block.tensor
        def _(pe):
            def turn_for_norm(k, src, i):
                tok = slice(i * P, (i + 1) * P)
                for d in range(DC):
                    mm = nc.tensor.transpose(norm_in[k][:, i, d * P:(d + 1) * P], src[:, d, tok], ident[:])
                mm.then_inc(norm_turned.sem, 1)

            def up(g, step):
                s = step % 2
                if step >= 2:
                    pe.wait_ge(relu_done.sem, relu_done.value(g, step - 2))
                if step == GATES:
                    pe.wait_ge(gates_done.sem, gates_done.value(0, 0))
                    for i in range(NT):
                        mm = nc.tensor.transpose(slot[s][:, i * P:(i + 1) * P],
                                                 gates_spread[:, i].rearrange("p e r -> p (e r)"), ident[:])
                    mm.then_inc(upped.sem, 1)
                    return
                pe.wait_ge(w1_split.sem, w1_split.value(g, w1_tile(step)))
                for b in range(NB):
                    cols = slice(b * QB, (b + 1) * QB)
                    if step == 0:
                        pe.wait_ge(x1_split.sem, x1_split.value(0, DC * b + DC - 1))
                        pe.wait_ge(x1_copied.sem, x1_copied.value(0, DC * b + DC - 1))
                    passes = [x for c in range(DC) for x in split3(
                        w1_hi[:, s, c, :], w1_lo[:, s, c, :], x1T_hi[:, c, cols], x1T_lo[:, c, cols])]
                    for j, (stationary, moving) in enumerate(passes):
                        mm = nc.tensor.matmul(slot[s][:, cols], stationary, moving, start=j == 0,
                                              stop=j == len(passes) - 1)
                mm.then_inc(upped.sem, 1)

            def down(g, step):
                s = step % 2
                pe.wait_ge(h_split.sem, h_split.value(g, step))
                for d in range(DC):
                    feats = slice(d * P, (d + 1) * P)
                    for b in range(NB):
                        cols = slice(b * QB, (b + 1) * QB)
                        for j, (stationary, moving) in enumerate(split3(
                                w2_hi[:, s, feats], w2_lo[:, s, feats], h_hi[:, s, cols], h_lo[:, s, cols])):
                            mm = nc.tensor.matmul(yT[d][b], stationary, moving, start=step == 0 and j == 0,
                                                  stop=step == NSTEPS - 1 and j == 2, skip_group_check=True)
                mm.then_inc(downed.sem, 1)

            for i in range(NT):
                turn_for_norm(0, resT, i)
            for b in range(NB):
                for d in range(DC):
                    for i in range(b * HALF, (b + 1) * HALF):
                        pe.wait_ge(normed.sem, normed.value(0, i))
                        at = d * QB + (i - b * HALF) * P
                        mm = nc.tensor.transpose(slot[b][:, at:at + P], x1[:, i, d * P:(d + 1) * P], ident[:])
                    mm.then_inc(x1_turned.sem, 1)
            up(0, 0)
            pe.wait_ge(small_in.sem, small_in.value(0, 3))
            for i in range(NT):
                for c in range(DC):
                    mm = nc.tensor.matmul(logits_ps[:, i, :], x1T[:, c, i * P:(i + 1) * P], router[:, c, :],
                                          start=c == 0, stop=c == DC - 1)
            mm.then_inc(logits_done.sem, 1)
            up(0, 1)
            for step in range(FIRST - 2):
                up(0, step + 2)
                if step == 0:
                    pe.wait_ge(routed.sem, routed.value(0, 0))
                down(0, step)
            with pe.Fori(0, ROUNDS) as g:
                for step in (FIRST, FIRST + 1):
                    up(g, step)
                    down(g, step - 2)
            for step in range(LAST, NSTEPS):
                up(0, step)
                down(0, step - 2)
            for step in (NSTEPS - 2, NSTEPS - 1):
                down(0, step)
            for i in range(NT):
                if i % HALF == 0:
                    pe.wait_ge(relu_done.sem, relu_done.value(0, NSTEPS - 1))
                    pe.wait_ge(res_done.sem, res_done.value(0, DC * (i // HALF) + DC - 1))
                turn_for_norm(1, outT, i)


def layer(nc, dram):
    with ExitStack() as ctx:
        kept = {
            "resT": ctx.enter_context(nc.sbuf_tensor("resT", [P, DC, T], F32)),
            "ident": ctx.enter_context(nc.sbuf_tensor("ident", [P, P], F32)),
            "minus_half": ctx.enter_context(nc.sbuf_tensor("minus_half", [P, NT], F32)),
        }
        attention(nc, kept, dram)
        experts(nc, kept, dram)


def laid_out(inputs):
    import numpy as np

    x = np.asarray(inputs["L0_attn_x"])[0]
    f = {k: np.asarray(v) for k, v in inputs.items()}

    def by_round(w, rounds):
        return w.T.reshape(DC, P, rounds, -1).transpose(2, 1, 0, 3)

    pad = NSHARED * P - NS * HID
    sw1 = np.pad(f["L0_ffn_sw1"].transpose(1, 0, 2).reshape(D, NS * HID), ((0, 0), (0, pad)))
    sw2 = np.pad(f["L0_ffn_sw2"].reshape(NS * HID, D), ((0, pad), (0, 0)))
    sb1 = np.pad(f["L0_ffn_sb1"].reshape(NS * HID), (0, pad))
    rw1 = f["L0_ffn_rw1"].reshape(NE, DC, P, NROUTED, EROWS).transpose(3, 2, 1, 0, 4).reshape(NROUTED, P, DC, P)
    rw2 = f["L0_ffn_rw2"].reshape(NE, NROUTED, EROWS, D).transpose(1, 0, 2, 3).reshape(NROUTED, P, D)
    rb1 = f["L0_ffn_rb1"].reshape(NE, NROUTED, EROWS).transpose(0, 2, 1).reshape(P, NROUTED)
    sw1 = sw1.reshape(DC, P, NSHARED, P).transpose(2, 1, 0, 3)
    return {
        "xT": x.T.reshape(DC, P, T).transpose(1, 0, 2),
        "wq": by_round(f["L0_attn_wq"], KVH),
        "wkv": np.concatenate([by_round(f["L0_attn_wk"], 1), by_round(f["L0_attn_wv"], 1)]),
        "wo": f["L0_attn_wo"].T.reshape(KVH, G, P, D).transpose(0, 2, 1, 3),
        "gammas": np.stack([f["L0_attn_q_gamma"], f["L0_attn_k_gamma"]], 1),
        "w1": np.concatenate([sw1, rw1]),
        "w2": np.concatenate([sw2.reshape(NSHARED, P, D), np.repeat(f["L0_ffn_rb2"], EROWS, 0)[None], rw2]),
        "b1": np.concatenate([sb1.reshape(NSHARED, P).T, rb1], 1),
        "shared_b2": f["L0_ffn_sb2"].reshape(NS, DC, P).transpose(2, 0, 1),
        "router": f["L0_ffn_router_w"].reshape(DC, P, NE).transpose(1, 0, 2),
        "router_b": np.broadcast_to(f["L0_ffn_router_b"], (P, NE)),
    }


def kernel(**inputs):
    import numpy as np
    from concourse import bacc
    from concourse.bass_utils import run_bass_kernel_spmd

    nc = bacc.Bacc("TRN2", target_bir_lowering=False, num_devices=1)
    arrays, dram = {}, {}
    for name, a in laid_out(inputs).items():
        arrays[f"in_{name}"] = np.ascontiguousarray(a)
        dram[name] = nc.dram_tensor(f"in_{name}", a.shape, F32, kind="ExternalInput").ap()
    dram["out"] = nc.dram_tensor("out_x", (T, D), F32, kind="ExternalOutput").ap()
    layer(nc, dram)
    r = run_bass_kernel_spmd(nc, [arrays], core_ids=[0])
    return r.results[0]["out_x"].reshape(1, T, D)
```

```python
from contextlib import ExitStack

import concourse.bass as bass
from concourse import mybir

F32 = mybir.dt.float32
F32R = mybir.dt.float32r
U32 = mybir.dt.uint32
ALU = mybir.AluOpType
ACT = mybir.ActivationFunctionType
AX = mybir.AxisListType

P = 128
T, D = 1024, 256
H, KVH, HD = 16, 4, 128
G = H // KVH
NT = T // P
DC = D // P
QB = 512
NB = T // QB
CAP, RMS_EPS, LN_EPS = 50.0, 1e-6, 1e-5
SCALE = HD ** -0.5

NE, NS, HID, TOPK = 32, 2, 176, 6
EROWS = P // NE
NROUTED = HID // EROWS
NSHARED = -(-NS * HID // P)

HEAD_STEPS = (
    ((0, 0, 0, 512), (0, 3, 512, 128), (0, 1, 640, 384)),
    ((1, 0, 0, 512), (1, 1, 512, 512)),
    ((0, 2, 0, 256), (1, 6, 256, 256)),
    ((1, 2, 0, 512), (1, 3, 512, 512)),
    ((1, 4, 0, 512), (1, 7, 512, 128), (1, 5, 640, 384)),
)
STEP_WIDTH = (1024, 1024, 512, 1024, 1024)
STEP_MASKS = (((0, 1, 128), (512, 2, 128)), (), ((0, 2, 256),), (), ((0, 1, 128), (512, 2, 128)))
STEP_ADDS = (
    ((0, (0, 128), 0, "copy"), (0, (128, 512), 128, 640), (0, (384, 512), 512, None)),
    ((1, (0, 512), 0, 512),),
    ((0, (256, 512), 0, None), (1, (256, 512), 256, None)),
    ((1, (0, 512), 0, None), (1, (0, 512), 512, None)),
    ((1, (0, 512), 0, None), (1, (128, 512), 640, None), (1, (384, 512), 512, None)),
)
NSTEP = len(HEAD_STEPS)
STEPS = G * NSTEP
PAIRS = NB * G
HI_ON_ACT = (1, 3)
HALF = NT // NB

LOOP_START = 9


def last_step(p):
    return NSTEP * (p // NB) + (2, 4)[p % NB]


def pairs(n, lag, end):
    return [p for p in range(NB * end // NSTEP) if last_step(p) + lag == n]


def q_heads(n, lead, end):
    return [j for j in range(2, end // NSTEP) if NSTEP * j - lead == n]


def q_halves(n, leads, end):
    return [(j, b) for b in range(NB) for j in q_heads(n, leads[b], end)]


OUT_UNITS = [(b, d) for b in range(NB) for d in range(DC)]
OUT_STEP = 24
WO_STEP = 14
LOOP, LAST = 2 * STEPS, STEPS


def slots(uses, first=0):
    return {u: ((first + i) % 2, uses[i - 2] if i >= 2 else None) for i, u in enumerate(uses)}


def step_uses(n, end):
    scores = [("scores", n + 2)] if n + 2 < end else []
    out = [("out", n - OUT_STEP)] if OUT_STEP <= n < OUT_STEP + len(OUT_UNITS) and end == LOOP else []
    q = [("q", j) for j in q_heads(n, 10, end)]
    return (out + scores if n == OUT_STEP + len(OUT_UNITS) - 1 else scores + out) + q


FRONT = (-KVH, 0, 1) + tuple(range(1 - KVH, 0))
FIRST_USES = [u for k in range(KVH) for u in (("q", FRONT[k]), ("v", k))]
FIRST_USES += [("q", j) for j in FRONT[KVH:]] + [("scores", 0), ("scores", 1)]
PLAN_FIRST = slots(FIRST_USES + [u for n in range(LOOP_START) for u in step_uses(n, LOOP)])
CARRIED = [("scores", LOOP_START), ("scores", LOOP_START + 1)]
PLAN_LOOP = slots(CARRIED + [u for n in range(LOOP_START, LOOP_START + STEPS) for u in step_uses(n, LOOP)],
                  PLAN_FIRST[CARRIED[0]][0])
PLAN_LAST = slots(CARRIED + [u for n in range(LOOP_START, LOOP_START + STEPS) for u in step_uses(n, LAST)],
                  PLAN_FIRST[CARRIED[0]][0])
for u in CARRIED:
    assert PLAN_FIRST[u][0] == PLAN_LOOP[u][0] == PLAN_LOOP[u[0], u[1] + STEPS][0]


def nth(j):
    return FRONT.index(j) - KVH if j < 2 else j


LAST_OUT = {STEPS - 1: ((0, (0, 1)),), STEPS: ((1, (0, 1)), (0, (2,))), STEPS + 2: ((1, (2,)),),
            STEPS + 4: ((0, (3,)),), STEPS + 6: ((1, (3,)),)}


class Signal:

    def __init__(self, sem, per_round=1, credit=0, unit=1):
        self.sem, self.per_round, self.credit, self.unit = sem, per_round, credit, unit

    def value(self, g, n):
        return g * (self.per_round * self.unit) + (n + 1 + self.credit) * self.unit


def f32(ap):
    return ap.bitcast(F32)


def split3(stat_hi, stat_lo, move_hi, move_lo):
    return ((stat_hi, move_hi), (stat_lo, move_hi), (stat_hi, move_lo))


ADDS = [(h, i, a) for h in range(LOOP // NSTEP) for i in range(NSTEP) for a in STEP_ADDS[i]]


def last_add(n):
    return max(k for k, (h, i, _) in enumerate(ADDS) if NSTEP * h + i == n)


def attention(nc, kept, dram):
    resT, ident, minus_half = kept["resT"], kept["ident"], kept["minus_half"]
    with ExitStack() as ctx:
        def sb(name, shape, dt=F32):
            return ctx.enter_context(nc.sbuf_tensor(name, shape, dt))

        def signal(name, per_round=1, credit=0, unit=1):
            return Signal(ctx.enter_context(nc.semaphore(name)), per_round, credit, unit)

        xT_hi, xT_lo = sb("xT_hi", [P, DC, T], F32R), sb("xT_lo", [P, DC, T], F32R)
        wq_raw = sb("wq_raw", [P, DC, G * HD])
        wq_hi, wq_lo = sb("wq_hi", [P, DC, G * HD], F32R), sb("wq_lo", [P, DC, G * HD], F32R)
        wo_raw = sb("wo_raw", [P, G, D])
        wo_hi, wo_lo = sb("wo_hi", [P, G, D], F32R), sb("wo_lo", [P, G, D], F32R)
        gammas = sb("gammas", [P, 2])
        causal = sb("causal", [P, 2, P])
        q_square = sb("q_square", [P, T])
        q_raw = sb("q_raw", [P, T])
        q_sum = sb("q_sum", [P, NB, HALF])
        q_var = sb("q_var", [P, NB, HALF])
        q_rinv = sb("q_rinv", [P, NB, HALF])
        q_norm = sb("q_norm", [P, NB, QB])
        qT_hi, qT_lo = sb("qT_hi", [P, 2, T], F32R), sb("qT_lo", [P, 2, T], F32R)
        k_norm = sb("k_norm", [P, KVH, T])
        v_all = sb("v_all", [P, KVH, NT, HD])
        kT_hi, kT_lo = sb("kT_hi", [P, T], F32R), sb("kT_lo", [P, T], F32R)
        v_hi, v_lo = sb("v_hi", [P, NT, HD], F32R), sb("v_lo", [P, NT, HD], F32R)
        capped = sb("capped", [P, 2, 1024])
        prob = sb("prob", [P, 2, 1024])
        prob_hi, prob_lo = sb("prob_hi", [P, 2, 1024], F32R), sb("prob_lo", [P, 2, 1024], F32R)
        prob_sum = sb("prob_sum", [P, 2, NB, QB])
        key_sum = sb("key_sum", [P, NB, HALF])
        inv_sum = sb("inv_sum", [P, NB, HALF])
        o_raw = sb("o_raw", [P, NB, QB])
        o_norm = sb("o_norm", [P, NB, QB])
        oT_hi, oT_lo = sb("oT_hi", [P, G, T], F32R), sb("oT_lo", [P, G, T], F32R)
        wkv_raw = [capped[:, n, :].rearrange("p (c k) -> p c k", c=DC) for n in range(2)]
        wkv_hi = [oT_hi[:, n, :].rearrange("p (c k) -> p c k", c=DC) for n in range(2)]
        wkv_lo = [oT_lo[:, n, :].rearrange("p (c k) -> p c k", c=DC) for n in range(2)]

        psum = ctx.enter_context(nc.psum_tensor("psum_attn", [P, 8, 512], F32))
        slot = [psum[:, 2 * s:2 * s + 2, :].rearrange("p b c -> p (b c)") for s in range(2)]
        o_ps = [psum[:, 4 + b, :] for b in range(NB)]
        x_ps = [psum[:, 6 + b, :] for b in range(NB)]

        def norm_ps(j, b):
            return (o_ps if j < 2 and nth(j) % 2 else x_ps)[b]

        def square_of(j):
            return o_raw[:].rearrange("p b c -> p (b c)") if j < 2 and nth(j) % 2 else q_square[:]

        def raw_of(j):
            return o_norm[:].rearrange("p b c -> p (b c)") if j < 2 and nth(j) % 2 else q_raw[:]

        x_in = [signal(f"x_in{b}", unit=16) for b in range(NB)]
        gammas_in = signal("gammas_in", unit=16)
        wkv_in = [signal(f"w{n}_in", unit=16) for n in "kv"]
        wq_in = signal("wq_in", unit=16)
        wo_in = signal("wo_in", unit=16)
        consts = signal("consts")
        x_hi_done, x_lo_done = signal("x_hi_done"), signal("x_lo_done")
        wkv_hi_done = [signal(f"w{n}_hi_done") for n in "kv"]
        wkv_split = [signal(f"w{n}_split") for n in "kv"]
        wq_hi_done, wq_split = signal("wq_hi_done"), signal("wq_split")
        wo_hi_done, wo_split = signal("wo_hi_done"), signal("wo_split", credit=1)
        v_projected, v_copied = signal("v_projected", KVH), signal("v_copied", KVH)
        q_projected = signal("q_projected", G, credit=KVH)
        q_squared = signal("q_squared", G, credit=KVH)
        q_copied = signal("q_copied", G, credit=KVH)
        q_turned = signal("q_turned", NB * G, credit=NB * KVH)
        q_summed = signal("q_summed", NB * G, credit=NB * KVH)
        q_var_done = signal("q_var_done", NB * G, credit=NB * KVH)
        q_rinv_done = signal("q_rinv_done", NB * G, credit=NB * KVH)
        q_spread = signal("q_spread", NB * G, credit=NB * KVH)
        q_normed = signal("q_normed", NB * G, credit=NB * KVH)
        q_hi_done = signal("q_hi_done", NB * G)
        q_split = signal("q_split", NB * G)
        k_hi_done, k_split = signal("k_hi_done", NB), signal("k_split", NB)
        v_hi_done, v_split = signal("v_hi_done", NB), signal("v_split", NB)
        scored = signal("scored", STEPS)
        tanh_done = signal("tanh_done", STEPS)
        exp_done = signal("exp_done", STEPS)
        masked = signal("masked", 3 * G)
        hi_act = signal("hi_act", len(HI_ON_ACT) * G)
        hi_dve = signal("hi_dve", (NSTEP - len(HI_ON_ACT)) * G)
        prob_split = signal("prob_split", STEPS)
        added = signal("added", len(ADDS) // 2)
        weighted = signal("weighted", STEPS)
        sums_turned = signal("sums_turned", PAIRS)
        sums_done = signal("sums_done", PAIRS)
        inv_done = signal("inv_done", PAIRS)
        spread = signal("spread", PAIRS)
        o_copied = signal("o_copied", PAIRS)
        o_normed = signal("o_normed", PAIRS)
        o_hi_done = signal("o_hi_done", PAIRS)
        o_split = signal("o_split", PAIRS)
        out_projected = signal("out_projected", len(OUT_UNITS))
        res_added = signal("res_added", len(OUT_UNITS))

        def out_at(u, end, plan):
            if end == LAST:
                b, d = OUT_UNITS[u]
                return slot[plan["scores", STEPS - 2 + b][0]][:, d * QB:(d + 1) * QB]
            return slot[plan["out", u][0]][:, 0:QB]

        def hi_event(n):
            h, i = divmod(n, NSTEP)
            if i in HI_ON_ACT:
                return hi_act, h * len(HI_ON_ACT) + HI_ON_ACT.index(i)
            rest = [j for j in range(NSTEP) if j not in HI_ON_ACT]
            return hi_dve, h * len(rest) + rest.index(i)

        def mask_event(n):
            return 3 * (n // NSTEP) + (n % NSTEP) // 2



        def q_dst(j, b):
            return k_norm[:, j + KVH, b * QB:(b + 1) * QB] if j < 0 else q_norm[:, b, :]

        block = ctx.enter_context(nc.Block())

        @block.sync
        def _(sp):
            for b in range(NB):
                cols = slice(b * QB, (b + 1) * QB)
                sp.dma_start(resT[:, :, cols], dram["xT"][:, :, cols]).then_inc(x_in[b].sem, 16)
                sp.dma_start(wkv_raw[b], dram["wkv"][b]).then_inc(wkv_in[b].sem, 16)
            sp.dma_start(gammas[:], dram["gammas"]).then_inc(gammas_in.sem, 16)
            sp.dma_start(wq_raw[:], dram["wq"][0]).then_inc(wq_in.sem, 16)
            with sp.Fori(0, KVH - 1) as g:
                sp.wait_ge(wo_split.sem, wo_split.value(g, -1))
                sp.dma_start(wo_raw[:], dram["wo"][g]).then_inc(wo_in.sem, 16)
                sp.wait_ge(wq_split.sem, wq_split.value(g, 0))
                sp.dma_start(wq_raw[:], dram["wq"][g + 1]).then_inc(wq_in.sem, 16)
            sp.wait_ge(wo_split.sem, wo_split.value(KVH - 1, -1))
            sp.dma_start(wo_raw[:], dram["wo"][KVH - 1]).then_inc(wo_in.sem, 16)

        @block.gpsimd
        def _(pool):
            nc.gpsimd.memset(minus_half[:], -0.5).then_inc(consts.sem, 1)
            nc.gpsimd.memset(ident[:], 0.0).then_inc(consts.sem, 1)
            nc.gpsimd.memset(causal[:], 1.0).then_inc(consts.sem, 1)
            pool.wait_ge(consts.sem, consts.value(0, 2))
            nc.gpsimd.affine_select(out=ident[:], in_=ident[:], compare_op=ALU.not_equal, fill=1.0, base=0,
                                    pattern=[[-1, P]], channel_multiplier=1).then_inc(consts.sem, 1)
            nc.gpsimd.affine_select(out=causal[:], in_=causal[:], compare_op=ALU.is_ge, fill=0.0, base=0,
                                    pattern=[[0, 2], [1, P]], channel_multiplier=-1).then_inc(consts.sem, 1)
            pool.wait_ge(consts.sem, consts.value(0, 4))

            def inverse_rms(g, j, b):
                pool.wait_ge(q_var_done.sem, q_var_done.value(g, NB * nth(j) + b))
                nc.gpsimd.tensor_tensor(q_rinv[:, b, :], q_var[:, b, :], minus_half[:, 0:HALF],
                                        ALU.pow).then_inc(q_rinv_done.sem, 1)

            def lo(out, whole, hi):
                return nc.gpsimd.tensor_tensor(out, whole, f32(hi), ALU.subtract)

            def q_lo(g, j, b):
                pool.wait_ge(q_hi_done.sem, q_hi_done.value(g, NB * j + b))
                cols = slice(b * QB, (b + 1) * QB)
                lo(qT_lo[:, j % 2, cols], q_norm[:, b, :], qT_hi[:, j % 2, cols]).then_inc(q_split.sem, 1)

            def step(g, n, end):
                if n < end and STEP_MASKS[n % NSTEP]:
                    pool.wait_ge(exp_done.sem, exp_done.value(g, n))
                    for first, blocks, stride in STEP_MASKS[n % NSTEP]:
                        part = prob[:, n % 2, first:first + blocks * stride].rearrange(
                            "p (b c) -> p b c", b=blocks)[:, :, 0:P]
                        last = nc.gpsimd.tensor_tensor(part, part, causal[:, 0:blocks, :], ALU.mult)
                    last.then_inc(masked.sem, 1)
                for j, b in q_halves(n, (7, 5), end):
                    inverse_rms(g, j, b)
                if n == WO_STEP + 1:
                    pool.wait_ge(wo_hi_done.sem, wo_hi_done.value(g, 0))
                    lo(wo_lo[:], wo_raw[:], wo_hi[:]).then_inc(wo_split.sem, 1)
                for j, b in q_halves(n, (3, 2), end):
                    q_lo(g, j, b)
                for p in pairs(n, 7, end):
                    h, b = divmod(p, NB)
                    cols = slice(b * QB, (b + 1) * QB)
                    pool.wait_ge(o_hi_done.sem, o_hi_done.value(g, p))
                    lo(oT_lo[:, h % G, cols], o_norm[:, b, :], oT_hi[:, h % G, cols]).then_inc(o_split.sem, 1)

            for j in FRONT:
                for b in range(NB):
                    inverse_rms(0, j, b)
            for n in range(LOOP_START):
                step(0, n, LOOP)
            with pool.Fori(0, KVH - 1) as g:
                for n in range(LOOP_START, LOOP_START + STEPS):
                    step(g, n, LOOP)
            for n in range(LOOP_START, LOOP_START + STEPS):
                step(KVH - 1, n, LAST)

        @block.scalar
        def _(act):
            for b in range(NB):
                cols = slice(b * QB, (b + 1) * QB)
                act.wait_ge(x_in[b].sem, x_in[b].value(0, 0))
                nc.scalar.activation(xT_hi[:, :, cols], resT[:, :, cols], ACT.Copy).then_inc(x_hi_done.sem, 1)
            act.wait_ge(wkv_in[1].sem, wkv_in[1].value(0, 0))
            nc.scalar.activation(wkv_hi[1], wkv_raw[1], ACT.Copy).then_inc(wkv_hi_done[1].sem, 1)
            act.wait_ge(gammas_in.sem, gammas_in.value(0, 0))

            def wq_hi_half(g, r):
                act.wait_ge(wq_in.sem, wq_in.value(g, r))
                if r > 0:
                    act.wait_ge(q_projected.sem, q_projected.value(g, G * r - 1))
                nc.scalar.activation(wq_hi[:], wq_raw[:], ACT.Copy).then_inc(wq_hi_done.sem, 1)

            def k_hi(g, r, b):
                cols = slice(b * QB, (b + 1) * QB)
                src = k_norm[:, r, cols] if isinstance(g, int) and g == 0 and r == 0 else k_norm[:, bass.ds(g + r, 1), cols]
                nc.scalar.activation(kT_hi[:, cols], src, ACT.Copy).then_inc(k_hi_done.sem, 1)

            def v_hi_half(g, r, b):
                tiles = slice(b * HALF, (b + 1) * HALF)
                src = v_all[:, r, tiles, :] if isinstance(g, int) and g == 0 and r == 0 else v_all[:, bass.ds(g + r, 1), tiles, :]
                nc.scalar.activation(v_hi[:, tiles, :], src, ACT.Copy).then_inc(v_hi_done.sem, 1)

            def leave_slot(g, j, plan):
                s, _ = plan["q", j]
                act.wait_ge(q_projected.sem, q_projected.value(g, nth(j)))
                before = nth(j) - 2 if j < 2 else j - 1
                if before >= -KVH:
                    act.wait_ge(q_turned.sem, q_turned.value(g, NB * before + NB - 1))
                nc.scalar.activation(square_of(j), slot[s], ACT.Square).then_inc(q_squared.sem, 1)
                if before >= -KVH:
                    act.wait_ge(q_normed.sem, q_normed.value(g, NB * before + NB - 1))
                gamma = gammas[:, 1:2] if j < 0 else gammas[:, 0:1]
                nc.scalar.activation(raw_of(j), slot[s], ACT.Copy, scale=gamma).then_inc(q_copied.sem, 1)

            def q_hi(g, j, b):
                act.wait_ge(q_normed.sem, q_normed.value(g, NB * nth(j) + b))
                nc.scalar.activation(qT_hi[:, j % 2, b * QB:(b + 1) * QB], q_norm[:, b, :],
                                     ACT.Copy).then_inc(q_hi_done.sem, 1)

            def step(g, n, end, plan):
                if n == NSTEP * 2 - 1 and end == LOOP:
                    wq_hi_half(g, 1)
                for j in q_heads(n, 7, end):
                    leave_slot(g, j, plan)
                if n < end:
                    s, w = n % 2, STEP_WIDTH[n % NSTEP]
                    act.wait_ge(scored.sem, scored.value(g, n))
                    nc.scalar.activation(capped[:, s, 0:w], slot[plan["scores", n][0]][:, 0:w], ACT.Tanh,
                                         scale=SCALE / CAP).then_inc(tanh_done.sem, 1)
                    if n == STEPS - 2 and end == LOOP:
                        k_hi(g, 1, 0)
                    act.wait_ge(tanh_done.sem, tanh_done.value(g, n))
                    if n >= 2:
                        act.wait_ge(added.sem, added.value(g, last_add(n - 2)))
                    nc.scalar.activation(prob[:, s, 0:w], capped[:, s, 0:w], ACT.Exp,
                                         scale=CAP).then_inc(exp_done.sem, 1)

                    if n % NSTEP in HI_ON_ACT:
                        act.wait_ge(exp_done.sem, exp_done.value(g, n))
                        if n >= 2:
                            act.wait_ge(weighted.sem, weighted.value(g, n - 2))
                        nc.scalar.activation(prob_hi[:, s, 0:w], prob[:, s, 0:w], ACT.Copy).then_inc(hi_act.sem, 1)
                if n == STEPS - 1 and end == LOOP:
                    k_hi(g, 1, 1)
                if n in (STEPS, STEPS + 1) and end == LOOP:
                    act.wait_ge(weighted.sem, weighted.value(g, n - 2))
                    v_hi_half(g, 1, n - STEPS)
                for p in pairs(n, 2, end):
                    act.wait_ge(weighted.sem, weighted.value(g, last_step(p)))
                    if p >= NB:
                        act.wait_ge(o_normed.sem, o_normed.value(g, p - NB))
                    else:
                        act.wait_ge(q_turned.sem, q_turned.value(g, NB * nth(FRONT[-1]) + NB - 1))
                    nc.scalar.activation(o_raw[:, p % NB, :], o_ps[p % NB], ACT.Copy).then_inc(o_copied.sem, 1)
                for j, b in q_halves(n, (4, 2), end):
                    q_hi(g, j, b)
                for p in pairs(n, 6, end):
                    h, b = divmod(p, NB)
                    act.wait_ge(o_normed.sem, o_normed.value(g, p))
                    if p >= PAIRS:
                        act.wait_ge(out_projected.sem, out_projected.value(g, DC * b + DC - 1))
                    nc.scalar.activation(oT_hi[:, h % G, b * QB:(b + 1) * QB], o_norm[:, b, :],
                                         ACT.Copy).then_inc(o_hi_done.sem, 1)
                if n == WO_STEP:
                    act.wait_ge(wo_in.sem, wo_in.value(g, 0))
                    nc.scalar.activation(wo_hi[:], wo_raw[:], ACT.Copy).then_inc(wo_hi_done.sem, 1)

            wq_hi_half(0, 0)
            for i, j in enumerate(FRONT):
                leave_slot(0, j, PLAN_FIRST)
                if i < KVH:
                    act.wait_ge(v_projected.sem, v_projected.value(0, i))
                    nc.scalar.activation(
                        v_all[:, :, 2 * i:2 * i + 2, :].rearrange("p g t c -> p t g c"),
                        slot[PLAN_FIRST["v", i][0]].rearrange("p (t g c) -> p t g c", t=2, g=KVH),
                        ACT.Copy).then_inc(v_copied.sem, 1)
                if i >= 1 and FRONT[i - 1] >= 0:
                    for b in range(NB):
                        q_hi(0, FRONT[i - 1], b)
                if i == KVH - 1:
                    act.wait_ge(q_normed.sem, q_normed.value(0, NB * nth(-KVH) + NB - 1))
                    act.wait_ge(v_copied.sem, v_copied.value(0, KVH - 1))
                    for b in range(NB):
                        k_hi(0, 0, b)
                        v_hi_half(0, 0, b)
            for n in range(LOOP_START):
                step(0, n, LOOP, PLAN_FIRST)
            with act.Fori(0, KVH - 1) as g:
                for n in range(LOOP_START, LOOP_START + STEPS):
                    step(g, n, LOOP, PLAN_LOOP)
            for n in range(LOOP_START, LOOP_START + STEPS):
                step(KVH - 1, n, LAST, PLAN_LAST)

        @block.vector
        def _(dve):
            dve.sem_inc(wo_split.sem, 1)

            def lo(out, whole, hi):
                return nc.vector.tensor_tensor(out, whole, f32(hi), ALU.subtract)

            dve.wait_ge(wkv_in[0].sem, wkv_in[0].value(0, 0))
            nc.vector.tensor_copy(wkv_hi[0], wkv_raw[0]).then_inc(wkv_hi_done[0].sem, 1)
            dve.wait_ge(wkv_hi_done[0].sem, wkv_hi_done[0].value(0, 0))
            lo(wkv_lo[0], wkv_raw[0], wkv_hi[0]).then_inc(wkv_split[0].sem, 1)
            for b in range(NB):
                cols = slice(b * QB, (b + 1) * QB)
                dve.wait_ge(x_hi_done.sem, x_hi_done.value(0, b))
                lo(xT_lo[:, :, cols], resT[:, :, cols], xT_hi[:, :, cols]).then_inc(x_lo_done.sem, 1)
            dve.wait_ge(wkv_hi_done[1].sem, wkv_hi_done[1].value(0, 0))
            lo(wkv_lo[1], wkv_raw[1], wkv_hi[1]).then_inc(wkv_split[1].sem, 1)

            def wq_lo_half(g, r):
                dve.wait_ge(wq_hi_done.sem, wq_hi_done.value(g, r))
                lo(wq_lo[:], wq_raw[:], wq_hi[:]).then_inc(wq_split.sem, 1)

            def k_lo(g, r, b):
                cols = slice(b * QB, (b + 1) * QB)
                src = k_norm[:, r, cols] if isinstance(g, int) and g == 0 and r == 0 else k_norm[:, bass.ds(g + r, 1), cols]
                dve.wait_ge(k_hi_done.sem, k_hi_done.value(g, NB * r + b))
                lo(kT_lo[:, cols], src, kT_hi[:, cols]).then_inc(k_split.sem, 1)

            def v_lo_half(g, r, b):
                tiles = slice(b * HALF, (b + 1) * HALF)
                src = v_all[:, r, tiles, :] if isinstance(g, int) and g == 0 and r == 0 else v_all[:, bass.ds(g + r, 1), tiles, :]
                dve.wait_ge(v_hi_done.sem, v_hi_done.value(g, NB * r + b))
                lo(v_lo[:, tiles, :], src, v_hi[:, tiles, :]).then_inc(v_split.sem, 1)

            def mean_square(g, j, b):
                dve.wait_ge(q_turned.sem, q_turned.value(g, NB * nth(j) + b))
                if j > -KVH:
                    dve.wait_ge(q_rinv_done.sem, q_rinv_done.value(g, NB * (nth(j) - 1) + b))
                nc.vector.tensor_reduce(q_sum[:, b, :], norm_ps(j, b).rearrange("p (i c) -> p i c", i=HALF), AX.X,
                                        ALU.add).then_inc(q_summed.sem, 1)
                dve.wait_ge(q_summed.sem, q_summed.value(g, NB * nth(j) + b))
                nc.vector.tensor_scalar(q_var[:, b, :], q_sum[:, b, :], 1.0 / HD, RMS_EPS, ALU.mult,
                                        ALU.add).then_inc(q_var_done.sem, 1)

            def normalise_q(g, j, b):
                dve.wait_ge(q_spread.sem, q_spread.value(g, NB * nth(j) + b))
                dve.wait_ge(q_copied.sem, q_copied.value(g, nth(j)))
                if j > 0:
                    dve.wait_ge(q_split.sem, q_split.value(g, NB * (j - 1) + b))
                nc.vector.tensor_tensor(q_dst(j, b), raw_of(j)[:, b * QB:(b + 1) * QB], norm_ps(j, b),
                                        ALU.mult).then_inc(q_normed.sem, 1)

            def step(g, n, end, plan):
                if n == NSTEP * 2 - 1 and end == LOOP:
                    wq_lo_half(g, 1)
                if end == LAST:
                    units = [DC * b + d for b, heads in LAST_OUT.get(n - 1, ()) if G - 1 in heads for d in range(DC)]
                else:
                    units = [n - OUT_STEP - 1] if OUT_STEP < n <= OUT_STEP + len(OUT_UNITS) else []
                for u in units:
                    b, d = OUT_UNITS[u]
                    cols = slice(b * QB, (b + 1) * QB)
                    dve.wait_ge(out_projected.sem, out_projected.value(g, u))
                    nc.vector.tensor_tensor(resT[:, d, cols], resT[:, d, cols], out_at(u, end, plan),
                                            ALU.add).then_inc(res_added.sem, 1)
                for p in pairs(n, 5, end):
                    b = p % NB
                    dve.wait_ge(spread.sem, spread.value(g, p))
                    dve.wait_ge(o_copied.sem, o_copied.value(g, p))
                    if p >= NB:
                        dve.wait_ge(o_split.sem, o_split.value(g, p - NB))
                    nc.vector.tensor_tensor(o_norm[:, b, :], o_raw[:, b, :], x_ps[b], ALU.mult).then_inc(o_normed.sem, 1)
                for j, b in q_halves(n, (7, 5), end):
                    mean_square(g, j, b)
                for j, b in q_halves(n, (6, 4), end):
                    normalise_q(g, j, b)
                if n == STEPS - 2 and end == LOOP:
                    k_lo(g, 1, 0)
                h, i = divmod(n, NSTEP)
                s, w = n % 2, STEP_WIDTH[i]
                if n < end:
                    if STEP_MASKS[i]:
                        dve.wait_ge(masked.sem, masked.value(g, mask_event(n)))
                    if n >= 2:
                        dve.wait_ge(weighted.sem, weighted.value(g, n - 2))
                    if i not in HI_ON_ACT:
                        nc.vector.tensor_copy(prob_hi[:, s, 0:w], prob[:, s, 0:w]).then_inc(hi_dve.sem, 1)
                    hi_done, event = hi_event(n)
                    dve.wait_ge(hi_done.sem, hi_done.value(g, event))
                    lo(prob_lo[:, s, 0:w], prob[:, s, 0:w], prob_hi[:, s, 0:w]).then_inc(prob_split.sem, 1)
                if n in (STEPS, STEPS + 1) and end == LOOP:
                    v_lo_half(g, 1, n - STEPS)
                if n == STEPS - 1 and end == LOOP:
                    k_lo(g, 1, 1)
                if n < end:
                    for k, (head, at, (b, (c0, c1), first, second)) in enumerate(ADDS):
                        if NSTEP * head + at != n:
                            continue
                        to = prob_sum[:, h % 2, b, c0:c1]
                        one = prob[:, s, first:first + c1 - c0]
                        if second is None:
                            dve.wait_ge(added.sem, added.value(g, k - 1))
                            add = nc.vector.tensor_tensor(to, to, one, ALU.add)
                        else:
                            if h >= 2:
                                dve.wait_ge(sums_turned.sem, sums_turned.value(g, NB * (h - 2) + b))
                            if second == "copy":
                                add = nc.vector.tensor_copy(to, one)
                            else:
                                add = nc.vector.tensor_tensor(to, one, prob[:, s, second:second + c1 - c0], ALU.add)
                        add.then_inc(added.sem, 1)
                for p in pairs(n, 3, end):
                    dve.wait_ge(sums_turned.sem, sums_turned.value(g, p))
                    nc.vector.tensor_reduce(key_sum[:, p % NB, :], x_ps[p % NB].rearrange("p (i c) -> p i c", i=HALF),
                                            AX.X, ALU.add).then_inc(sums_done.sem, 1)
                    dve.wait_ge(sums_done.sem, sums_done.value(g, p))
                    nc.vector.reciprocal(inv_sum[:, p % NB, :], key_sum[:, p % NB, :]).then_inc(inv_done.sem, 1)




            def q_lo(g, j, b):
                dve.wait_ge(q_hi_done.sem, q_hi_done.value(g, NB * j + b))
                cols = slice(b * QB, (b + 1) * QB)
                lo(qT_lo[:, j % 2, cols], q_norm[:, b, :], qT_hi[:, j % 2, cols]).then_inc(q_split.sem, 1)

            wq_lo_half(0, 0)
            for i, j in enumerate(FRONT):
                for b in range(NB):
                    mean_square(0, j, b)
                if i >= 1 and FRONT[i - 1] >= 0:
                    for b in range(NB):
                        q_lo(0, FRONT[i - 1], b)
                for b in range(NB):
                    normalise_q(0, j, b)
                if i == KVH - 1:
                    for b in range(NB):
                        k_lo(0, 0, b)
                        v_lo_half(0, 0, b)
            for n in range(LOOP_START):
                step(0, n, LOOP, PLAN_FIRST)
            with dve.Fori(0, KVH - 1) as g:
                for n in range(LOOP_START, LOOP_START + STEPS):
                    step(g, n, LOOP, PLAN_LOOP)
            for n in range(LOOP_START, LOOP_START + STEPS):
                step(KVH - 1, n, LAST, PLAN_LAST)

        @block.tensor
        def _(pe):
            pe.wait_ge(consts.sem, consts.value(0, 4))


            def accumulate(out, passes, first=True, final=True):
                for j, (stationary, moving) in enumerate(passes):
                    mm = nc.tensor.matmul(out, stationary, moving, start=first and j == 0,
                                          stop=final and j == len(passes) - 1, skip_group_check=True)
                return mm

            def take_slot(g, use, plan):
                s, before = plan[use]
                if before is not None:
                    kind, i = before
                    if kind == "scores":
                        pe.wait_ge(tanh_done.sem, tanh_done.value(g, i))
                    elif kind == "q":
                        pe.wait_ge(q_copied.sem, q_copied.value(g, nth(i)))
                    elif kind == "v":
                        pe.wait_ge(v_copied.sem, v_copied.value(g, i))
                    else:
                        pe.wait_ge(res_added.sem, res_added.value(g, i))
                return slot[s]

            def project_q(g, j, plan):
                out = take_slot(g, ("q", j), plan)
                if j < 0:
                    w_hi, w_lo, head = wkv_hi[0], wkv_lo[0], slice((j + KVH) * HD, (j + KVH + 1) * HD)
                    pe.wait_ge(wkv_split[0].sem, wkv_split[0].value(0, 0))
                else:
                    w_hi, w_lo, head = wq_hi, wq_lo, slice(j % G * HD, (j % G + 1) * HD)
                    pe.wait_ge(wq_split.sem, wq_split.value(g, j // G))
                for b in range(NB):
                    cols = slice(b * QB, (b + 1) * QB)
                    if j == -KVH:
                        pe.wait_ge(x_lo_done.sem, x_lo_done.value(0, b))
                    mm = accumulate(out[:, cols], [x for c in range(DC) for x in split3(
                        w_hi[:, c, head], w_lo[:, c, head], xT_hi[:, c, cols], xT_lo[:, c, cols])])
                mm.then_inc(q_projected.sem, 1)

            def project_v(i):
                out = take_slot(0, ("v", i), PLAN_FIRST)
                pe.wait_ge(wkv_split[1].sem, wkv_split[1].value(0, 0))
                for t in range(2):
                    tok = slice((2 * i + t) * P, (2 * i + t + 1) * P)
                    mm = accumulate(out[:, t * 512:(t + 1) * 512], [x for c in range(DC) for x in split3(
                        xT_hi[:, c, tok], xT_lo[:, c, tok], wkv_hi[1][:, c, :], wkv_lo[1][:, c, :])])
                mm.then_inc(v_projected.sem, 1)

            def sum_squares(g, j, b):
                pe.wait_ge(q_squared.sem, q_squared.value(g, nth(j)))
                if j >= 3:
                    pe.wait_ge(o_normed.sem, o_normed.value(g, NB * (j - 3) + b))
                elif nth(j) >= 2 - KVH:
                    pe.wait_ge(q_normed.sem, q_normed.value(g, NB * (nth(j) - 2) + b))
                turn(norm_ps(j, b), square_of(j)[:, b * QB:(b + 1) * QB]).then_inc(q_turned.sem, 1)

            def turn(out, rows):
                for i in range(HALF):
                    mm = nc.tensor.transpose(out[:, i * P:(i + 1) * P], rows[:, i * P:(i + 1) * P], ident[:])
                return mm

            def spread_columns(out, columns):
                for i in range(HALF):
                    mm = nc.tensor.transpose(out[:, i * P:(i + 1) * P], columns[:, i:i + 1].broadcast_to([P, P]), ident[:])
                return mm

            def spread_rms(g, j, b):
                pe.wait_ge(q_rinv_done.sem, q_rinv_done.value(g, NB * nth(j) + b))
                spread_columns(norm_ps(j, b), q_rinv[:, b, :]).then_inc(q_spread.sem, 1)

            def score(g, n, plan):
                h, i = divmod(n, NSTEP)
                out = take_slot(g, ("scores", n), plan)
                pe.wait_ge(q_split.sem, q_split.value(g, NB * h + (i >= 1)))
                if h % G == 0 and i in (0, 2):
                    pe.wait_ge(k_split.sem, k_split.value(g, NB * (h // G) + (i == 2)))
                for b, kt, col, w in HEAD_STEPS[i]:
                    keys = slice(kt * P, (kt + 1) * P)
                    queries = slice((b + 1) * QB - w, (b + 1) * QB)
                    mm = accumulate(out[:, col:col + w], split3(
                        kT_hi[:, keys], kT_lo[:, keys], qT_hi[:, h % 2, queries], qT_lo[:, h % 2, queries]))
                mm.then_inc(scored.sem, 1)

            def weigh(g, n):
                h, i = divmod(n, NSTEP)
                s = n % 2
                pe.wait_ge(prob_split.sem, prob_split.value(g, n))
                if h % G == 0 and i in (0, 2):
                    pe.wait_ge(v_split.sem, v_split.value(g, NB * (h // G) + (i == 2)))
                for b, kt, col, w in HEAD_STEPS[i]:
                    p = NB * h + b
                    if kt == 0:
                        if p >= NB:
                            pe.wait_ge(o_copied.sem, o_copied.value(g, p - NB))
                        else:
                            pe.wait_ge(q_normed.sem, q_normed.value(g, NB + b))
                    mm = accumulate(o_ps[b][:, QB - w:QB], split3(
                        v_hi[:, kt, :], v_lo[:, kt, :], prob_hi[:, s, col:col + w], prob_lo[:, s, col:col + w]),
                        first=kt == 0, final=n == last_step(p))
                mm.then_inc(weighted.sem, 1)

            def sum_keys(g, p, end):
                h, b = divmod(p, NB)
                pe.wait_ge(added.sem, added.value(g, last_add(last_step(p))))
                if h + 2 < end // NSTEP:
                    pe.wait_ge(q_normed.sem, q_normed.value(g, NB * (h + 2) + b))
                elif p >= NB:
                    pe.wait_ge(o_normed.sem, o_normed.value(g, p - NB))
                turn(x_ps[b], prob_sum[:, h % 2, b, :]).then_inc(sums_turned.sem, 1)

            def project_out(g, u, plan):
                b, d = OUT_UNITS[u]
                out = take_slot(g, ("out", u), plan)
                pe.wait_ge(wo_split.sem, wo_split.value(g, 0))
                pe.wait_ge(o_split.sem, o_split.value(g, NB * (G - 1) + b))
                cols, feats = slice(b * QB, (b + 1) * QB), slice(d * P, (d + 1) * P)
                accumulate(out[:, 0:QB], [x for h in range(G) for x in split3(
                    wo_hi[:, h, feats], wo_lo[:, h, feats], oT_hi[:, h, cols], oT_lo[:, h, cols])]
                ).then_inc(out_projected.sem, 1)

            def project_out_heads(g, b, heads, plan):
                cols = slice(b * QB, (b + 1) * QB)
                if 0 in heads:
                    pe.wait_ge(tanh_done.sem, tanh_done.value(g, STEPS - 2 + b))
                pe.wait_ge(wo_split.sem, wo_split.value(g, 0))
                pe.wait_ge(o_split.sem, o_split.value(g, NB * heads[-1] + b))
                for d in range(DC):
                    feats = slice(d * P, (d + 1) * P)
                    mm = accumulate(out_at(DC * b + d, LAST, plan), [x for h in heads for x in split3(
                        wo_hi[:, h, feats], wo_lo[:, h, feats], oT_hi[:, h, cols], oT_lo[:, h, cols])],
                        first=0 in heads, final=G - 1 in heads)
                    if G - 1 in heads:
                        mm.then_inc(out_projected.sem, 1)

            def step(g, n, end, plan):
                for kind, i in step_uses(n, end):
                    if kind == "out":
                        project_out(g, i, plan)
                    elif kind == "scores":
                        score(g, i, plan)
                    else:
                        project_q(g, i, plan)
                if end == LAST:
                    for b, heads in LAST_OUT.get(n, ()):
                        project_out_heads(g, b, heads, plan)
                for j, b in q_halves(n, (7, 5), end):
                    spread_rms(g, j, b)
                for p in pairs(n, 2, end):
                    sum_keys(g, p, end)
                if n < end:
                    weigh(g, n)
                for j, b in q_halves(n, (9, 7), end):
                    sum_squares(g, j, b)
                for p in pairs(n, 3, end):
                    pe.wait_ge(inv_done.sem, inv_done.value(g, p))
                    spread_columns(x_ps[p % NB], inv_sum[:, p % NB, :]).then_inc(spread.sem, 1)

            for i in range(len(FRONT) + 1):
                if i < len(FRONT):
                    project_q(0, FRONT[i], PLAN_FIRST)
                else:
                    score(0, 0, PLAN_FIRST)
                if i > KVH:
                    for b in range(NB):
                        spread_rms(0, FRONT[i - 2], b)
                if i >= 1:
                    for b in range(NB):
                        sum_squares(0, FRONT[i - 1], b)
                if i < KVH:
                    project_v(i)
                if 1 <= i < KVH:
                    for b in range(NB):
                        spread_rms(0, FRONT[i - 1], b)
            score(0, 1, PLAN_FIRST)
            for b in range(NB):
                spread_rms(0, FRONT[-1], b)
            for n in range(LOOP_START):
                step(0, n, LOOP, PLAN_FIRST)
            with pe.Fori(0, KVH - 1) as g:
                for n in range(LOOP_START, LOOP_START + STEPS):
                    step(g, n, LOOP, PLAN_LOOP)
            for n in range(LOOP_START, LOOP_START + STEPS):
                step(KVH - 1, n, LAST, PLAN_LAST)


def experts(nc, kept, dram):
    resT, ident, minus_half = kept["resT"], kept["ident"], kept["minus_half"]
    NSTEPS = NSHARED + 1 + NROUTED
    GATES = NSHARED
    FIRST, LAST = GATES + 3, NSTEPS - 2
    ROUNDS = (LAST - FIRST) // 2
    assert FIRST % 2 == 0 and (LAST - FIRST) % 2 == 0

    def w1_tile(step):
        assert step != GATES
        return step - 1 if step > GATES else step

    def w1_load(step):
        return sum(1 for x in range(step % 2, step, 2) if x != GATES)

    with ExitStack() as ctx:
        def sb(name, shape, dt=F32):
            return ctx.enter_context(nc.sbuf_tensor(name, shape, dt))

        def signal(name, per_round=1, credit=0, unit=1):
            return Signal(ctx.enter_context(nc.semaphore(name)), per_round, credit, unit)

        w1_raw, w2_raw = sb("w1_raw", [P, 2, DC, P]), sb("w2_raw", [P, 2, D])
        w1_hi, w1_lo = sb("w1_hi", [P, 2, DC, P], F32R), sb("w1_lo", [P, 2, DC, P], F32R)
        w2_hi, w2_lo = sb("w2_hi", [P, 2, D], F32R), sb("w2_lo", [P, 2, D], F32R)
        b1 = sb("b1", [P, NSHARED + NROUTED])
        shared_b2 = sb("shared_b2", [P, NS, DC])
        shared_b2_sum = sb("shared_b2_sum", [P, DC])
        shared_b2_mean = sb("shared_b2_mean", [P, DC])
        router = sb("router", [P, DC, NE])
        router_b = sb("router_b", [P, NE])
        stats = sb("stats", [P, 2, NT, 6])
        mean_var = sb("mean_var", [P, 2, NT, 2])
        var_eps = sb("ln_var_eps", [P, 2, NT])
        rstd = sb("rstd", [P, 2, NT])
        minus_mean, norm_shift = sb("minus_mean", [P, 2, HALF]), sb("norm_shift", [P, 2, HALF])
        x1 = sb("x1", [P, NT, D])
        x1T = sb("x1T", [P, DC, T])
        x1T_hi, x1T_lo = sb("x1T_hi", [P, DC, T], F32R), sb("x1T_lo", [P, DC, T], F32R)
        logits = sb("logits", [P, NT, NE])
        top8 = sb("top8", [P, NT, 8])
        top_id = sb("top_id", [P, NT, 8], U32)
        top_id_f = sb("top_id_f", [P, NT, 8])
        expert_id = sb("expert_id", [P, NE])
        chosen_by = sb("chosen_by", [P, NT, NE, TOPK])
        chosen = sb("chosen", [P, NT, NE])
        below_max = sb("below_max", [P, NT, NE])
        weight = sb("weight", [P, NT, NE])
        kept_weight = sb("kept_weight", [P, NT, NE])
        weight_sum = sb("weight_sum", [P, NT])
        weight_inv = sb("weight_inv", [P, NT])
        gates = sb("gates", [P, NT, NE])
        gates_spread = sb("gates_spread", [P, NT, NE, EROWS])
        gatesT = sb("gatesT", [P, T])
        hidden = sb("hidden", [P, 2, T])
        gated = sb("gated", [P, 2, T])
        h_hi, h_lo = sb("h_hi", [P, 2, T], F32R), sb("h_lo", [P, 2, T], F32R)
        outT = sb("outT", [P, DC, T])
        result = sb("result", [P, NT, D])

        psum = ctx.enter_context(nc.psum_tensor("psum_moe", [P, 8, 512], F32))
        yT = [[psum[:, NB * d + b, :] for b in range(NB)] for d in range(DC)]
        slot = [psum[:, 4 + 2 * s:6 + 2 * s, :].rearrange("p b c -> p (b c)") for s in range(2)]
        norm_in = [psum[:, 4 * k:4 * k + 4, :].rearrange("p b (i c) -> p (b i) c", c=D) for k in range(2)]
        logits_ps = psum[:, 0, 0:NT * NE].rearrange("p (i e) -> p i e", i=NT)

        small_in = signal("moe_small_in", unit=16)
        w1_in = [signal(f"w1_in{s}", unit=16) for s in range(2)]
        w2_in = [signal(f"w2_in{s}", unit=16) for s in range(2)]
        expert_id_done = signal("expert_id_done")
        norm_turned = signal("norm_turned", NT)
        norm_stats = signal("norm_stats", NT)
        norm_mean = signal("norm_mean", NT)
        norm_var = signal("norm_var", NB)
        norm_rstd = signal("norm_rstd", NB)
        norm_shift_done = signal("norm_shift_done")
        normed = [signal(f"moe_normed{b}", HALF) for b in range(NB)]
        x1_turned = signal("x1_turned", NB * DC)
        x1_hi_done = signal("x1_hi_done", NB * DC)
        x1_copied = signal("x1_copied", NB * DC)
        x1_split = signal("x1_split", NB * DC)
        bias_done = signal("bias_done")
        logits_done = signal("logits_done")
        routed = signal("routed")
        below_max_done = signal("below_max_done")
        weight_done = signal("weight_done")
        gates_done = signal("gates_done")
        w1_hi_done, w1_split = signal("w1_hi_done", 2), signal("w1_split", 2)
        w2_hi_done, w2_split = signal("w2_hi_done", 2), signal("w2_split", 2)
        upped = signal("upped", 2)
        relu_done = signal("relu_done", 2)
        gate_done = signal("gate_done", 2)
        h_hi_done = signal("h_hi_done", 2)
        h_split = signal("h_split", 2)
        downed = signal("downed", 2)
        res_done = signal("moe_res_done", NB * DC)
        stored = signal("stored", unit=16)

        block = ctx.enter_context(nc.Block())


        @block.sync
        def _(sp):
            def load(g, step):
                s = step % 2
                if step != GATES:
                    if step >= 2:
                        before = step - 2 if step - 2 != GATES else step - 4
                        sp.wait_ge(w1_split.sem, w1_split.value(g, w1_tile(before)))
                    sp.dma_start(w1_raw[:, s], dram["w1"][2 * g + w1_tile(step)]).then_inc(w1_in[s].sem, 16)
                if step >= 2:
                    sp.wait_ge(w2_split.sem, w2_split.value(g, step - 2))
                sp.dma_start(w2_raw[:, s], dram["w2"][2 * g + step]).then_inc(w2_in[s].sem, 16)

            load(0, 0)
            load(0, 1)
            for to, of in ((router, "router"), (router_b, "router_b"), (b1, "b1"), (shared_b2, "shared_b2")):
                sp.dma_start(to[:], dram[of]).then_inc(small_in.sem, 16)
            for step in range(2, FIRST):
                load(0, step)
            with sp.Fori(0, ROUNDS) as g:
                load(g, FIRST)
                load(g, FIRST + 1)
            for step in range(LAST, NSTEPS):
                load(0, step)
            out = dram["out"].rearrange("(i p) d -> p i d", p=P)
            for b in range(NB):
                tiles = slice(b * HALF, (b + 1) * HALF)
                sp.wait_ge(normed[b].sem, normed[b].value(1, HALF - 1))
                sp.dma_start(out[:, tiles, :], result[:, tiles, :]).then_inc(stored.sem, 16)
            sp.wait_ge(stored.sem, stored.value(0, NB - 1))

        @block.gpsimd
        def _(pool):
            nc.gpsimd.iota(expert_id[:], pattern=[[1, NE]], base=0, channel_multiplier=0,
                           allow_small_or_imprecise_dtypes=True).then_inc(expert_id_done.sem, 1)
            for k in range(2):
                for b in range(NB):
                    tiles = slice(b * HALF, (b + 1) * HALF)
                    pool.wait_ge(norm_var.sem, norm_var.value(k, b))
                    nc.gpsimd.tensor_tensor(rstd[:, k, tiles], var_eps[:, k, tiles], minus_half[:, tiles],
                                            ALU.pow).then_inc(norm_rstd.sem, 1)
                    if b == 0:
                        pool.wait_ge(norm_rstd.sem, norm_rstd.value(k, b))
                        nc.gpsimd.tensor_tensor(norm_shift[:, k, :], minus_mean[:, k, :], rstd[:, k, tiles],
                                                ALU.mult).then_inc(norm_shift_done.sem, 1)

        @block.scalar
        def _(act):
            def normalise(k, to):
                act.wait_ge(norm_shift_done.sem, norm_shift_done.value(k, 0))
                for i in range(HALF):
                    nc.scalar.activation(to[:, i, :], norm_in[k][:, i, :], ACT.Identity, bias=norm_shift[:, k, i:i + 1],
                                         scale=rstd[:, k, i:i + 1]).then_inc(normed[0].sem, 1)

            normalise(0, x1)
            for u in range(NB * DC):
                b, d = divmod(u, DC)
                cols = slice(b * QB, (b + 1) * QB)
                turned = slot[b][:, d * QB:(d + 1) * QB]
                act.wait_ge(x1_turned.sem, x1_turned.value(0, u))
                nc.scalar.activation(x1T_hi[:, d, cols], turned, ACT.Copy).then_inc(x1_hi_done.sem, 1)
                nc.scalar.activation(x1T[:, d, cols], turned, ACT.Copy).then_inc(x1_copied.sem, 1)
            act.wait_ge(small_in.sem, small_in.value(0, 3))

            def relu(g, step):
                s = step % 2
                act.wait_ge(upped.sem, upped.value(g, step))
                if step >= 2:
                    act.wait_ge(gate_done.sem, gate_done.value(g, step - 2))
                if step == GATES:
                    nc.scalar.activation(gatesT[:], slot[s], ACT.Copy).then_inc(relu_done.sem, 1)
                else:
                    t = w1_tile(step) if step < FIRST or step >= LAST + 1 else bass.ds(2 * g + w1_tile(step), 1)
                    bias = b1[:, t:t + 1] if isinstance(t, int) else b1[:, t]
                    nc.scalar.activation(hidden[:, s, :], slot[s], ACT.Relu, bias=bias).then_inc(relu_done.sem, 1)

            def hi(g, step):
                s = step % 2
                act.wait_ge(gate_done.sem, gate_done.value(g, step))
                if step >= 2:
                    act.wait_ge(downed.sem, downed.value(g, step - 2))
                nc.scalar.activation(h_hi[:, s, :], gated[:, s, :], ACT.Copy).then_inc(h_hi_done.sem, 1)

            relu(0, 0)
            hi(0, 0)
            relu(0, 1)
            act.wait_ge(below_max_done.sem, below_max_done.value(0, 0))
            nc.scalar.activation(weight[:], below_max[:], ACT.Exp).then_inc(weight_done.sem, 1)
            for step in range(1, FIRST - 1):
                relu(0, step + 1)
                hi(0, step)
            with act.Fori(0, ROUNDS) as g:
                for step in (FIRST, FIRST + 1):
                    relu(g, step)
                    hi(g, step - 1)
            for step in range(LAST, NSTEPS):
                relu(0, step)
                hi(0, step - 1)
            hi(0, NSTEPS - 1)
            normalise(1, result)

        @block.vector
        def _(dve):
            def statistics(k, b):
                tiles = slice(b * HALF, (b + 1) * HALF)
                for i in range(b * HALF, (b + 1) * HALF):
                    dve.wait_ge(norm_turned.sem, norm_turned.value(k, i | 1))
                    nc.vector.bn_stats(stats[:, k, i, :], norm_in[k][:, i, :]).then_inc(norm_stats.sem, 1)
                for i in range(b * HALF, (b + 1) * HALF):
                    dve.wait_ge(norm_stats.sem, norm_stats.value(k, i))
                    nc.vector.bn_aggr(mean_var[:, k, i, :], stats[:, k, i, :]).then_inc(norm_mean.sem, 1)
                dve.wait_ge(norm_mean.sem, norm_mean.value(k, (b + 1) * HALF - 1))
                if b == 0:
                    nc.vector.tensor_scalar(minus_mean[:, k, :], mean_var[:, k, tiles, 0], -1.0, None, ALU.mult)
                nc.vector.tensor_scalar(var_eps[:, k, tiles], mean_var[:, k, tiles, 1], LN_EPS, None,
                                        ALU.add).then_inc(norm_var.sem, 1)

            def normalise(k, to):
                dve.wait_ge(norm_rstd.sem, norm_rstd.value(k, 1))
                for i in range(HALF, NT):
                    nc.vector.tensor_scalar(to[:, i, :], norm_in[k][:, i, :], mean_var[:, k, i, 0:1],
                                            rstd[:, k, i:i + 1], ALU.subtract, ALU.mult).then_inc(normed[1].sem, 1)

            def split_w1(g, step):
                s = step % 2
                t = w1_tile(step)
                dve.wait_ge(w1_in[s].sem, w1_in[s].value(g, w1_load(step)))
                if step >= 2:
                    dve.wait_ge(upped.sem, upped.value(g, step - 2))
                nc.vector.tensor_copy(w1_hi[:, s], w1_raw[:, s]).then_inc(w1_hi_done.sem, 1)
                dve.wait_ge(w1_hi_done.sem, w1_hi_done.value(g, t))
                nc.vector.tensor_tensor(w1_lo[:, s], w1_raw[:, s], f32(w1_hi[:, s]), ALU.subtract).then_inc(w1_split.sem, 1)

            def split_w2(g, step):
                s = step % 2
                dve.wait_ge(w2_in[s].sem, w2_in[s].value(g, step // 2))
                if step >= 2:
                    dve.wait_ge(downed.sem, downed.value(g, step - 2))
                nc.vector.tensor_copy(w2_hi[:, s], w2_raw[:, s]).then_inc(w2_hi_done.sem, 1)
                dve.wait_ge(w2_hi_done.sem, w2_hi_done.value(g, step))
                nc.vector.tensor_tensor(w2_lo[:, s], w2_raw[:, s], f32(w2_hi[:, s]), ALU.subtract).then_inc(w2_split.sem, 1)

            def gate_hidden(g, step):
                s = step % 2
                split_w2(g, step)
                dve.wait_ge(relu_done.sem, relu_done.value(g, step))
                if step < GATES:
                    gate = nc.vector.tensor_scalar(gated[:, s, :], hidden[:, s, :], 1.0 / NS, None, ALU.mult)
                elif step == GATES:
                    gate = nc.vector.tensor_scalar(gated[:, s, :], gatesT[:], 1.0 / EROWS, None, ALU.mult)
                else:
                    gate = nc.vector.tensor_tensor(gated[:, s, :], hidden[:, s, :], gatesT[:], ALU.mult)
                gate.then_inc(gate_done.sem, 1)

            def hidden_lo(g, step):
                s = step % 2
                dve.wait_ge(h_hi_done.sem, h_hi_done.value(g, step))
                nc.vector.tensor_tensor(h_lo[:, s, :], gated[:, s, :], f32(h_hi[:, s, :]), ALU.subtract).then_inc(h_split.sem, 1)

            def hidden_step(g, step):
                gate_hidden(g, step)
                if step + 2 < NSTEPS and step + 2 != GATES:
                    split_w1(g, step + 2)
                hidden_lo(g, step)

            for b in range(NB):
                statistics(0, b)
            split_w1(0, 0)
            split_w1(0, 1)
            normalise(0, x1)
            for u in range(NB * DC):
                b, d = divmod(u, DC)
                cols = slice(b * QB, (b + 1) * QB)
                dve.wait_ge(x1_copied.sem, x1_copied.value(0, u))
                nc.vector.tensor_tensor(x1T_lo[:, d, cols], slot[b][:, d * QB:(d + 1) * QB], f32(x1T_hi[:, d, cols]),
                                        ALU.subtract).then_inc(x1_split.sem, 1)
            dve.wait_ge(small_in.sem, small_in.value(0, 3))
            nc.vector.tensor_tensor(shared_b2_sum[:], shared_b2[:, 0, :], shared_b2[:, 1, :], ALU.add).then_inc(bias_done.sem, 1)
            dve.wait_ge(bias_done.sem, bias_done.value(0, 0))
            nc.vector.tensor_scalar(shared_b2_mean[:], shared_b2_sum[:], 1.0 / NS, None, ALU.mult).then_inc(bias_done.sem, 1)

            split_w1(0, 2)
            gate_hidden(0, 0)

            dve.wait_ge(logits_done.sem, logits_done.value(0, 0))
            nc.vector.tensor_tensor(logits[:], logits_ps, router_b[:].unsqueeze(1).broadcast_to([P, NT, NE]),
                                    ALU.add).then_inc(routed.sem, 1)
            dve.wait_ge(routed.sem, routed.value(0, 0))
            for i in range(NT):
                last = nc.vector.max(top8[:, i, :], logits[:, i, :])
            last.then_inc(routed.sem, 1)
            dve.wait_ge(routed.sem, routed.value(0, 1))
            nc.vector.tensor_tensor(below_max[:], logits[:], top8[:, :, 0:1].broadcast_to([P, NT, NE]),
                                    ALU.subtract).then_inc(below_max_done.sem, 1)
            for i in range(NT):
                last = nc.vector.max_index(top_id[:, i, :], top8[:, i, :], logits[:, i, :])
            last.then_inc(routed.sem, 1)
            dve.wait_ge(routed.sem, routed.value(0, 2))
            nc.vector.tensor_copy(top_id_f[:], top_id[:]).then_inc(routed.sem, 1)

            hidden_lo(0, 0)
            gate_hidden(0, 1)

            dve.wait_ge(routed.sem, routed.value(0, 3))
            dve.wait_ge(expert_id_done.sem, expert_id_done.value(0, 0))
            nc.vector.tensor_tensor(
                chosen_by[:], expert_id[:].unsqueeze(1).unsqueeze(3).broadcast_to([P, NT, NE, TOPK]),
                top_id_f[:, :, 0:TOPK].unsqueeze(2).broadcast_to([P, NT, NE, TOPK]), ALU.is_equal).then_inc(routed.sem, 1)
            dve.wait_ge(routed.sem, routed.value(0, 4))
            nc.vector.tensor_reduce(chosen[:], chosen_by[:], AX.X, ALU.max).then_inc(routed.sem, 1)
            dve.wait_ge(routed.sem, routed.value(0, 5))
            hidden_lo(0, 1)
            dve.wait_ge(weight_done.sem, weight_done.value(0, 0))
            nc.vector.tensor_tensor(kept_weight[:], weight[:], chosen[:], ALU.mult).then_inc(routed.sem, 1)
            dve.wait_ge(routed.sem, routed.value(0, 6))
            nc.vector.tensor_reduce(weight_sum[:], kept_weight[:], AX.X, ALU.add).then_inc(routed.sem, 1)
            dve.wait_ge(routed.sem, routed.value(0, 7))
            nc.vector.reciprocal(weight_inv[:], weight_sum[:]).then_inc(routed.sem, 1)
            dve.wait_ge(routed.sem, routed.value(0, 8))
            nc.vector.tensor_tensor(gates[:], kept_weight[:], weight_inv[:].unsqueeze(2).broadcast_to([P, NT, NE]),
                                    ALU.mult).then_inc(routed.sem, 1)
            dve.wait_ge(routed.sem, routed.value(0, 9))
            nc.vector.tensor_copy(gates_spread[:], gates[:].unsqueeze(3).broadcast_to([P, NT, NE, EROWS])
                                  ).then_inc(gates_done.sem, 1)

            for step in range(2, FIRST):
                hidden_step(0, step)
            with dve.Fori(0, ROUNDS) as g:
                hidden_step(g, FIRST)
                hidden_step(g, FIRST + 1)
            for step in range(LAST, NSTEPS):
                hidden_step(0, step)

            dve.wait_ge(downed.sem, downed.value(0, NSTEPS - 1))
            for b in range(NB):
                for d in range(DC):
                    cols = slice(b * QB, (b + 1) * QB)
                    nc.vector.scalar_tensor_tensor(out=outT[:, d, cols], in0=yT[d][b], scalar=shared_b2_mean[:, d:d + 1],
                                                   in1=x1T[:, d, cols], op0=ALU.add,
                                                   op1=ALU.add).then_inc(res_done.sem, 1)
            for b in range(NB):
                statistics(1, b)
            normalise(1, result)

        @block.tensor
        def _(pe):
            def turn_for_norm(k, src, i):
                tok = slice(i * P, (i + 1) * P)
                for d in range(DC):
                    mm = nc.tensor.transpose(norm_in[k][:, i, d * P:(d + 1) * P], src[:, d, tok], ident[:])
                mm.then_inc(norm_turned.sem, 1)

            def up(g, step):
                s = step % 2
                if step >= 2:
                    pe.wait_ge(relu_done.sem, relu_done.value(g, step - 2))
                if step == GATES:
                    pe.wait_ge(gates_done.sem, gates_done.value(0, 0))
                    for i in range(NT):
                        mm = nc.tensor.transpose(slot[s][:, i * P:(i + 1) * P],
                                                 gates_spread[:, i].rearrange("p e r -> p (e r)"), ident[:])
                    mm.then_inc(upped.sem, 1)
                    return
                pe.wait_ge(w1_split.sem, w1_split.value(g, w1_tile(step)))
                for b in range(NB):
                    cols = slice(b * QB, (b + 1) * QB)
                    if step == 0:
                        pe.wait_ge(x1_split.sem, x1_split.value(0, DC * b + DC - 1))
                        pe.wait_ge(x1_copied.sem, x1_copied.value(0, DC * b + DC - 1))
                    passes = [x for c in range(DC) for x in split3(
                        w1_hi[:, s, c, :], w1_lo[:, s, c, :], x1T_hi[:, c, cols], x1T_lo[:, c, cols])]
                    for j, (stationary, moving) in enumerate(passes):
                        mm = nc.tensor.matmul(slot[s][:, cols], stationary, moving, start=j == 0,
                                              stop=j == len(passes) - 1)
                mm.then_inc(upped.sem, 1)

            def down(g, step):
                s = step % 2
                pe.wait_ge(h_split.sem, h_split.value(g, step))
                for d in range(DC):
                    feats = slice(d * P, (d + 1) * P)
                    for b in range(NB):
                        cols = slice(b * QB, (b + 1) * QB)
                        for j, (stationary, moving) in enumerate(split3(
                                w2_hi[:, s, feats], w2_lo[:, s, feats], h_hi[:, s, cols], h_lo[:, s, cols])):
                            mm = nc.tensor.matmul(yT[d][b], stationary, moving, start=step == 0 and j == 0,
                                                  stop=step == NSTEPS - 1 and j == 2, skip_group_check=True)
                mm.then_inc(downed.sem, 1)

            for i in range(NT):
                turn_for_norm(0, resT, i)
            for b in range(NB):
                for d in range(DC):
                    for i in range(b * HALF, (b + 1) * HALF):
                        pe.wait_ge(normed[b].sem, normed[b].value(0, i - b * HALF))
                        at = d * QB + (i - b * HALF) * P
                        mm = nc.tensor.transpose(slot[b][:, at:at + P], x1[:, i, d * P:(d + 1) * P], ident[:])
                    mm.then_inc(x1_turned.sem, 1)
            up(0, 0)
            pe.wait_ge(small_in.sem, small_in.value(0, 3))
            for i in range(NT):
                for c in range(DC):
                    mm = nc.tensor.matmul(logits_ps[:, i, :], x1T[:, c, i * P:(i + 1) * P], router[:, c, :],
                                          start=c == 0, stop=c == DC - 1)
            mm.then_inc(logits_done.sem, 1)
            up(0, 1)
            for step in range(FIRST - 2):
                if step + 2 != GATES:
                    up(0, step + 2)
                if step == 0:
                    pe.wait_ge(routed.sem, routed.value(0, 0))
                down(0, step)
                if step + 2 == GATES:
                    up(0, step + 2)
            with pe.Fori(0, ROUNDS) as g:
                for step in (FIRST, FIRST + 1):
                    up(g, step)
                    down(g, step - 2)
            for step in range(LAST, NSTEPS):
                up(0, step)
                down(0, step - 2)
            for step in (NSTEPS - 2, NSTEPS - 1):
                down(0, step)
            for i in range(NT):
                if i % HALF == 0:
                    pe.wait_ge(relu_done.sem, relu_done.value(0, NSTEPS - 1))
                    pe.wait_ge(res_done.sem, res_done.value(0, DC * (i // HALF) + DC - 1))
                turn_for_norm(1, outT, i)


def layer(nc, dram):
    with ExitStack() as ctx:
        kept = {
            "resT": ctx.enter_context(nc.sbuf_tensor("resT", [P, DC, T], F32)),
            "ident": ctx.enter_context(nc.sbuf_tensor("ident", [P, P], F32)),
            "minus_half": ctx.enter_context(nc.sbuf_tensor("minus_half", [P, NT], F32)),
        }
        attention(nc, kept, dram)
        experts(nc, kept, dram)


def laid_out(inputs):
    import numpy as np

    x = np.asarray(inputs["L0_attn_x"])[0]
    f = {k: np.asarray(v) for k, v in inputs.items()}

    def by_round(w, rounds):
        return w.T.reshape(DC, P, rounds, -1).transpose(2, 1, 0, 3)

    pad = NSHARED * P - NS * HID
    sw1 = np.pad(f["L0_ffn_sw1"].transpose(1, 0, 2).reshape(D, NS * HID), ((0, 0), (0, pad)))
    sw2 = np.pad(f["L0_ffn_sw2"].reshape(NS * HID, D), ((0, pad), (0, 0)))
    sb1 = np.pad(f["L0_ffn_sb1"].reshape(NS * HID), (0, pad))
    rw1 = f["L0_ffn_rw1"].reshape(NE, DC, P, NROUTED, EROWS).transpose(3, 2, 1, 0, 4).reshape(NROUTED, P, DC, P)
    rw2 = f["L0_ffn_rw2"].reshape(NE, NROUTED, EROWS, D).transpose(1, 0, 2, 3).reshape(NROUTED, P, D)
    rb1 = f["L0_ffn_rb1"].reshape(NE, NROUTED, EROWS).transpose(0, 2, 1).reshape(P, NROUTED)
    sw1 = sw1.reshape(DC, P, NSHARED, P).transpose(2, 1, 0, 3)
    return {
        "xT": x.T.reshape(DC, P, T).transpose(1, 0, 2),
        "wq": by_round(f["L0_attn_wq"], KVH),
        "wkv": np.concatenate([by_round(f["L0_attn_wk"], 1), by_round(f["L0_attn_wv"], 1)]),
        "wo": f["L0_attn_wo"].T.reshape(KVH, G, P, D).transpose(0, 2, 1, 3),
        "gammas": np.stack([f["L0_attn_q_gamma"], f["L0_attn_k_gamma"]], 1),
        "w1": np.concatenate([sw1, rw1]),
        "w2": np.concatenate([sw2.reshape(NSHARED, P, D), np.repeat(f["L0_ffn_rb2"], EROWS, 0)[None], rw2]),
        "b1": np.concatenate([sb1.reshape(NSHARED, P).T, rb1], 1),
        "shared_b2": f["L0_ffn_sb2"].reshape(NS, DC, P).transpose(2, 0, 1),
        "router": f["L0_ffn_router_w"].reshape(DC, P, NE).transpose(1, 0, 2),
        "router_b": np.broadcast_to(f["L0_ffn_router_b"], (P, NE)),
    }


def kernel(**inputs):
    import numpy as np
    from concourse import bacc
    from concourse.bass_utils import run_bass_kernel_spmd

    nc = bacc.Bacc("TRN2", target_bir_lowering=False, num_devices=1)
    arrays, dram = {}, {}
    for name, a in laid_out(inputs).items():
        arrays[f"in_{name}"] = np.ascontiguousarray(a)
        dram[name] = nc.dram_tensor(f"in_{name}", a.shape, F32, kind="ExternalInput").ap()
    dram["out"] = nc.dram_tensor("out_x", (T, D), F32, kind="ExternalOutput").ap()
    layer(nc, dram)
    r = run_bass_kernel_spmd(nc, [arrays], core_ids=[0])
    return r.results[0]["out_x"].reshape(1, T, D)
```

```python
from contextlib import ExitStack

import concourse.bass as bass
from concourse import mybir

F32 = mybir.dt.float32
F32R = mybir.dt.float32r
U32 = mybir.dt.uint32
ALU = mybir.AluOpType
ACT = mybir.ActivationFunctionType
AX = mybir.AxisListType

P = 128
T, D = 1024, 256
H, KVH, HD = 16, 4, 128
G = H // KVH
NT = T // P
DC = D // P
QB = 512
NB = T // QB
CAP, RMS_EPS, LN_EPS = 50.0, 1e-6, 1e-5
SCALE = HD ** -0.5

NE, NS, HID, TOPK = 32, 2, 176, 6
EROWS = P // NE
NROUTED = HID // EROWS
NSHARED = -(-NS * HID // P)

HEAD_STEPS = (
    ((0, 0, 0, 512), (0, 3, 512, 128), (0, 1, 640, 384)),
    ((1, 0, 0, 512), (1, 1, 512, 512)),
    ((0, 2, 0, 256), (1, 6, 256, 256)),
    ((1, 2, 0, 512), (1, 3, 512, 512)),
    ((1, 4, 0, 512), (1, 7, 512, 128), (1, 5, 640, 384)),
)
STEP_WIDTH = (1024, 1024, 512, 1024, 1024)
STEP_MASKS = (((0, 1, 128), (512, 2, 128)), (), ((0, 2, 256),), (), ((0, 1, 128), (512, 2, 128)))
STEP_ADDS = (
    ((0, (0, 128), 0, "copy"), (0, (128, 512), 128, 640), (0, (384, 512), 512, None)),
    ((1, (0, 512), 0, 512),),
    ((0, (256, 512), 0, None), (1, (256, 512), 256, None)),
    ((1, (0, 512), 0, None), (1, (0, 512), 512, None)),
    ((1, (0, 512), 0, None), (1, (128, 512), 640, None), (1, (384, 512), 512, None)),
)
NSTEP = len(HEAD_STEPS)
STEPS = G * NSTEP
PAIRS = NB * G
HI_ON_ACT = (1, 3)
HALF = NT // NB

LOOP_START = 9


def last_step(p):
    return NSTEP * (p // NB) + (2, 4)[p % NB]


def pairs(n, lag, end):
    return [p for p in range(NB * end // NSTEP) if last_step(p) + lag == n]


def q_heads(n, lead, end):
    return [j for j in range(2, end // NSTEP) if NSTEP * j - lead == n]


def q_halves(n, leads, end):
    return [(j, b) for b in range(NB) for j in q_heads(n, leads[b], end)]


OUT_LAG = (4, 3)
WO_STEP = STEPS + 4
LOOP, LAST = 2 * STEPS, STEPS


def out_pairs(n, lag, end):
    return [p for p in range(NB * end // NSTEP) if last_step(p) + OUT_LAG[p % NB] + lag == n]


def slots(uses, first=0):
    return {u: ((first + i) % 2, uses[i - 2] if i >= 2 else None) for i, u in enumerate(uses)}


def step_uses(n, end):
    out = [("out", p) for p in out_pairs(n, 0, end)]
    scores = [("scores", n + 2)] if n + 2 < end else []
    return out + scores + [("q", j) for j in q_heads(n, 10, end)]


FRONT = (-KVH, 0, 1) + tuple(range(1 - KVH, 0))
FIRST_USES = [u for k in range(KVH) for u in (("q", FRONT[k]), ("v", k))]
FIRST_USES += [("q", j) for j in FRONT[KVH:]] + [("scores", 0), ("scores", 1)]
PLAN_FIRST = slots(FIRST_USES + [u for n in range(LOOP_START) for u in step_uses(n, LOOP)])
CARRIED = [("scores", LOOP_START), ("scores", LOOP_START + 1)]
PLAN_LOOP = slots(CARRIED + [u for n in range(LOOP_START, LOOP_START + STEPS) for u in step_uses(n, LOOP)],
                  PLAN_FIRST[CARRIED[0]][0])
PLAN_LAST = slots(CARRIED + [u for n in range(LOOP_START, LOOP_START + STEPS) for u in step_uses(n, LAST)],
                  PLAN_FIRST[CARRIED[0]][0])
for u in CARRIED:
    assert PLAN_FIRST[u][0] == PLAN_LOOP[u][0] == PLAN_LOOP[u[0], u[1] + STEPS][0]


def nth(j):
    return FRONT.index(j) - KVH if j < 2 else j


class Signal:

    def __init__(self, sem, per_round=1, credit=0, unit=1):
        self.sem, self.per_round, self.credit, self.unit = sem, per_round, credit, unit

    def value(self, g, n):
        return g * (self.per_round * self.unit) + (n + 1 + self.credit) * self.unit


def f32(ap):
    return ap.bitcast(F32)


def split3(stat_hi, stat_lo, move_hi, move_lo):
    return ((stat_hi, move_hi), (stat_lo, move_hi), (stat_hi, move_lo))


ADDS = [(h, i, a) for h in range(LOOP // NSTEP) for i in range(NSTEP) for a in STEP_ADDS[i]]


def last_add(n):
    return max(k for k, (h, i, _) in enumerate(ADDS) if NSTEP * h + i == n)


def attention(nc, kept, dram):
    res, ident, minus_half = kept["res"], kept["ident"], kept["minus_half"]
    with ExitStack() as ctx:
        def sb(name, shape, dt=F32):
            return ctx.enter_context(nc.sbuf_tensor(name, shape, dt))

        def signal(name, per_round=1, credit=0, unit=1):
            return Signal(ctx.enter_context(nc.semaphore(name)), per_round, credit, unit)

        xT_hi, xT_lo = sb("xT_hi", [P, DC, T], F32R), sb("xT_lo", [P, DC, T], F32R)
        wq_raw = sb("wq_raw", [P, DC, G * HD])
        wq_hi, wq_lo = sb("wq_hi", [P, DC, G * HD], F32R), sb("wq_lo", [P, DC, G * HD], F32R)
        wo_raw = sb("wo_raw", [P, G, D])
        wo_hi, wo_lo = sb("wo_hi", [P, G, D], F32R), sb("wo_lo", [P, G, D], F32R)
        gammas = sb("gammas", [P, 2])
        causal = sb("causal", [P, 2, P])
        q_square = sb("q_square", [P, T])
        q_raw = sb("q_raw", [P, T])
        q_raw_odd = sb("q_raw_odd", [P, T])
        q_sum = sb("q_sum", [P, NB, HALF])
        q_var = sb("q_var", [P, NB, HALF])
        q_rinv = sb("q_rinv", [P, NB, HALF])
        q_norm = sb("q_norm", [P, NB, QB])
        qT_hi, qT_lo = sb("qT_hi", [P, 2, T], F32R), sb("qT_lo", [P, 2, T], F32R)
        k_norm = sb("k_norm", [P, KVH, T])
        v_all = sb("v_all", [P, KVH, NT, HD])
        kT_hi, kT_lo = sb("kT_hi", [P, T], F32R), sb("kT_lo", [P, T], F32R)
        v_hi, v_lo = sb("v_hi", [P, NT, HD], F32R), sb("v_lo", [P, NT, HD], F32R)
        capped = sb("capped", [P, 2, 1024])
        prob = sb("prob", [P, 2, 1024])
        prob_hi, prob_lo = sb("prob_hi", [P, 2, 1024], F32R), sb("prob_lo", [P, 2, 1024], F32R)
        prob_sum = sb("prob_sum", [P, 2, NB, QB])
        key_sum = sb("key_sum", [P, NB, HALF])
        inv_sum = sb("inv_sum", [P, NB, HALF])
        o_raw = sb("o_raw", [P, NB, QB])
        oT_hi, oT_lo = sb("oT_hi", [P, 2, T], F32R), sb("oT_lo", [P, 2, T], F32R)
        wkv_raw = [capped[:, n, :].rearrange("p (c k) -> p c k", c=DC) for n in range(2)]
        wkv_hi = [oT_hi[:, n, :].rearrange("p (c k) -> p c k", c=DC) for n in range(2)]
        wkv_lo = [oT_lo[:, n, :].rearrange("p (c k) -> p c k", c=DC) for n in range(2)]

        xT_raw = prob_sum[:].rearrange("p h b c -> p h (b c)")

        psum = ctx.enter_context(nc.psum_tensor("psum_attn", [P, 8, 512], F32))
        slot = [psum[:, 2 * s:2 * s + 2, :].rearrange("p b c -> p (b c)") for s in range(2)]
        o_ps = [psum[:, 4 + b, :] for b in range(NB)]
        x_ps = [psum[:, 6 + b, :] for b in range(NB)]

        def norm_ps(j, b):
            return (o_ps if j < 2 and nth(j) % 2 == 0 else x_ps)[b]

        def square_of(j):
            return o_raw[:].rearrange("p b c -> p (b c)") if j < 2 and nth(j) % 2 else q_square[:]

        def raw_of(j):
            return q_raw_odd[:] if j < 2 and nth(j) % 2 else q_raw[:]

        x_in = [signal(f"x_in{b}", unit=16) for b in range(NB)]
        gammas_in = signal("gammas_in", unit=16)
        res_in = signal("res_in", unit=16)
        wkv_in = [signal(f"w{n}_in", unit=16) for n in "kv"]
        wq_in = signal("wq_in", unit=16)
        wo_in = signal("wo_in", unit=16)
        consts = signal("consts")
        x_hi_done, x_lo_done = signal("x_hi_done"), signal("x_lo_done")
        wkv_hi_done = [signal(f"w{n}_hi_done") for n in "kv"]
        wkv_split = [signal(f"w{n}_split") for n in "kv"]
        wq_hi_done, wq_split = signal("wq_hi_done"), signal("wq_split")
        wo_hi_done, wo_split = signal("wo_hi_done"), signal("wo_split")
        v_projected, v_copied = signal("v_projected", KVH), signal("v_copied", KVH)
        q_projected = signal("q_projected", G, credit=KVH)
        q_squared = signal("q_squared", G, credit=KVH)
        q_copied = signal("q_copied", G, credit=KVH)
        q_turned = signal("q_turned", NB * G, credit=NB * KVH)
        q_summed = signal("q_summed", NB * G, credit=NB * KVH)
        q_var_done = signal("q_var_done", NB * G, credit=NB * KVH)
        q_rinv_done = signal("q_rinv_done", NB * G, credit=NB * KVH)
        q_spread = signal("q_spread", NB * G, credit=NB * KVH)
        q_normed = signal("q_normed", NB * G, credit=NB * KVH)
        q_hi_done = signal("q_hi_done", NB * G)
        q_split = signal("q_split", NB * G)
        k_hi_done, k_split = signal("k_hi_done", NB), signal("k_split", NB)
        v_hi_done, v_split = signal("v_hi_done", NB), signal("v_split", NB)
        scored = signal("scored", STEPS)
        tanh_done = signal("tanh_done", STEPS)
        exp_done = signal("exp_done", STEPS)
        masked = signal("masked", 3 * G)
        hi_act = signal("hi_act", len(HI_ON_ACT) * G)
        hi_dve = signal("hi_dve", (NSTEP - len(HI_ON_ACT)) * G)
        prob_split = signal("prob_split", STEPS)
        added = signal("added", len(ADDS) // 2)
        weighted = signal("weighted", STEPS)
        sums_turned = signal("sums_turned", PAIRS)
        sums_done = signal("sums_done", PAIRS)
        inv_done = signal("inv_done", PAIRS)
        o_hi_done = signal("o_hi_done", PAIRS)
        o_split = signal("o_split", PAIRS)
        out_projected = signal("out_projected", PAIRS)
        res_added = signal("res_added", PAIRS)

        def hi_event(n):
            h, i = divmod(n, NSTEP)
            if i in HI_ON_ACT:
                return hi_act, h * len(HI_ON_ACT) + HI_ON_ACT.index(i)
            rest = [j for j in range(NSTEP) if j not in HI_ON_ACT]
            return hi_dve, h * len(rest) + rest.index(i)

        def mask_event(n):
            return 3 * (n // NSTEP) + (n % NSTEP) // 2



        def q_dst(j, b):
            return k_norm[:, j + KVH, b * QB:(b + 1) * QB] if j < 0 else q_norm[:, b, :]

        block = ctx.enter_context(nc.Block())

        @block.sync
        def _(sp):
            for b in range(NB):
                cols = slice(b * QB, (b + 1) * QB)
                sp.dma_start(xT_raw[:, :, cols], dram["xT"][:, :, cols]).then_inc(x_in[b].sem, 16)
                sp.dma_start(wkv_raw[b], dram["wkv"][b]).then_inc(wkv_in[b].sem, 16)
            sp.dma_start(gammas[:], dram["gammas"]).then_inc(gammas_in.sem, 16)
            sp.dma_start(wq_raw[:], dram["wq"][0]).then_inc(wq_in.sem, 16)
            sp.dma_start(wo_raw[:], dram["wo"][0]).then_inc(wo_in.sem, 16)
            sp.dma_start(res[:], dram["x"].rearrange("(i p) d -> p i d", p=P)).then_inc(res_in.sem, 16)
            with sp.Fori(0, KVH - 1) as g:
                sp.wait_ge(wq_split.sem, wq_split.value(g, 0))
                sp.dma_start(wq_raw[:], dram["wq"][g + 1]).then_inc(wq_in.sem, 16)
                sp.wait_ge(wo_split.sem, wo_split.value(g, 0))
                sp.dma_start(wo_raw[:], dram["wo"][g + 1]).then_inc(wo_in.sem, 16)

        @block.gpsimd
        def _(pool):
            nc.gpsimd.memset(minus_half[:], -0.5).then_inc(consts.sem, 1)
            nc.gpsimd.memset(ident[:], 0.0).then_inc(consts.sem, 1)
            nc.gpsimd.memset(causal[:], 1.0).then_inc(consts.sem, 1)
            pool.wait_ge(consts.sem, consts.value(0, 2))
            nc.gpsimd.affine_select(out=ident[:], in_=ident[:], compare_op=ALU.not_equal, fill=1.0, base=0,
                                    pattern=[[-1, P]], channel_multiplier=1).then_inc(consts.sem, 1)
            nc.gpsimd.affine_select(out=causal[:], in_=causal[:], compare_op=ALU.is_ge, fill=0.0, base=0,
                                    pattern=[[0, 2], [1, P]], channel_multiplier=-1).then_inc(consts.sem, 1)
            pool.wait_ge(consts.sem, consts.value(0, 4))

            def inverse_rms(g, j, b):
                pool.wait_ge(q_var_done.sem, q_var_done.value(g, NB * nth(j) + b))
                nc.gpsimd.tensor_tensor(q_rinv[:, b, :], q_var[:, b, :], minus_half[:, 0:HALF],
                                        ALU.pow).then_inc(q_rinv_done.sem, 1)

            def lo(out, whole, hi):
                return nc.gpsimd.tensor_tensor(out, whole, f32(hi), ALU.subtract)

            def wo_lo_part(g, r):
                pool.wait_ge(wo_hi_done.sem, wo_hi_done.value(g, r))
                lo(wo_lo[:], wo_raw[:], wo_hi[:]).then_inc(wo_split.sem, 1)

            def q_lo(g, j, b):
                pool.wait_ge(q_hi_done.sem, q_hi_done.value(g, NB * j + b))
                cols = slice(b * QB, (b + 1) * QB)
                lo(qT_lo[:, j % 2, cols], q_norm[:, b, :], qT_hi[:, j % 2, cols]).then_inc(q_split.sem, 1)

            def step(g, n, end):
                if n < end and STEP_MASKS[n % NSTEP]:
                    pool.wait_ge(exp_done.sem, exp_done.value(g, n))
                    for first, blocks, stride in STEP_MASKS[n % NSTEP]:
                        part = prob[:, n % 2, first:first + blocks * stride].rearrange(
                            "p (b c) -> p b c", b=blocks)[:, :, 0:P]
                        last = nc.gpsimd.tensor_tensor(part, part, causal[:, 0:blocks, :], ALU.mult)
                    last.then_inc(masked.sem, 1)

                if n == NSTEP * 2 - 1 and end == LOOP:
                    pool.wait_ge(wq_hi_done.sem, wq_hi_done.value(g, 1))
                    lo(wq_lo[:], wq_raw[:], wq_hi[:]).then_inc(wq_split.sem, 1)
                if n == WO_STEP + 1 and end == LOOP:
                    wo_lo_part(g, 1)
                for j, b in q_halves(n, (3, 2), end):
                    q_lo(g, j, b)
                for j, b in q_halves(n, (7, 5), end):
                    inverse_rms(g, j, b)
                if n == STEPS - 1 and end == LOOP:
                    cols = slice(QB, T)
                    pool.wait_ge(k_hi_done.sem, k_hi_done.value(g, NB + 1))
                    lo(kT_lo[:, cols], k_norm[:, bass.ds(g + 1, 1), cols], kT_hi[:, cols]).then_inc(k_split.sem, 1)
                if n in (STEPS, STEPS + 1) and end == LOOP:
                    b = n - STEPS
                    tiles = slice(b * HALF, (b + 1) * HALF)
                    pool.wait_ge(v_hi_done.sem, v_hi_done.value(g, NB + b))
                    lo(v_lo[:, tiles, :], v_all[:, bass.ds(g + 1, 1), tiles, :], v_hi[:, tiles, :]).then_inc(v_split.sem, 1)
                for p in pairs(n, 2, end):
                    h, b = divmod(p, NB)
                    cols = slice(b * QB, (b + 1) * QB)
                    pool.wait_ge(o_hi_done.sem, o_hi_done.value(g, p))
                    if p >= 2 * NB:
                        pool.wait_ge(out_projected.sem, out_projected.value(g, p - 2 * NB))
                    lo(oT_lo[:, h % 2, cols], o_raw[:, b, :], oT_hi[:, h % 2, cols]).then_inc(o_split.sem, 1)

            wo_lo_part(0, 0)
            for j in FRONT[:-1]:
                for b in range(NB):
                    inverse_rms(0, j, b)
            for n in range(LOOP_START):
                step(0, n, LOOP)
                if n == 0:
                    for b in range(NB):
                        inverse_rms(0, FRONT[-1], b)
            with pool.Fori(0, KVH - 1) as g:
                for n in range(LOOP_START, LOOP_START + STEPS):
                    step(g, n, LOOP)
            for n in range(LOOP_START, LOOP_START + STEPS):
                step(KVH - 1, n, LAST)

        @block.scalar
        def _(act):
            for b in range(NB):
                cols = slice(b * QB, (b + 1) * QB)
                act.wait_ge(x_in[b].sem, x_in[b].value(0, 0))
                nc.scalar.activation(xT_hi[:, :, cols], xT_raw[:, :, cols], ACT.Copy).then_inc(x_hi_done.sem, 1)
            act.wait_ge(wkv_in[1].sem, wkv_in[1].value(0, 0))
            nc.scalar.activation(wkv_hi[1], wkv_raw[1], ACT.Copy).then_inc(wkv_hi_done[1].sem, 1)
            act.wait_ge(gammas_in.sem, gammas_in.value(0, 0))

            def wq_hi_half(g, r):
                act.wait_ge(wq_in.sem, wq_in.value(g, r))
                if r > 0:
                    act.wait_ge(q_projected.sem, q_projected.value(g, G * r - 1))
                nc.scalar.activation(wq_hi[:], wq_raw[:], ACT.Copy).then_inc(wq_hi_done.sem, 1)

            def k_hi(g, r, b):
                cols = slice(b * QB, (b + 1) * QB)
                src = k_norm[:, r, cols] if isinstance(g, int) and g == 0 and r == 0 else k_norm[:, bass.ds(g + r, 1), cols]
                nc.scalar.activation(kT_hi[:, cols], src, ACT.Copy).then_inc(k_hi_done.sem, 1)

            def v_hi_half(g, r, b):
                tiles = slice(b * HALF, (b + 1) * HALF)
                src = v_all[:, r, tiles, :] if isinstance(g, int) and g == 0 and r == 0 else v_all[:, bass.ds(g + r, 1), tiles, :]
                nc.scalar.activation(v_hi[:, tiles, :], src, ACT.Copy).then_inc(v_hi_done.sem, 1)

            def leave_slot(g, j, plan):
                s, _ = plan["q", j]
                act.wait_ge(q_projected.sem, q_projected.value(g, nth(j)))
                before = nth(j) - 2 if j < 2 else j - 1
                if before >= -KVH:
                    act.wait_ge(q_turned.sem, q_turned.value(g, NB * before + NB - 1))
                nc.scalar.activation(square_of(j), slot[s], ACT.Square).then_inc(q_squared.sem, 1)
                if before >= -KVH:
                    act.wait_ge(q_normed.sem, q_normed.value(g, NB * before + NB - 1))
                gamma = gammas[:, 1:2] if j < 0 else gammas[:, 0:1]
                nc.scalar.activation(raw_of(j), slot[s], ACT.Copy, scale=gamma).then_inc(q_copied.sem, 1)

            def q_hi(g, j, b):
                act.wait_ge(q_normed.sem, q_normed.value(g, NB * nth(j) + b))
                nc.scalar.activation(qT_hi[:, j % 2, b * QB:(b + 1) * QB], q_norm[:, b, :],
                                     ACT.Copy).then_inc(q_hi_done.sem, 1)

            def step(g, n, end, plan):
                if n == NSTEP * 2 - 1 and end == LOOP:
                    wq_hi_half(g, 1)

                if n < end:
                    s, w = n % 2, STEP_WIDTH[n % NSTEP]
                    act.wait_ge(scored.sem, scored.value(g, n))
                    nc.scalar.activation(capped[:, s, 0:w], slot[plan["scores", n][0]][:, 0:w], ACT.Tanh,
                                         scale=SCALE / CAP).then_inc(tanh_done.sem, 1)
                    if n == STEPS - 2 and end == LOOP:
                        k_hi(g, 1, 0)
                    act.wait_ge(tanh_done.sem, tanh_done.value(g, n))
                    if n >= 2:
                        act.wait_ge(added.sem, added.value(g, last_add(n - 2)))
                    nc.scalar.activation(prob[:, s, 0:w], capped[:, s, 0:w], ACT.Exp,
                                         scale=CAP).then_inc(exp_done.sem, 1)

                    if n % NSTEP in HI_ON_ACT:
                        act.wait_ge(exp_done.sem, exp_done.value(g, n))
                        if n >= 2:
                            act.wait_ge(weighted.sem, weighted.value(g, n - 2))
                        nc.scalar.activation(prob_hi[:, s, 0:w], prob[:, s, 0:w], ACT.Copy).then_inc(hi_act.sem, 1)
                if n == STEPS - 1 and end == LOOP:
                    k_hi(g, 1, 1)
                if n in (STEPS, STEPS + 1) and end == LOOP:
                    act.wait_ge(weighted.sem, weighted.value(g, n - 2))
                    v_hi_half(g, 1, n - STEPS)
                for p in pairs(n, 2, end):
                    h, b = divmod(p, NB)
                    act.wait_ge(weighted.sem, weighted.value(g, last_step(p)))
                    if p >= NB:
                        act.wait_ge(o_split.sem, o_split.value(g, p - NB))
                    else:
                        act.wait_ge(q_turned.sem, q_turned.value(g, NB * nth(FRONT[-1]) + NB - 1))
                    nc.scalar.activation(o_raw[:, b, :], o_ps[b], ACT.Copy)
                    if p >= 2 * NB:
                        act.wait_ge(out_projected.sem, out_projected.value(g, p - 2 * NB))
                    nc.scalar.activation(oT_hi[:, h % 2, b * QB:(b + 1) * QB], o_ps[b],
                                         ACT.Copy).then_inc(o_hi_done.sem, 1)
                for j, b in q_halves(n, (4, 2), end):
                    q_hi(g, j, b)
                for j in q_heads(n, 8, end):
                    leave_slot(g, j, plan)
                if n == WO_STEP and end == LOOP:
                    wo_hi_part(g, 1)

            def wo_hi_part(g, r):
                act.wait_ge(wo_in.sem, wo_in.value(g, r))
                if r > 0:
                    act.wait_ge(out_projected.sem, out_projected.value(g, PAIRS - 1))
                nc.scalar.activation(wo_hi[:], wo_raw[:], ACT.Copy).then_inc(wo_hi_done.sem, 1)

            wq_hi_half(0, 0)
            wo_hi_part(0, 0)
            for i, j in enumerate(FRONT):
                leave_slot(0, j, PLAN_FIRST)
                if i < KVH:
                    act.wait_ge(v_projected.sem, v_projected.value(0, i))
                    nc.scalar.activation(
                        v_all[:, :, 2 * i:2 * i + 2, :].rearrange("p g t c -> p t g c"),
                        slot[PLAN_FIRST["v", i][0]].rearrange("p (t g c) -> p t g c", t=2, g=KVH),
                        ACT.Copy).then_inc(v_copied.sem, 1)
                if i >= 1 and FRONT[i - 1] >= 0:
                    for b in range(NB):
                        q_hi(0, FRONT[i - 1], b)
                if i == 1:
                    act.wait_ge(q_normed.sem, q_normed.value(0, NB * nth(-KVH) + NB - 1))
                    for b in range(NB):
                        k_hi(0, 0, b)
                if i == KVH - 1:
                    act.wait_ge(v_copied.sem, v_copied.value(0, KVH - 1))
                    for b in range(NB):
                        v_hi_half(0, 0, b)
            for n in range(LOOP_START):
                step(0, n, LOOP, PLAN_FIRST)
            with act.Fori(0, KVH - 1) as g:
                for n in range(LOOP_START, LOOP_START + STEPS):
                    step(g, n, LOOP, PLAN_LOOP)
            for n in range(LOOP_START, LOOP_START + STEPS):
                step(KVH - 1, n, LAST, PLAN_LAST)

        @block.vector
        def _(dve):
            def lo(out, whole, hi):
                return nc.vector.tensor_tensor(out, whole, f32(hi), ALU.subtract)

            dve.wait_ge(wkv_in[0].sem, wkv_in[0].value(0, 0))
            nc.vector.tensor_copy(wkv_hi[0], wkv_raw[0]).then_inc(wkv_hi_done[0].sem, 1)
            dve.wait_ge(wkv_hi_done[0].sem, wkv_hi_done[0].value(0, 0))
            lo(wkv_lo[0], wkv_raw[0], wkv_hi[0]).then_inc(wkv_split[0].sem, 1)
            for b in range(NB):
                cols = slice(b * QB, (b + 1) * QB)
                dve.wait_ge(x_hi_done.sem, x_hi_done.value(0, b))
                lo(xT_lo[:, :, cols], xT_raw[:, :, cols], xT_hi[:, :, cols]).then_inc(x_lo_done.sem, 1)
            dve.wait_ge(wkv_hi_done[1].sem, wkv_hi_done[1].value(0, 0))
            lo(wkv_lo[1], wkv_raw[1], wkv_hi[1]).then_inc(wkv_split[1].sem, 1)

            def wq_lo_half(g, r):
                dve.wait_ge(wq_hi_done.sem, wq_hi_done.value(g, r))
                lo(wq_lo[:], wq_raw[:], wq_hi[:]).then_inc(wq_split.sem, 1)

            def k_lo(g, r, b):
                cols = slice(b * QB, (b + 1) * QB)
                src = k_norm[:, r, cols] if isinstance(g, int) and g == 0 and r == 0 else k_norm[:, bass.ds(g + r, 1), cols]
                dve.wait_ge(k_hi_done.sem, k_hi_done.value(g, NB * r + b))
                lo(kT_lo[:, cols], src, kT_hi[:, cols]).then_inc(k_split.sem, 1)

            def first_v_lo(b):
                tiles = slice(b * HALF, (b + 1) * HALF)
                dve.wait_ge(v_hi_done.sem, v_hi_done.value(0, b))
                lo(v_lo[:, tiles, :], v_all[:, 0, tiles, :], v_hi[:, tiles, :]).then_inc(v_split.sem, 1)

            def mean_square(g, j, b):
                dve.wait_ge(q_turned.sem, q_turned.value(g, NB * nth(j) + b))
                if j > -KVH:
                    dve.wait_ge(q_rinv_done.sem, q_rinv_done.value(g, NB * (nth(j) - 1) + b))
                nc.vector.tensor_reduce(q_sum[:, b, :], norm_ps(j, b).rearrange("p (i c) -> p i c", i=HALF), AX.X,
                                        ALU.add).then_inc(q_summed.sem, 1)
                dve.wait_ge(q_summed.sem, q_summed.value(g, NB * nth(j) + b))
                nc.vector.tensor_scalar(q_var[:, b, :], q_sum[:, b, :], 1.0 / HD, RMS_EPS, ALU.mult,
                                        ALU.add).then_inc(q_var_done.sem, 1)

            def normalise_q(g, j, b):
                dve.wait_ge(q_spread.sem, q_spread.value(g, NB * nth(j) + b))
                dve.wait_ge(q_copied.sem, q_copied.value(g, nth(j)))
                if j > 0:
                    dve.wait_ge(q_split.sem, q_split.value(g, NB * (j - 1) + b))
                nc.vector.tensor_tensor(q_dst(j, b), raw_of(j)[:, b * QB:(b + 1) * QB], norm_ps(j, b),
                                        ALU.mult).then_inc(q_normed.sem, 1)

            def step(g, n, end, plan):

                if n == STEPS - 2 and end == LOOP:
                    k_lo(g, 1, 0)
                for p in out_pairs(n, 1, end):
                    b = p % NB
                    dve.wait_ge(out_projected.sem, out_projected.value(g, p))
                    dve.wait_ge(inv_done.sem, inv_done.value(g, p))
                    if p >= NB:
                        dve.wait_ge(res_added.sem, res_added.value(g, p - NB))
                    else:
                        dve.wait_ge(res_in.sem, res_in.value(0, 0))
                    for i in range(HALF):
                        tile = res[:, b * HALF + i, :]
                        last = nc.vector.scalar_tensor_tensor(
                            out=tile, in0=slot[plan["out", p][0]][:, i * D:(i + 1) * D],
                            scalar=inv_sum[:, b, i:i + 1], in1=tile, op0=ALU.mult, op1=ALU.add)
                    last.then_inc(res_added.sem, 1)
                for j, b in q_halves(n, (7, 5), end):
                    mean_square(g, j, b)
                for j, b in q_halves(n, (6, 4), end):
                    normalise_q(g, j, b)

                h, i = divmod(n, NSTEP)
                s, w = n % 2, STEP_WIDTH[i]
                if n < end:
                    if STEP_MASKS[i]:
                        dve.wait_ge(masked.sem, masked.value(g, mask_event(n)))
                    if n >= 2:
                        dve.wait_ge(weighted.sem, weighted.value(g, n - 2))
                    if i not in HI_ON_ACT:
                        nc.vector.tensor_copy(prob_hi[:, s, 0:w], prob[:, s, 0:w]).then_inc(hi_dve.sem, 1)
                    hi_done, event = hi_event(n)
                    dve.wait_ge(hi_done.sem, hi_done.value(g, event))
                    lo(prob_lo[:, s, 0:w], prob[:, s, 0:w], prob_hi[:, s, 0:w]).then_inc(prob_split.sem, 1)


                if n < end:
                    for k, (head, at, (b, (c0, c1), first, second)) in enumerate(ADDS):
                        if NSTEP * head + at != n:
                            continue
                        to = prob_sum[:, h % 2, b, c0:c1]
                        one = prob[:, s, first:first + c1 - c0]
                        if second is None:
                            dve.wait_ge(added.sem, added.value(g, k - 1))
                            add = nc.vector.tensor_tensor(to, to, one, ALU.add)
                        else:
                            if h >= 2:
                                dve.wait_ge(sums_turned.sem, sums_turned.value(g, NB * (h - 2) + b))
                            if second == "copy":
                                add = nc.vector.tensor_copy(to, one)
                            else:
                                add = nc.vector.tensor_tensor(to, one, prob[:, s, second:second + c1 - c0], ALU.add)
                        add.then_inc(added.sem, 1)
                for p in pairs(n, 3, end):
                    dve.wait_ge(sums_turned.sem, sums_turned.value(g, p))
                    nc.vector.tensor_reduce(key_sum[:, p % NB, :], x_ps[p % NB].rearrange("p (i c) -> p i c", i=HALF),
                                            AX.X, ALU.add).then_inc(sums_done.sem, 1)
                    dve.wait_ge(sums_done.sem, sums_done.value(g, p))
                    nc.vector.reciprocal(inv_sum[:, p % NB, :], key_sum[:, p % NB, :]).then_inc(inv_done.sem, 1)




            def q_lo(g, j, b):
                dve.wait_ge(q_hi_done.sem, q_hi_done.value(g, NB * j + b))
                cols = slice(b * QB, (b + 1) * QB)
                lo(qT_lo[:, j % 2, cols], q_norm[:, b, :], qT_hi[:, j % 2, cols]).then_inc(q_split.sem, 1)

            wq_lo_half(0, 0)
            for i, j in enumerate(FRONT[:-1]):
                for b in range(NB):
                    mean_square(0, j, b)
                if i >= 1 and FRONT[i - 1] >= 0:
                    for b in range(NB):
                        q_lo(0, FRONT[i - 1], b)
                for b in range(NB):
                    normalise_q(0, j, b)
                if i == 0:
                    for b in range(NB):
                        k_lo(0, 0, b)
                if i == KVH - 1:
                    for b in range(NB):
                        first_v_lo(b)
            for n in range(LOOP_START):
                step(0, n, LOOP, PLAN_FIRST)
                if n == 0:
                    for b in range(NB):
                        mean_square(0, FRONT[-1], b)
                    for b in range(NB):
                        normalise_q(0, FRONT[-1], b)
            with dve.Fori(0, KVH - 1) as g:
                for n in range(LOOP_START, LOOP_START + STEPS):
                    step(g, n, LOOP, PLAN_LOOP)
            for n in range(LOOP_START, LOOP_START + STEPS):
                step(KVH - 1, n, LAST, PLAN_LAST)

        @block.tensor
        def _(pe):
            pe.wait_ge(consts.sem, consts.value(0, 4))


            def accumulate(out, passes, first=True, final=True):
                for j, (stationary, moving) in enumerate(passes):
                    mm = nc.tensor.matmul(out, stationary, moving, start=first and j == 0,
                                          stop=final and j == len(passes) - 1, skip_group_check=True)
                return mm

            def take_slot(g, use, plan):
                s, before = plan[use]
                if before is not None:
                    kind, i = before
                    if kind == "scores":
                        pe.wait_ge(tanh_done.sem, tanh_done.value(g, i))
                    elif kind == "q":
                        pe.wait_ge(q_copied.sem, q_copied.value(g, nth(i)))
                    elif kind == "v":
                        pe.wait_ge(v_copied.sem, v_copied.value(g, i))
                    else:
                        pe.wait_ge(res_added.sem, res_added.value(g, i))
                return slot[s]

            def project_q(g, j, plan):
                out = take_slot(g, ("q", j), plan)
                if j < 0:
                    w_hi, w_lo, head = wkv_hi[0], wkv_lo[0], slice((j + KVH) * HD, (j + KVH + 1) * HD)
                    pe.wait_ge(wkv_split[0].sem, wkv_split[0].value(0, 0))
                else:
                    w_hi, w_lo, head = wq_hi, wq_lo, slice(j % G * HD, (j % G + 1) * HD)
                    pe.wait_ge(wq_split.sem, wq_split.value(g, j // G))
                for b in range(NB):
                    cols = slice(b * QB, (b + 1) * QB)
                    if j == -KVH:
                        pe.wait_ge(x_lo_done.sem, x_lo_done.value(0, b))
                    mm = accumulate(out[:, cols], [x for c in range(DC) for x in split3(
                        w_hi[:, c, head], w_lo[:, c, head], xT_hi[:, c, cols], xT_lo[:, c, cols])])
                mm.then_inc(q_projected.sem, 1)

            def project_v(i):
                out = take_slot(0, ("v", i), PLAN_FIRST)
                pe.wait_ge(wkv_split[1].sem, wkv_split[1].value(0, 0))
                for t in range(2):
                    tok = slice((2 * i + t) * P, (2 * i + t + 1) * P)
                    mm = accumulate(out[:, t * 512:(t + 1) * 512], [x for c in range(DC) for x in split3(
                        xT_hi[:, c, tok], xT_lo[:, c, tok], wkv_hi[1][:, c, :], wkv_lo[1][:, c, :])])
                mm.then_inc(v_projected.sem, 1)

            def sum_squares(g, j, b):
                pe.wait_ge(q_squared.sem, q_squared.value(g, nth(j)))
                if j >= 3:
                    pe.wait_ge(sums_done.sem, sums_done.value(g, NB * (j - 3) + b))
                elif nth(j) >= 2 - KVH:
                    before = nth(j) - (1 if j == 2 else 2)
                    pe.wait_ge(q_normed.sem, q_normed.value(g, NB * before + b))
                turn(norm_ps(j, b), square_of(j)[:, b * QB:(b + 1) * QB]).then_inc(q_turned.sem, 1)

            def turn(out, rows):
                for i in range(HALF):
                    mm = nc.tensor.transpose(out[:, i * P:(i + 1) * P], rows[:, i * P:(i + 1) * P], ident[:])
                return mm

            def spread_columns(out, columns):
                for i in range(HALF):
                    mm = nc.tensor.transpose(out[:, i * P:(i + 1) * P], columns[:, i:i + 1].broadcast_to([P, P]), ident[:])
                return mm

            def spread_rms(g, j, b):
                pe.wait_ge(q_rinv_done.sem, q_rinv_done.value(g, NB * nth(j) + b))
                spread_columns(norm_ps(j, b), q_rinv[:, b, :]).then_inc(q_spread.sem, 1)

            def score(g, n, plan):
                h, i = divmod(n, NSTEP)
                out = take_slot(g, ("scores", n), plan)
                pe.wait_ge(q_split.sem, q_split.value(g, NB * h + (i >= 1)))
                if h % G == 0 and i in (0, 2):
                    pe.wait_ge(k_split.sem, k_split.value(g, NB * (h // G) + (i == 2)))
                for b, kt, col, w in HEAD_STEPS[i]:
                    keys = slice(kt * P, (kt + 1) * P)
                    queries = slice((b + 1) * QB - w, (b + 1) * QB)
                    mm = accumulate(out[:, col:col + w], split3(
                        kT_hi[:, keys], kT_lo[:, keys], qT_hi[:, h % 2, queries], qT_lo[:, h % 2, queries]))
                mm.then_inc(scored.sem, 1)

            def weigh(g, n):
                h, i = divmod(n, NSTEP)
                s = n % 2
                pe.wait_ge(prob_split.sem, prob_split.value(g, n))
                if h % G == 0 and i in (0, 2):
                    pe.wait_ge(v_split.sem, v_split.value(g, NB * (h // G) + (i == 2)))
                for b, kt, col, w in HEAD_STEPS[i]:
                    p = NB * h + b
                    if kt == 0:
                        if p >= NB:
                            pe.wait_ge(o_hi_done.sem, o_hi_done.value(g, p - NB))
                        else:
                            pe.wait_ge(q_normed.sem, q_normed.value(g, b))
                    mm = accumulate(o_ps[b][:, QB - w:QB], split3(
                        v_hi[:, kt, :], v_lo[:, kt, :], prob_hi[:, s, col:col + w], prob_lo[:, s, col:col + w]),
                        first=kt == 0, final=n == last_step(p))
                mm.then_inc(weighted.sem, 1)

            def sum_keys(g, p, end):
                h, b = divmod(p, NB)
                pe.wait_ge(added.sem, added.value(g, last_add(last_step(p))))
                if h + 2 < end // NSTEP:
                    pe.wait_ge(q_normed.sem, q_normed.value(g, NB * (h + 2) + b))
                elif p >= NB:
                    pe.wait_ge(sums_done.sem, sums_done.value(g, p - NB))
                turn(x_ps[b], prob_sum[:, h % 2, b, :]).then_inc(sums_turned.sem, 1)

            def project_out(g, p, plan):
                h, b = divmod(p, NB)
                out = take_slot(g, ("out", p), plan)
                pe.wait_ge(wo_split.sem, wo_split.value(g, h // G))
                pe.wait_ge(o_split.sem, o_split.value(g, p))
                for i in range(HALF):
                    tok = slice(b * QB + i * P, b * QB + (i + 1) * P)
                    mm = accumulate(out[:, i * D:(i + 1) * D], split3(
                        oT_hi[:, h % 2, tok], oT_lo[:, h % 2, tok], wo_hi[:, h % G, :], wo_lo[:, h % G, :]))
                mm.then_inc(out_projected.sem, 1)

            def step(g, n, end, plan):
                for kind, i in step_uses(n, end):
                    if kind == "out":
                        project_out(g, i, plan)
                        for p in pairs(n, 2, end):
                            sum_keys(g, p, end)
                    elif kind == "scores":
                        score(g, i, plan)
                    else:
                        project_q(g, i, plan)
                for j, b in q_halves(n, (7, 5), end):
                    spread_rms(g, j, b)
                if not out_pairs(n, 0, end):
                    for p in pairs(n, 2, end):
                        sum_keys(g, p, end)
                if n < end:
                    weigh(g, n)
                for j, b in q_halves(n, (9, 7), end):
                    sum_squares(g, j, b)

            for i in range(len(FRONT) + 1):
                if i < len(FRONT):
                    project_q(0, FRONT[i], PLAN_FIRST)
                else:
                    score(0, 0, PLAN_FIRST)
                    score(0, 1, PLAN_FIRST)
                if i > KVH:
                    for b in range(NB):
                        spread_rms(0, FRONT[i - 2], b)
                if i >= 1:
                    for b in range(NB):
                        sum_squares(0, FRONT[i - 1], b)
                if i < KVH:
                    project_v(i)
                if 1 <= i < KVH:
                    for b in range(NB):
                        spread_rms(0, FRONT[i - 1], b)
            for n in range(LOOP_START):
                step(0, n, LOOP, PLAN_FIRST)
                if n == 0:
                    for b in range(NB):
                        spread_rms(0, FRONT[-1], b)
            with pe.Fori(0, KVH - 1) as g:
                for n in range(LOOP_START, LOOP_START + STEPS):
                    step(g, n, LOOP, PLAN_LOOP)
            for n in range(LOOP_START, LOOP_START + STEPS):
                step(KVH - 1, n, LAST, PLAN_LAST)


def experts(nc, kept, dram):
    res, ident, minus_half = kept["res"], kept["ident"], kept["minus_half"]
    NSTEPS = NSHARED + 1 + NROUTED
    GATES = NSHARED
    FIRST, LAST = GATES + 3, NSTEPS - 2
    ROUNDS = (LAST - FIRST) // 2
    NORM_ACT = (4, 6)
    assert FIRST % 2 == 0 and (LAST - FIRST) % 2 == 0

    def w1_tile(step):
        assert step != GATES
        return step - 1 if step > GATES else step

    def w1_load(step):
        return sum(1 for x in range(step % 2, step, 2) if x != GATES)

    with ExitStack() as ctx:
        def sb(name, shape, dt=F32):
            return ctx.enter_context(nc.sbuf_tensor(name, shape, dt))

        def signal(name, per_round=1, credit=0, unit=1):
            return Signal(ctx.enter_context(nc.semaphore(name)), per_round, credit, unit)

        w1_raw, w2_raw = sb("w1_raw", [P, 2, DC, P]), sb("w2_raw", [P, 2, D])
        w1_hi, w1_lo = sb("w1_hi", [P, 2, DC, P], F32R), sb("w1_lo", [P, 2, DC, P], F32R)
        w2_hi, w2_lo = sb("w2_hi", [P, 2, D], F32R), sb("w2_lo", [P, 2, D], F32R)
        b1 = sb("b1", [P, NSHARED + NROUTED])
        shared_b2 = sb("shared_b2", [P, NS, DC])
        shared_b2_sum = sb("shared_b2_sum", [P, DC])
        shared_b2_mean = sb("shared_b2_mean", [P, DC])
        router = sb("router", [P, DC, NE])
        router_b = sb("router_b", [P, NE])
        stats = sb("stats", [P, 2, NT, 6])
        mean_var = sb("mean_var", [P, 2, NT, 2])
        var_eps = sb("ln_var_eps", [P, 2, NT])
        rstd = sb("rstd", [P, 2, NT])
        minus_mean, norm_shift = sb("minus_mean", [P, 2, NT]), sb("norm_shift", [P, 2, NT])
        x1 = sb("x1", [P, NT, D])
        x1T = sb("x1T", [P, DC, T])
        x1T_hi, x1T_lo = sb("x1T_hi", [P, DC, T], F32R), sb("x1T_lo", [P, DC, T], F32R)
        logits = sb("logits", [P, NT, NE])
        top8 = sb("top8", [P, NT, 8])
        top_id = sb("top_id", [P, NT, 8], U32)
        top_id_f = sb("top_id_f", [P, NT, 8])
        expert_id = sb("expert_id", [P, NE])
        chosen_by = sb("chosen_by", [P, NT, NE, TOPK])
        chosen = sb("chosen", [P, NT, NE])
        below_max = sb("below_max", [P, NT, NE])
        weight = sb("weight", [P, NT, NE])
        kept_weight = sb("kept_weight", [P, NT, NE])
        weight_sum = sb("weight_sum", [P, NT])
        weight_inv = sb("weight_inv", [P, NT])
        gates = sb("gates", [P, NT, NE])
        gates_spread = sb("gates_spread", [P, NT, NE, EROWS])
        gatesT = sb("gatesT", [P, T])
        hidden = sb("hidden", [P, 2, T])
        gated = sb("gated", [P, 2, T])
        h_hi, h_lo = sb("h_hi", [P, 2, T], F32R), sb("h_lo", [P, 2, T], F32R)
        outT = sb("outT", [P, DC, T])
        result = sb("result", [P, NT, D])

        psum = ctx.enter_context(nc.psum_tensor("psum_moe", [P, 8, 512], F32))
        yT = [[psum[:, NB * d + b, :] for b in range(NB)] for d in range(DC)]
        slot = [psum[:, 4 + 2 * s:6 + 2 * s, :].rearrange("p b c -> p (b c)") for s in range(2)]
        norm_in = [res, psum[:, 4:8, :].rearrange("p b (i c) -> p (b i) c", c=D)]
        logits_ps = psum[:, 0, 0:NT * NE].rearrange("p (i e) -> p i e", i=NT)

        small_in = signal("moe_small_in", unit=16)
        w1_in = [signal(f"w1_in{s}", unit=16) for s in range(2)]
        w2_in = [signal(f"w2_in{s}", unit=16) for s in range(2)]
        expert_id_done = signal("expert_id_done")
        norm_turned = signal("norm_turned", NT)
        norm_stats = signal("norm_stats", NT)
        norm_mean = signal("norm_mean", NT)
        norm_var = signal("norm_var", NB)
        norm_rstd = signal("norm_rstd", NB)
        norm_shift_done = signal("norm_shift_done", NB)
        normed = [[signal(f"norm{k}_by_act"), signal(f"norm{k}_by_dve")] for k in range(2)]
        x1_turned = signal("x1_turned", NB * DC)
        x1_hi_done = signal("x1_hi_done", NB * DC)
        x1_copied = signal("x1_copied", NB * DC)
        x1_split = signal("x1_split", NB * DC)
        last_gated, last_hi_done = signal("last_gated", NB), signal("last_hi_done", NB)
        last_split, last_downed = signal("last_split", NB), signal("last_downed", NB)
        bias_done = signal("bias_done")
        logits_done = signal("logits_done")
        routed = signal("routed")
        below_max_done = signal("below_max_done")
        weight_done = signal("weight_done")
        gates_done = signal("gates_done")
        w1_hi_done, w1_split = signal("w1_hi_done", 2), signal("w1_split", 2)
        w2_hi_done, w2_split = signal("w2_hi_done", 2), signal("w2_split", 2)
        upped = signal("upped", 2)
        relu_done = signal("relu_done", 2)
        gate_done = signal("gate_done", 2)
        h_hi_done = signal("h_hi_done", 2)
        h_split = signal("h_split", 2)
        downed = signal("downed", 2)
        res_done = signal("moe_res_done", NB * DC)
        stored = signal("stored", unit=16)

        block = ctx.enter_context(nc.Block())


        @block.sync
        def _(sp):
            def load(g, step):
                s = step % 2
                if step != GATES:
                    if step >= 2:
                        before = step - 2 if step - 2 != GATES else step - 4
                        sp.wait_ge(w1_split.sem, w1_split.value(g, w1_tile(before)))
                    sp.dma_start(w1_raw[:, s], dram["w1"][2 * g + w1_tile(step)]).then_inc(w1_in[s].sem, 16)
                if step >= 2:
                    sp.wait_ge(w2_split.sem, w2_split.value(g, step - 2))
                sp.dma_start(w2_raw[:, s], dram["w2"][2 * g + step]).then_inc(w2_in[s].sem, 16)

            load(0, 0)
            load(0, 1)
            for to, of in ((router, "router"), (router_b, "router_b"), (b1, "b1"), (shared_b2, "shared_b2")):
                sp.dma_start(to[:], dram[of]).then_inc(small_in.sem, 16)
            for step in range(2, FIRST):
                load(0, step)
            with sp.Fori(0, ROUNDS) as g:
                load(g, FIRST)
                load(g, FIRST + 1)
            for step in range(LAST, NSTEPS):
                load(0, step)
            out = dram["out"].rearrange("(i p) d -> p i d", p=P)
            for b in range(NB):
                tiles = slice(b * HALF, (b + 1) * HALF)
                sp.wait_ge(normed[1][0].sem, normed[1][0].value(0, min((b + 1) * HALF, NORM_ACT[1]) - 1))
                if (b + 1) * HALF > NORM_ACT[1]:
                    sp.wait_ge(normed[1][1].sem, normed[1][1].value(0, (b + 1) * HALF - NORM_ACT[1] - 1))
                sp.dma_start(out[:, tiles, :], result[:, tiles, :]).then_inc(stored.sem, 16)
            sp.wait_ge(stored.sem, stored.value(0, NB - 1))

        @block.gpsimd
        def _(pool):
            nc.gpsimd.iota(expert_id[:], pattern=[[1, NE]], base=0, channel_multiplier=0,
                           allow_small_or_imprecise_dtypes=True).then_inc(expert_id_done.sem, 1)
            for k in range(2):
                if k == 1:
                    for step in range(GATES - 1):
                        pool.wait_ge(h_hi_done.sem, h_hi_done.value(0, step))
                        nc.gpsimd.tensor_tensor(h_lo[:, step, :], gated[:, step, :], f32(h_hi[:, step, :]),
                                                ALU.subtract).then_inc(h_split.sem, 1)
                for b in range(NB):
                    tiles = slice(b * HALF, (b + 1) * HALF)
                    pool.wait_ge(norm_var.sem, norm_var.value(k, b))
                    nc.gpsimd.tensor_tensor(rstd[:, k, tiles], var_eps[:, k, tiles], minus_half[:, tiles],
                                            ALU.pow).then_inc(norm_rstd.sem, 1)
                    pool.wait_ge(norm_rstd.sem, norm_rstd.value(k, b))
                    nc.gpsimd.tensor_tensor(norm_shift[:, k, tiles], minus_mean[:, k, tiles], rstd[:, k, tiles],
                                            ALU.mult).then_inc(norm_shift_done.sem, 1)

        @block.scalar
        def _(act):
            def normalise(k, to):
                for i in range(NORM_ACT[k]):
                    if i % HALF == 0:
                        act.wait_ge(norm_shift_done.sem, norm_shift_done.value(k, i // HALF))
                    nc.scalar.activation(to[:, i, :], norm_in[k][:, i, :], ACT.Identity, bias=norm_shift[:, k, i:i + 1],
                                         scale=rstd[:, k, i:i + 1]).then_inc(normed[k][0].sem, 1)

            normalise(0, x1)
            for u in range(NB * DC):
                b, d = divmod(u, DC)
                cols = slice(b * QB, (b + 1) * QB)
                turned = slot[b][:, d * QB:(d + 1) * QB]
                act.wait_ge(x1_turned.sem, x1_turned.value(0, u))
                nc.scalar.activation(x1T_hi[:, d, cols], turned, ACT.Copy).then_inc(x1_hi_done.sem, 1)

            act.wait_ge(small_in.sem, small_in.value(0, 3))

            def relu(g, step):
                s = step % 2
                act.wait_ge(upped.sem, upped.value(g, step))
                if step >= 2:
                    act.wait_ge(gate_done.sem, gate_done.value(g, step - 2))
                if step == GATES:
                    nc.scalar.activation(gatesT[:], slot[s], ACT.Copy).then_inc(relu_done.sem, 1)
                else:
                    t = w1_tile(step) if step < FIRST or step >= LAST + 1 else bass.ds(2 * g + w1_tile(step), 1)
                    bias = b1[:, t:t + 1] if isinstance(t, int) else b1[:, t]
                    nc.scalar.activation(hidden[:, s, :], slot[s], ACT.Relu, bias=bias).then_inc(relu_done.sem, 1)

            def hi(g, step):
                s = step % 2
                act.wait_ge(gate_done.sem, gate_done.value(g, step))
                if step >= 2:
                    act.wait_ge(downed.sem, downed.value(g, step - 2))
                nc.scalar.activation(h_hi[:, s, :], gated[:, s, :], ACT.Copy).then_inc(h_hi_done.sem, 1)

            relu(0, 0)
            hi(0, 0)
            relu(0, 1)
            act.wait_ge(below_max_done.sem, below_max_done.value(0, 0))
            nc.scalar.activation(weight[:], below_max[:], ACT.Exp).then_inc(weight_done.sem, 1)
            hi(0, 1)
            relu(0, 2)
            for step in range(2, FIRST - 1):
                relu(0, step + 1)
                hi(0, step)
            with act.Fori(0, ROUNDS) as g:
                for step in (FIRST, FIRST + 1):
                    relu(g, step)
                    hi(g, step - 1)
            for step in range(LAST, NSTEPS):
                relu(0, step)
                hi(0, step - 1)
            s = (NSTEPS - 1) % 2
            act.wait_ge(downed.sem, downed.value(0, NSTEPS - 3))
            for b in range(NB):
                cols = slice(b * QB, (b + 1) * QB)
                act.wait_ge(last_gated.sem, last_gated.value(0, b))
                nc.scalar.activation(h_hi[:, s, cols], gated[:, s, cols], ACT.Copy).then_inc(last_hi_done.sem, 1)
            normalise(1, result)

        @block.vector
        def _(dve):
            def statistics(k, b):
                tiles = slice(b * HALF, (b + 1) * HALF)
                for i in range(b * HALF, (b + 1) * HALF):
                    if k == 1:
                        dve.wait_ge(norm_turned.sem, norm_turned.value(0, i | 1))
                    nc.vector.bn_stats(stats[:, k, i, :], norm_in[k][:, i, :]).then_inc(norm_stats.sem, 1)
                for i in range(b * HALF, (b + 1) * HALF):
                    dve.wait_ge(norm_stats.sem, norm_stats.value(k, i))
                    nc.vector.bn_aggr(mean_var[:, k, i, :], stats[:, k, i, :]).then_inc(norm_mean.sem, 1)
                dve.wait_ge(norm_mean.sem, norm_mean.value(k, (b + 1) * HALF - 1))
                nc.vector.tensor_scalar(minus_mean[:, k, tiles], mean_var[:, k, tiles, 0], -1.0, None, ALU.mult)
                nc.vector.tensor_scalar(var_eps[:, k, tiles], mean_var[:, k, tiles, 1], LN_EPS, None,
                                        ALU.add).then_inc(norm_var.sem, 1)

            def normalise(k, to):
                dve.wait_ge(norm_rstd.sem, norm_rstd.value(k, 1))
                for i in range(NORM_ACT[k], NT):
                    nc.vector.tensor_scalar(to[:, i, :], norm_in[k][:, i, :], mean_var[:, k, i, 0:1],
                                            rstd[:, k, i:i + 1], ALU.subtract, ALU.mult).then_inc(normed[k][1].sem, 1)

            def split_w1(g, step):
                s = step % 2
                t = w1_tile(step)
                dve.wait_ge(w1_in[s].sem, w1_in[s].value(g, w1_load(step)))
                if step >= 2:
                    dve.wait_ge(upped.sem, upped.value(g, step - 2))
                nc.vector.tensor_copy(w1_hi[:, s], w1_raw[:, s]).then_inc(w1_hi_done.sem, 1)
                dve.wait_ge(w1_hi_done.sem, w1_hi_done.value(g, t))
                nc.vector.tensor_tensor(w1_lo[:, s], w1_raw[:, s], f32(w1_hi[:, s]), ALU.subtract).then_inc(w1_split.sem, 1)

            def split_w2(g, step):
                s = step % 2
                dve.wait_ge(w2_in[s].sem, w2_in[s].value(g, step // 2))
                if step >= 2:
                    dve.wait_ge(downed.sem, downed.value(g, step - 2))
                nc.vector.tensor_copy(w2_hi[:, s], w2_raw[:, s]).then_inc(w2_hi_done.sem, 1)
                dve.wait_ge(w2_hi_done.sem, w2_hi_done.value(g, step))
                nc.vector.tensor_tensor(w2_lo[:, s], w2_raw[:, s], f32(w2_hi[:, s]), ALU.subtract).then_inc(w2_split.sem, 1)

            def gate_hidden(g, step):
                s = step % 2
                split_w2(g, step)
                dve.wait_ge(relu_done.sem, relu_done.value(g, step))
                if step < GATES:
                    gate = nc.vector.tensor_scalar(gated[:, s, :], hidden[:, s, :], 1.0 / NS, None, ALU.mult)
                elif step == GATES:
                    gate = nc.vector.tensor_scalar(gated[:, s, :], gatesT[:], 1.0 / EROWS, None, ALU.mult)
                else:
                    gate = nc.vector.tensor_tensor(gated[:, s, :], hidden[:, s, :], gatesT[:], ALU.mult)
                gate.then_inc(gate_done.sem, 1)

            def hidden_lo(g, step):
                s = step % 2
                dve.wait_ge(h_hi_done.sem, h_hi_done.value(g, step))
                nc.vector.tensor_tensor(h_lo[:, s, :], gated[:, s, :], f32(h_hi[:, s, :]), ALU.subtract).then_inc(h_split.sem, 1)

            def hidden_step(g, step):
                gate_hidden(g, step)
                if step + 2 < NSTEPS and step + 2 != GATES:
                    split_w1(g, step + 2)
                hidden_lo(g, step)

            for b in range(NB):
                statistics(0, b)
            split_w1(0, 0)
            split_w1(0, 1)
            normalise(0, x1)
            for u in range(NB * DC):
                b, d = divmod(u, DC)
                cols = slice(b * QB, (b + 1) * QB)
                dve.wait_ge(x1_hi_done.sem, x1_hi_done.value(0, u))
                nc.vector.tensor_tensor(x1T_lo[:, d, cols], slot[b][:, d * QB:(d + 1) * QB], f32(x1T_hi[:, d, cols]),
                                        ALU.subtract).then_inc(x1_split.sem, 1)
            for u in range(NB * DC):
                b, d = divmod(u, DC)
                cols = slice(b * QB, (b + 1) * QB)
                dve.wait_ge(x1_split.sem, x1_split.value(0, u))
                nc.vector.tensor_tensor(x1T[:, d, cols], f32(x1T_hi[:, d, cols]), f32(x1T_lo[:, d, cols]),
                                        ALU.add).then_inc(x1_copied.sem, 1)
            dve.wait_ge(small_in.sem, small_in.value(0, 3))
            nc.vector.tensor_tensor(shared_b2_sum[:], shared_b2[:, 0, :], shared_b2[:, 1, :], ALU.add).then_inc(bias_done.sem, 1)
            dve.wait_ge(bias_done.sem, bias_done.value(0, 0))
            nc.vector.tensor_scalar(shared_b2_mean[:], shared_b2_sum[:], 1.0 / NS, None, ALU.mult).then_inc(bias_done.sem, 1)

            split_w1(0, 2)
            gate_hidden(0, 0)

            dve.wait_ge(logits_done.sem, logits_done.value(0, 0))
            nc.vector.tensor_tensor(logits[:], logits_ps, router_b[:].unsqueeze(1).broadcast_to([P, NT, NE]),
                                    ALU.add).then_inc(routed.sem, 1)
            dve.wait_ge(routed.sem, routed.value(0, 0))
            for i in range(NT):
                last = nc.vector.max(top8[:, i, :], logits[:, i, :])
            last.then_inc(routed.sem, 1)
            dve.wait_ge(routed.sem, routed.value(0, 1))
            nc.vector.tensor_tensor(below_max[:], logits[:], top8[:, :, 0:1].broadcast_to([P, NT, NE]),
                                    ALU.subtract).then_inc(below_max_done.sem, 1)
            for i in range(NT):
                last = nc.vector.max_index(top_id[:, i, :], top8[:, i, :], logits[:, i, :])
            last.then_inc(routed.sem, 1)
            dve.wait_ge(routed.sem, routed.value(0, 2))
            nc.vector.tensor_copy(top_id_f[:], top_id[:]).then_inc(routed.sem, 1)

            gate_hidden(0, 1)

            dve.wait_ge(routed.sem, routed.value(0, 3))
            dve.wait_ge(expert_id_done.sem, expert_id_done.value(0, 0))
            nc.vector.tensor_tensor(
                chosen_by[:], expert_id[:].unsqueeze(1).unsqueeze(3).broadcast_to([P, NT, NE, TOPK]),
                top_id_f[:, :, 0:TOPK].unsqueeze(2).broadcast_to([P, NT, NE, TOPK]), ALU.is_equal).then_inc(routed.sem, 1)
            dve.wait_ge(routed.sem, routed.value(0, 4))
            nc.vector.tensor_reduce(chosen[:], chosen_by[:], AX.X, ALU.max).then_inc(routed.sem, 1)
            dve.wait_ge(routed.sem, routed.value(0, 5))
            dve.wait_ge(weight_done.sem, weight_done.value(0, 0))
            nc.vector.tensor_tensor(kept_weight[:], weight[:], chosen[:], ALU.mult).then_inc(routed.sem, 1)
            dve.wait_ge(routed.sem, routed.value(0, 6))
            nc.vector.tensor_reduce(weight_sum[:], kept_weight[:], AX.X, ALU.add).then_inc(routed.sem, 1)
            dve.wait_ge(routed.sem, routed.value(0, 7))
            nc.vector.reciprocal(weight_inv[:], weight_sum[:]).then_inc(routed.sem, 1)
            dve.wait_ge(routed.sem, routed.value(0, 8))
            nc.vector.tensor_tensor(gates[:], kept_weight[:], weight_inv[:].unsqueeze(2).broadcast_to([P, NT, NE]),
                                    ALU.mult).then_inc(routed.sem, 1)
            dve.wait_ge(routed.sem, routed.value(0, 9))
            nc.vector.tensor_copy(gates_spread[:], gates[:].unsqueeze(3).broadcast_to([P, NT, NE, EROWS])
                                  ).then_inc(gates_done.sem, 1)

            for step in range(2, FIRST):
                hidden_step(0, step)
            with dve.Fori(0, ROUNDS) as g:
                hidden_step(g, FIRST)
                hidden_step(g, FIRST + 1)
            for step in range(LAST, NSTEPS - 1):
                hidden_step(0, step)
            step, s = NSTEPS - 1, (NSTEPS - 1) % 2
            dve.wait_ge(relu_done.sem, relu_done.value(0, step))
            dve.wait_ge(downed.sem, downed.value(0, step - 2))
            for b in range(NB):
                cols = slice(b * QB, (b + 1) * QB)
                nc.vector.tensor_tensor(gated[:, s, cols], hidden[:, s, cols], gatesT[:, cols],
                                        ALU.mult).then_inc(last_gated.sem, 1)
            split_w2(0, step)
            for b in range(NB):
                cols = slice(b * QB, (b + 1) * QB)
                dve.wait_ge(last_hi_done.sem, last_hi_done.value(0, b))
                nc.vector.tensor_tensor(h_lo[:, s, cols], gated[:, s, cols], f32(h_hi[:, s, cols]),
                                        ALU.subtract).then_inc(last_split.sem, 1)

            for b in range(NB):
                dve.wait_ge(last_downed.sem, last_downed.value(0, b))
                for d in range(DC):
                    cols = slice(b * QB, (b + 1) * QB)
                    nc.vector.scalar_tensor_tensor(out=outT[:, d, cols], in0=yT[d][b], scalar=shared_b2_mean[:, d:d + 1],
                                                   in1=x1T[:, d, cols], op0=ALU.add,
                                                   op1=ALU.add).then_inc(res_done.sem, 1)
            for b in range(NB):
                statistics(1, b)
            normalise(1, result)

        @block.tensor
        def _(pe):
            def turn_for_norm(src, i):
                tok = slice(i * P, (i + 1) * P)
                for d in range(DC):
                    mm = nc.tensor.transpose(norm_in[1][:, i, d * P:(d + 1) * P], src[:, d, tok], ident[:])
                mm.then_inc(norm_turned.sem, 1)

            def up(g, step):
                s = step % 2
                if step >= 2:
                    pe.wait_ge(relu_done.sem, relu_done.value(g, step - 2))
                if step == GATES:
                    pe.wait_ge(gates_done.sem, gates_done.value(0, 0))
                    for i in range(NT):
                        mm = nc.tensor.transpose(slot[s][:, i * P:(i + 1) * P],
                                                 gates_spread[:, i].rearrange("p e r -> p (e r)"), ident[:])
                    mm.then_inc(upped.sem, 1)
                    return
                pe.wait_ge(w1_split.sem, w1_split.value(g, w1_tile(step)))
                for b in range(NB):
                    cols = slice(b * QB, (b + 1) * QB)
                    if step == 0:
                        pe.wait_ge(x1_split.sem, x1_split.value(0, DC * b + DC - 1))

                    passes = [x for c in range(DC) for x in split3(
                        w1_hi[:, s, c, :], w1_lo[:, s, c, :], x1T_hi[:, c, cols], x1T_lo[:, c, cols])]
                    for j, (stationary, moving) in enumerate(passes):
                        mm = nc.tensor.matmul(slot[s][:, cols], stationary, moving, start=j == 0,
                                              stop=j == len(passes) - 1)
                mm.then_inc(upped.sem, 1)

            def down(g, step):
                s = step % 2
                pe.wait_ge(h_split.sem, h_split.value(g, step))
                for d in range(DC):
                    feats = slice(d * P, (d + 1) * P)
                    for b in range(NB):
                        cols = slice(b * QB, (b + 1) * QB)
                        for j, (stationary, moving) in enumerate(split3(
                                w2_hi[:, s, feats], w2_lo[:, s, feats], h_hi[:, s, cols], h_lo[:, s, cols])):
                            mm = nc.tensor.matmul(yT[d][b], stationary, moving, start=step == 0 and j == 0,
                                                  stop=False, skip_group_check=True)
                mm.then_inc(downed.sem, 1)

            for b in range(NB):
                for d in range(DC):
                    for i in range(b * HALF, (b + 1) * HALF):
                        if i < NORM_ACT[0]:
                            pe.wait_ge(normed[0][0].sem, normed[0][0].value(0, i))
                        else:
                            pe.wait_ge(normed[0][1].sem, normed[0][1].value(0, i - NORM_ACT[0]))
                        at = d * QB + (i - b * HALF) * P
                        mm = nc.tensor.transpose(slot[b][:, at:at + P], x1[:, i, d * P:(d + 1) * P], ident[:])
                    mm.then_inc(x1_turned.sem, 1)
            up(0, 0)
            pe.wait_ge(small_in.sem, small_in.value(0, 3))
            pe.wait_ge(x1_copied.sem, x1_copied.value(0, NB * DC - 1))
            for i in range(NT):
                for c in range(DC):
                    mm = nc.tensor.matmul(logits_ps[:, i, :], x1T[:, c, i * P:(i + 1) * P], router[:, c, :],
                                          start=c == 0, stop=c == DC - 1)
            mm.then_inc(logits_done.sem, 1)
            up(0, 1)
            for step in range(FIRST - 2):
                if step + 2 != GATES:
                    up(0, step + 2)
                if step == 0:
                    pe.wait_ge(routed.sem, routed.value(0, 0))
                down(0, step)
                if step + 2 == GATES:
                    up(0, step + 2)
            with pe.Fori(0, ROUNDS) as g:
                for step in (FIRST, FIRST + 1):
                    up(g, step)
                    down(g, step - 2)
            for step in range(LAST, NSTEPS):
                up(0, step)
                down(0, step - 2)
            down(0, NSTEPS - 2)
            s = (NSTEPS - 1) % 2
            for b in range(NB):
                pe.wait_ge(last_split.sem, last_split.value(0, b))
                cols = slice(b * QB, (b + 1) * QB)
                for d in range(DC):
                    feats = slice(d * P, (d + 1) * P)
                    for j, (stationary, moving) in enumerate(split3(
                            w2_hi[:, s, feats], w2_lo[:, s, feats], h_hi[:, s, cols], h_lo[:, s, cols])):
                        mm = nc.tensor.matmul(yT[d][b], stationary, moving, start=False, stop=j == 2,
                                              skip_group_check=True)
                mm.then_inc(last_downed.sem, 1)
            for i in range(NT):
                if i % HALF == 0:
                    pe.wait_ge(relu_done.sem, relu_done.value(0, NSTEPS - 1))
                    pe.wait_ge(res_done.sem, res_done.value(0, DC * (i // HALF) + DC - 1))
                turn_for_norm(outT, i)


def layer(nc, dram):
    with ExitStack() as ctx:
        kept = {
            "res": ctx.enter_context(nc.sbuf_tensor("res", [P, NT, D], F32)),
            "ident": ctx.enter_context(nc.sbuf_tensor("ident", [P, P], F32)),
            "minus_half": ctx.enter_context(nc.sbuf_tensor("minus_half", [P, NT], F32)),
        }
        attention(nc, kept, dram)
        experts(nc, kept, dram)


def laid_out(inputs):
    import numpy as np

    x = np.asarray(inputs["L0_attn_x"])[0]
    f = {k: np.asarray(v) for k, v in inputs.items()}

    def by_round(w, rounds):
        return w.T.reshape(DC, P, rounds, -1).transpose(2, 1, 0, 3)

    pad = NSHARED * P - NS * HID
    sw1 = np.pad(f["L0_ffn_sw1"].transpose(1, 0, 2).reshape(D, NS * HID), ((0, 0), (0, pad)))
    sw2 = np.pad(f["L0_ffn_sw2"].reshape(NS * HID, D), ((0, pad), (0, 0)))
    sb1 = np.pad(f["L0_ffn_sb1"].reshape(NS * HID), (0, pad))
    rw1 = f["L0_ffn_rw1"].reshape(NE, DC, P, NROUTED, EROWS).transpose(3, 2, 1, 0, 4).reshape(NROUTED, P, DC, P)
    rw2 = f["L0_ffn_rw2"].reshape(NE, NROUTED, EROWS, D).transpose(1, 0, 2, 3).reshape(NROUTED, P, D)
    rb1 = f["L0_ffn_rb1"].reshape(NE, NROUTED, EROWS).transpose(0, 2, 1).reshape(P, NROUTED)
    sw1 = sw1.reshape(DC, P, NSHARED, P).transpose(2, 1, 0, 3)
    return {
        "x": x,
        "xT": x.T.reshape(DC, P, T).transpose(1, 0, 2),
        "wq": by_round(f["L0_attn_wq"], KVH),
        "wkv": np.concatenate([by_round(f["L0_attn_wk"], 1), by_round(f["L0_attn_wv"], 1)]),
        "wo": f["L0_attn_wo"].T.reshape(KVH, G, P, D).transpose(0, 2, 1, 3),
        "gammas": np.stack([f["L0_attn_q_gamma"], f["L0_attn_k_gamma"]], 1),
        "w1": np.concatenate([sw1, rw1]),
        "w2": np.concatenate([sw2.reshape(NSHARED, P, D), np.repeat(f["L0_ffn_rb2"], EROWS, 0)[None], rw2]),
        "b1": np.concatenate([sb1.reshape(NSHARED, P).T, rb1], 1),
        "shared_b2": f["L0_ffn_sb2"].reshape(NS, DC, P).transpose(2, 0, 1),
        "router": f["L0_ffn_router_w"].reshape(DC, P, NE).transpose(1, 0, 2),
        "router_b": np.broadcast_to(f["L0_ffn_router_b"], (P, NE)),
    }


def kernel(**inputs):
    import numpy as np
    from concourse import bacc
    from concourse.bass_utils import run_bass_kernel_spmd

    nc = bacc.Bacc("TRN2", target_bir_lowering=False, num_devices=1)
    arrays, dram = {}, {}
    for name, a in laid_out(inputs).items():
        arrays[f"in_{name}"] = np.ascontiguousarray(a)
        dram[name] = nc.dram_tensor(f"in_{name}", a.shape, F32, kind="ExternalInput").ap()
    dram["out"] = nc.dram_tensor("out_x", (T, D), F32, kind="ExternalOutput").ap()
    layer(nc, dram)
    r = run_bass_kernel_spmd(nc, [arrays], core_ids=[0])
    return r.results[0]["out_x"].reshape(1, T, D)
```
